# Optimizing a Trainium2 kernel written in Bass

```python
import numpy as np
import jax
import jax.numpy as jnp

def _softmax(x, axis=-1):
    return jax.nn.softmax(x, axis=axis)

def _gelu(x):
    return jax.nn.gelu(x, approximate=True)

def _silu(x):
    return jax.nn.silu(x)

def _sigmoid(x):
    return jax.nn.sigmoid(x)

def _layernorm(x, axis=-1, eps=1e-05):
    m = jnp.mean(x, axis=axis, keepdims=True)
    v = jnp.var(x, axis=axis, keepdims=True)
    return (x - m) / jnp.sqrt(v + eps)

def _scatter_add(tgt, idx, src, axis=0):
    return tgt.at[idx].add(src)

def _segment_sum(src, seg, n):
    return jax.ops.segment_sum(src, seg, n)
kernel_name = 'mk_xattn_ffn_d2_seqx_r4_a9946f'

def setup_inputs(seed: int=0):
    np.random.seed(seed)
    _w = jnp.asarray

    def _rec_inputs():
        import jax
        import jax.numpy as jnp
        _rk = jax.random.key(seed)
        x = -0.0003929 + 0.9999 * jax.random.normal(jax.random.fold_in(_rk, 1), (4, 1024, 256), jnp.float32)
        _lenS = 1024 - jax.random.randint(jax.random.fold_in(_rk, 7), (4,), 0, max(1, 1024 // 4) + 1, jnp.int32)
        _lenS2 = 77 - jax.random.randint(jax.random.fold_in(_rk, 8), (4,), 0, max(1, 77 // 4) + 1, jnp.int32)
        _ctx_1024P = jax.random.normal(jax.random.fold_in(_rk, 11), (4, 16, 256), jnp.float32)
        _ctx_1024c = jax.random.dirichlet(jax.random.fold_in(_rk, 511), 0.3 * jnp.ones((16,), jnp.float32), (4, 77))
        _ctx_1024t = jnp.einsum('bsk,bkd->bsd', _ctx_1024c, _ctx_1024P)
        _ctx_1024t = _ctx_1024t * jax.lax.rsqrt(jnp.mean(jnp.square(_ctx_1024t)) + 1e-12) * 0.953939
        ctx_1024 = 2.81802e-05 + 1.00001 * (_ctx_1024t + 0.3 * jax.random.normal(jax.random.fold_in(_rk, 611), (4, 77, 256), jnp.float32))
        return (x, ctx_1024)
    x, ctx_1024 = _rec_inputs()

    def _L0_xattn_setup():
        import jax, jax.numpy as jnp
        import numpy as np
        key = jax.random.key(seed)
        k1, k2, k3 = jax.random.split(key, 3)
        B, L, D = (8, 512, 256)
        ix = jax.random.normal(k1, (B, L, D), dtype=jnp.float32)
        iother = jax.random.normal(k2, (B, L, D), dtype=jnp.float32)
        W = jax.random.normal(k3, (D, D), dtype=jnp.float32) * (1.0 / np.sqrt(D))
        b = jnp.zeros((D,), dtype=jnp.float32)
        return {'ix': ix, 'iother': iother, 'W': W, 'b': b}
    _L0_xattn_all = _L0_xattn_setup()
    _L0_xattn_in = {k: v for k, v in _L0_xattn_all.items() if k in ('W', 'b')}
    del _L0_xattn_all

    def _L0_ffn_setup():
        import jax, jax.numpy as jnp
        import numpy as np
        EMBED_DIM = 256
        HIDDEN_DIM = 1024
        NUM_EXPERTS = 8
        TOP_K = 2
        key = jax.random.key(seed)
        ks = jax.random.split(key, 4)
        std1 = float(np.sqrt(2.0 / EMBED_DIM))
        std2 = float(np.sqrt(2.0 / HIDDEN_DIM))
        x = jax.random.normal(ks[0], (1, 512, EMBED_DIM), dtype=jnp.float32)
        w_router = jax.random.normal(ks[1], (EMBED_DIM, NUM_EXPERTS), dtype=jnp.float32) * 0.02
        w1 = jax.random.normal(ks[2], (NUM_EXPERTS, EMBED_DIM, HIDDEN_DIM), dtype=jnp.float32) * std1
        b1 = jnp.zeros((NUM_EXPERTS, HIDDEN_DIM), dtype=jnp.float32)
        w2 = jax.random.normal(ks[3], (NUM_EXPERTS, HIDDEN_DIM, EMBED_DIM), dtype=jnp.float32) * std2
        b2 = jnp.zeros((NUM_EXPERTS, EMBED_DIM), dtype=jnp.float32)
        return {'x': x, 'w_router': w_router, 'w1': w1, 'b1': b1, 'w2': w2, 'b2': b2}
    _L0_ffn_all = _L0_ffn_setup()
    _L0_ffn_in = {k: v for k, v in _L0_ffn_all.items() if k in ('w_router', 'w1', 'b1', 'w2', 'b2')}
    del _L0_ffn_all

    def _L1_xattn_setup():
        import jax, jax.numpy as jnp
        import numpy as np
        D_MODEL = 256
        B, S = (4, 512)
        key = jax.random.key(seed)
        ks = jax.random.split(key, 10)
        s = 1.0 / np.sqrt(D_MODEL)
        return {'k': jax.random.normal(ks[0], (B, S, D_MODEL), jnp.float32), 'v': jax.random.normal(ks[1], (B, S, D_MODEL), jnp.float32), 'q': jax.random.normal(ks[2], (B, S, D_MODEL), jnp.float32), 'Wk': jax.random.normal(ks[3], (D_MODEL, D_MODEL), jnp.float32) * s, 'Wv': jax.random.normal(ks[4], (D_MODEL, D_MODEL), jnp.float32) * s, 'bv': jnp.zeros((D_MODEL,), jnp.float32), 'Wq': jax.random.normal(ks[5], (D_MODEL, D_MODEL), jnp.float32) * s, 'bq': jnp.zeros((D_MODEL,), jnp.float32), 'Wo': jax.random.normal(ks[6], (D_MODEL, D_MODEL), jnp.float32) * s, 'bo': jnp.zeros((D_MODEL,), jnp.float32)}
    _L1_xattn_all = _L1_xattn_setup()
    _L1_xattn_in = {k: v for k, v in _L1_xattn_all.items() if k in ('Wk', 'Wv', 'bv', 'Wq', 'bq', 'Wo', 'bo')}
    del _L1_xattn_all

    def _L1_ffn_setup():
        import jax, jax.numpy as jnp
        import numpy as np
        EPS = 1e-05

        def act_quant(x):
            scale = 127.0 / jnp.clip(jnp.max(jnp.abs(x), axis=-1, keepdims=True), EPS, None)
            q = jnp.clip(jnp.round(x * scale), -128.0, 127.0) / scale
            return x + jax.lax.stop_gradient(q - x)

        def weight_quant(w):
            scale = 1.0 / jnp.clip(jnp.mean(jnp.abs(w)), EPS, None)
            q = jnp.clip(jnp.round(w * scale), -1.0, 1.0) / scale
            return w + jax.lax.stop_gradient(q - w)

        def bitlinear(x, w):
            return act_quant(x) @ weight_quant(w).T
        key = jax.random.key(seed)
        k1, k2, k3, k4 = jax.random.split(key, 4)
        H, I = (256, 1024)
        B, S = (4, 1024)
        init = 0.02
        x = jax.random.normal(k1, (B, S, H), dtype=jnp.float32)
        w_gate = jax.random.normal(k2, (I, H), dtype=jnp.float32) * init
        w_up = jax.random.normal(k3, (I, H), dtype=jnp.float32) * init
        w_down = jax.random.normal(k4, (H, I), dtype=jnp.float32) * init
        return {'x': x, 'w_gate': w_gate, 'w_up': w_up, 'w_down': w_down}
    _L1_ffn_all = _L1_ffn_setup()
    _L1_ffn_in = {k: v for k, v in _L1_ffn_all.items() if k in ('w_gate', 'w_up', 'w_down')}
    del _L1_ffn_all
    return {'x': x, 'ctx_1024': ctx_1024, 'L0_xattn_W': _L0_xattn_in['W'], 'L0_xattn_b': _L0_xattn_in['b'], 'L0_ffn_w_router': _L0_ffn_in['w_router'], 'L0_ffn_w1': _L0_ffn_in['w1'], 'L0_ffn_b1': _L0_ffn_in['b1'], 'L0_ffn_w2': _L0_ffn_in['w2'], 'L0_ffn_b2': _L0_ffn_in['b2'], 'L1_xattn_Wk': _L1_xattn_in['Wk'], 'L1_xattn_Wv': _L1_xattn_in['Wv'], 'L1_xattn_bv': _L1_xattn_in['bv'], 'L1_xattn_Wq': _L1_xattn_in['Wq'], 'L1_xattn_bq': _L1_xattn_in['bq'], 'L1_xattn_Wo': _L1_xattn_in['Wo'], 'L1_xattn_bo': _L1_xattn_in['bo'], 'L1_ffn_w_gate': _L1_ffn_in['w_gate'], 'L1_ffn_w_up': _L1_ffn_in['w_up'], 'L1_ffn_w_down': _L1_ffn_in['w_down']}

def reference(x, ctx_1024, L0_xattn_W, L0_xattn_b, L0_ffn_w_router, L0_ffn_w1, L0_ffn_b1, L0_ffn_w2, L0_ffn_b2, L1_xattn_Wk, L1_xattn_Wv, L1_xattn_bv, L1_xattn_Wq, L1_xattn_bq, L1_xattn_Wo, L1_xattn_bo, L1_ffn_w_gate, L1_ffn_w_up, L1_ffn_w_down):
    import jax
    import jax.numpy as jnp

    def _L0_xattn_ref(ix, iother, W, b):
        import jax, jax.numpy as jnp
        import numpy as np
        ex = ix @ W.T + b
        eother = iother @ W.T + b
        align = jnp.einsum('bld,bmd->blm', ex, eother)
        align = jax.nn.softmax(align, axis=-1)
        aligned = jnp.einsum('blm,bmd->bld', align, iother)
        return aligned

    def _L0_ffn_ref(x, w_router, w1, b1, w2, b2):
        import jax, jax.numpy as jnp
        import numpy as np
        EMBED_DIM = 256
        HIDDEN_DIM = 1024
        NUM_EXPERTS = 8
        TOP_K = 2
        orig_shape = x.shape
        xf = x.reshape(-1, EMBED_DIM)
        logits = xf @ w_router
        probs = jax.nn.softmax(logits, axis=-1)
        topk_w, topk_idx = jax.lax.top_k(probs, TOP_K)
        mask = jax.nn.one_hot(topk_idx, NUM_EXPERTS, dtype=xf.dtype)
        weights = jnp.sum(topk_w[..., None] * mask, axis=1)
        h = jnp.einsum('te,ieh->tih', xf, w1) + b1
        h = jax.nn.gelu(h)
        out = jnp.einsum('tih,ihe->tie', h, w2) + b2
        out = jnp.sum(out * weights[..., None], axis=1)
        return out.reshape(orig_shape)

    def _L1_xattn_ref(k, v, q, Wk, Wv, bv, Wq, bq, Wo, bo):
        import jax, jax.numpy as jnp
        import numpy as np
        D_MODEL = 256
        B, S = (4, 512)
        kp = jnp.einsum('bsd,ed->bse', k, Wk)
        vp = jnp.einsum('bsd,ed->bse', v, Wv) + bv
        qp = jnp.einsum('bsd,ed->bse', q, Wq) + bq
        scale = 1.0 / jnp.sqrt(jnp.float32(kp.shape[-1]))
        scores = jnp.einsum('bqd,bkd->bqk', qp, kp) * scale
        probs = jax.nn.softmax(scores, axis=-1)
        ctx = jnp.einsum('bqk,bkd->bqd', probs, vp)
        return jnp.einsum('bqd,ed->bqe', ctx, Wo) + bo

    def _L1_ffn_ref(x, w_gate, w_up, w_down):
        import jax, jax.numpy as jnp
        import numpy as np
        EPS = 1e-05

        def act_quant(x):
            scale = 127.0 / jnp.clip(jnp.max(jnp.abs(x), axis=-1, keepdims=True), EPS, None)
            q = jnp.clip(jnp.round(x * scale), -128.0, 127.0) / scale
            return x + jax.lax.stop_gradient(q - x)

        def weight_quant(w):
            scale = 1.0 / jnp.clip(jnp.mean(jnp.abs(w)), EPS, None)
            q = jnp.clip(jnp.round(w * scale), -1.0, 1.0) / scale
            return w + jax.lax.stop_gradient(q - w)

        def bitlinear(x, w):
            return act_quant(x) @ weight_quant(w).T
        g = bitlinear(x, w_gate)
        u = bitlinear(x, w_up)
        h = jnp.square(jax.nn.relu(g)) * u
        return bitlinear(h, w_down)
    x = x + _L0_xattn_ref(_layernorm(x, axis=-1), ctx_1024, L0_xattn_W, L0_xattn_b)
    x = x + _L0_ffn_ref(_layernorm(x, axis=-1), L0_ffn_w_router, L0_ffn_w1, L0_ffn_b1, L0_ffn_w2, L0_ffn_b2)
    x = x + _L1_xattn_ref(ctx_1024, ctx_1024, _layernorm(x, axis=-1), L1_xattn_Wk, L1_xattn_Wv, L1_xattn_bv, L1_xattn_Wq, L1_xattn_bq, L1_xattn_Wo, L1_xattn_bo)
    x = x + _L1_ffn_ref(_layernorm(x, axis=-1), L1_ffn_w_gate, L1_ffn_w_up, L1_ffn_w_down)
    return x

_drawn_inputs = setup_inputs


def setup_inputs(seed=0):
    import zlib

    import numpy as np

    out = dict(_drawn_inputs(seed))
    spreads = {'L0_xattn_b': (0.0, 0.1),
     'L0_ffn_b1': (0.0, 0.524),
     'L0_ffn_b2': (0.0, 0.528),
     'L1_xattn_bv': (0.0, 0.1),
     'L1_xattn_bq': (0.0, 0.636),
     'L1_xattn_bo': (0.0, 0.1)}
    factors = {'L1_ffn_w_gate': 8.0, 'L1_ffn_w_up': 8.0, 'L1_ffn_w_down': 8.0}
    for name, (base, spread) in spreads.items():
        noise = np.random.default_rng([zlib.crc32(name.encode()), seed]).standard_normal(out[name].shape)
        drawn = base * np.exp(spread * noise) if base else spread * noise
        out[name] = jnp.asarray(drawn.astype(out[name].dtype))
    for name, factor in factors.items():
        out[name] = (out[name] * factor).astype(out[name].dtype)
    return out
```

```python
from contextlib import ExitStack

import concourse.bass as bass
from concourse import mybir

ALU = mybir.AluOpType
ACT = mybir.ActivationFunctionType
AX = mybir.AxisListType
F32 = mybir.dt.float32
F16 = mybir.dt.float16
BF16 = mybir.dt.bfloat16
I32 = mybir.dt.int32
U32 = mybir.dt.uint32

P = 128
B, S, D = 4, 1024, 256
M = 77
E, TOP, H = 8, 2, 1024
KD, KH = D // P, H // P
TOK = B * S
ST, TJ = 2, 4
TILES = TOK // P
BLK = 256
NBLK = TOK * TOP // BLK + E - 1
REGION = TOK + BLK
NROW = 3 * KD + E * KH
LN_EPS = 1e-5
Q_EPS = 1e-5
MAGIC = 1.5 * 2.0 ** 23


class Order:

    def __init__(self, eng, sem):
        self.eng, self.sem, self.n = eng, sem, 0

    def did(self, instruction):
        self.n += 1
        instruction.then_inc(self.sem, 1)

    def sync(self):
        if self.n:
            self.eng.wait_ge(self.sem, self.n)

    def clear(self):
        self.sync()
        self.eng.sem_clear(self.sem)
        self.n = 0


def build(nc, x, ctx_in, w0, b0, wr, w1, b1, w2, b2, wk, wv, bv, wq, bq, wo, bo, wg, wu, wd, out):
    x_rows = x.rearrange("b s d -> (b s) d")
    out_rows = out.rearrange("b s d -> (b s) d")
    x1_rows = nc.dram_tensor("x1_rows", (TOK, D), F32, kind="Internal").ap()
    sent = nc.dram_tensor("sent", (E * REGION, 2 * D), F16, kind="Internal").ap()
    made = nc.dram_tensor("made", (NBLK * BLK, D), F32, kind="Internal").ap()

    with ExitStack() as keep:
        def sb(name, shape, dt, stack=keep):
            return stack.enter_context(nc.sbuf_tensor(name, shape, dt))

        def sem(name):
            return keep.enter_context(nc.semaphore(name))

        def pair(name):
            return [sem(f"{name}{s}") for s in range(ST)]

        def pair_sb(name, shape, dt, stack):
            return [sb(f"{name}{s}", shape, dt, stack) for s in range(ST)]

        ps = keep.enter_context(nc.psum_tensor("ps", [P, 8, 512], F32))

        ident = sb("ident", [P, P], F32)
        ident16 = sb("ident16", [P, P], F16)
        identb = sb("identb", [P, P], BF16)
        ones = sb("ones", [P, P], F32)
        onesb = sb("onesb", [P, P], BF16)
        before = sb("before", [P, P], BF16)
        iota8 = sb("iota8", [P, E], F32)
        magic = sb("magic", [P, 1], F32)
        wr_sb = sb("wr_sb", [P, KD, E], F32)
        ctx_sb = sb("ctx_sb", [M, B, D], F32)
        g0 = sb("g0", [P, KD, B * M], F32)
        c0 = sb("c0", [1, B * M], F32)
        g1 = sb("g1", [P, KD, B * M], F32)
        c1 = sb("c1", [1, B * M], F32)
        vo = sb("vo", [M, B, D], F32)
        bcols = sb("bcols", [P, NROW], F32)
        b2_sb = sb("b2_sb", [P, E, D], F32)
        expert = sb("expert", [P, TILES * TOP], F32)
        weight = sb("weight", [P, TILES * TOP], F32)
        rank = sb("rank", [P, TILES * TOP], F32)
        y_slot = sb("y_slot", [P, TILES * TOP], U32)
        prior = sb("prior", [P, TJ + 1, E], BF16)
        block_expert = sb("block_expert", [1, NBLK + 1], I32)
        block_row = sb("block_row", [1, NBLK + 1], I32)
        pad_row = sb("pad_row", [1, E], I32)

        s12 = ExitStack()
        w1h = sb("w1h", [P, E * KD, H], F16, s12)
        w1l = sb("w1l", [P, E * KD, H], F16, s12)
        w2h = sb("w2h", [P, E * KH, D], F16, s12)
        w2l = sb("w2l", [P, E * KH, D], F16, s12)

        s0 = ExitStack()
        w0_sb = sb("w0_sb", [P, KD, D], F32, s0)
        wq_sb = sb("wq_sb", [P, KD, D], F32, s0)
        wk_sb = sb("wk_sb", [P, KD, D], F32, s0)
        wv_sb = sb("wv_sb", [P, KD, D], F32, s0)
        wo_sb = sb("wo_sb", [P, KD, D], F32, s0)
        bcols_in = sb("bcols_in", [NROW, P], F32, s0)
        bo_row = sb("bo_row", [1, D], F32, s0)
        w0T = sb("w0T", [P, KD, D], F32, s0)
        wkT = sb("wkT", [P, KD, D], F32, s0)
        wvT = sb("wvT", [P, KD, D], F32, s0)
        woT = sb("woT", [P, KD, D], F32, s0)
        ctxT = sb("ctxT", [P, KD, B * M], F32, s0)
        eoT = sb("eoT", [P, KD, B * M], F32, s0)
        kpT = sb("kpT", [P, KD, B * M], F32, s0)
        vpT = sb("vpT", [P, KD, B * M], F32, s0)
        s0.close()

        s1 = ExitStack()
        xa = pair_sb("xa", [P, TJ, D], F32, s1)
        xn = pair_sb("xn", [P, TJ, D], F32, s1)
        xT = pair_sb("xT", [P, KD, TJ * P], F32, s1)
        pr = pair_sb("pr", [P, TJ, M], F32, s1)
        prT = pair_sb("prT", [M, TJ * P], F32, s1)
        rows = pair_sb("rows", [P, TJ, 2 * D], F16, s1)
        stage = pair_sb("stage", [P, 1024], F32, s1)
        stat = pair_sb("stat", [P, TJ, 6], F32, s1)
        mv = pair_sb("mv", [P, TJ, 2], F32, s1)
        nt = pair_sb("nt", [P, 4, TJ], F32, s1)
        nmax = pair_sb("nmax", [P, TJ], F32, s1)
        esum = pair_sb("esum", [P, TJ], F32, s1)
        rinv = pair_sb("rinv", [P, TJ], F32, s1)
        pe_ = pair_sb("pe_", [P, TJ, E], F32, s1)
        top = pair_sb("top", [P, TJ, E], F32, s1)
        topi = pair_sb("topi", [P, TJ, E], U32, s1)
        ex2 = pair_sb("ex2", [P, TJ * TOP], F32, s1)
        hot = pair_sb("hot", [P, TJ * TOP, E], F32, s1)
        picks = pair_sb("picks", [P, TJ, E], BF16, s1)
        pri = pair_sb("pri", [P, TJ, E], BF16, s1)
        prod = pair_sb("prod", [P, TJ * TOP, E], F32, s1)
        rk2 = pair_sb("rk2", [P, TJ * TOP], F32, s1)
        x_slot = pair_sb("x_slot", [P, TJ * TOP], U32, s1)
        zrow = sb("zrow", [P, 2, 2 * D], F16, s1)
        s1.close()

        st = ExitStack()
        cnt = sb("cnt", [P, E], F32, st)
        nb = sb("nb", [P, E], F32, st)
        cum = sb("cum", [P, E + 1], F32, st)
        yhot = sb("yhot", [P, TILES * TOP, E], F32, st)
        ybase = sb("ybase", [P, TILES * TOP], F32, st)
        bnum = sb("bnum", [1, NBLK + 1], F32, st)
        bcmp = sb("bcmp", [1, NBLK + 1, E], F32, st)
        bcnt = sb("bcnt", [1, NBLK + 1, E], F32, st)
        bexp = sb("bexp", [1, NBLK + 1], F32, st)
        bcum = sb("bcum", [1, NBLK + 1], F32, st)
        prow = sb("prow", [1, E], F32, st)
        st.close()

        s2 = ExitStack()
        bx = sb("bx", [P, 2, 2 * D], F16, s2)
        bxT = sb("bxT", [P, 2 * KD, BLK], F16, s2)
        hid = sb("hid", [P, KH, BLK], F32, s2)
        hidh = sb("hidh", [P, KH, BLK], F16, s2)
        hidl = sb("hidl", [P, KH, BLK], F16, s2)
        by = sb("by", [P, 2, D], F32, s2)
        s2.close()
        s12.close()

        s3 = ExitStack()
        gy = sb("gy", [P, TILES * TOP, D], F32, s3)
        tern = [sb(f"tern{n}", [P, H // P * D], F32, s3) for n in range(2)]
        ternq = [sb(f"ternq{n}", [P, H // P * D], BF16, s3) for n in range(2)]
        wgT = sb("wgT", [P, KD, H], BF16, s3)
        wuT = sb("wuT", [P, KD, H], BF16, s3)
        wdT = sb("wdT", [P, KH, D], BF16, s3)
        tsum = sb("tsum", [P, 3], F32, s3)
        tscale = sb("tscale", [P, 3], F32, s3)
        wmean = sb("wmean", [P, 3], F32, s3)
        xc = pair_sb("xc", [P, TJ, D], F32, s3)
        xn3 = pair_sb("xn3", [P, TJ, D], F32, s3)
        xT3 = pair_sb("xT3", [P, KD, TJ * P], F32, s3)
        pr3 = pair_sb("pr3", [P, TJ, M], F32, s3)
        prT3 = pair_sb("prT3", [M, TJ * P], F32, s3)
        stat3 = pair_sb("stat3", [P, TJ, 6], F32, s3)
        mv3 = pair_sb("mv3", [P, TJ, 2], F32, s3)
        nt3 = pair_sb("nt3", [P, 4, TJ], F32, s3)
        nmax3 = pair_sb("nmax3", [P, TJ], F32, s3)
        esum3 = pair_sb("esum3", [P, TJ], F32, s3)
        rinv3 = pair_sb("rinv3", [P, TJ], F32, s3)
        xmax = pair_sb("xmax", [P, TJ], F32, s3)
        xscale = pair_sb("xscale", [P, TJ], F32, s3)
        hfac = pair_sb("hfac", [P, 2, TJ], F32, s3)
        xq = pair_sb("xq", [P, TJ, D], BF16, s3)
        xqT = pair_sb("xqT", [P, KD, TJ * P], BF16, s3)
        relu = pair_sb("relu", [P, H], F32, s3)
        hh = pair_sb("hh", [P, H], F32, s3)
        hr = pair_sb("hr", [P, H], F32, s3)
        hq = pair_sb("hq", [P, H], BF16, s3)
        hqT = pair_sb("hqT", [P, KH, P], BF16, s3)
        hm = pair_sb("hm", [P, 5, TJ], F32, s3)
        xo = pair_sb("xo", [P, TJ, D], F32, s3)
        s3.close()

        consts_made, pool_order, vec_order = sem("consts_made"), sem("pool_order"), sem("vec_order")
        ctx_in_sem, weights_in = sem("ctx_loaded"), sem("weights_loaded")
        setup_mm, setup_out, act_order = sem("setup_mm"), sem("setup_out"), sem("act_order")
        stage_full, high_done, low_done = pair("stage_full"), pair("high_done"), pair("low_done")
        x_in, ln1, xT1_mm, xT1, score_mm, score_max, probs = (
            pair(n) for n in ("x_in", "ln1", "xT1_mm", "xT1", "score_mm", "score_max", "probs"))
        probsT_mm, probsT, attn_mm, x1_made, x1_out, ln2 = (
            pair(n) for n in ("probsT_mm", "probsT", "attn_mm", "x1_made", "x1_out", "ln2"))
        xT2_mm, xT2, logit_mm, logit_max, gates, picked, rank_mm, placed, rows_sent = (
            pair(n) for n in ("xT2_mm", "xT2", "logit_mm", "logit_max", "gates", "picked", "rank_mm",
                              "placed", "rows_sent"))
        rows_free = pair("rows_free")
        zeros_made, count_mm, tables, pads_sent = sem("zeros_made"), sem("count_mm"), sem("tables"), sem("pads_sent")
        y_placed = sem("y_placed")
        bx_in, bxT_mm, bxT_made = sem("bx_in"), sem("bxT_mm"), sem("bxT_made")
        hid_mm, hid_made, hid_split = sem("hid_mm"), sem("hid_made"), sem("hid_split")
        by_mm, by_made, by_out = sem("by_mm"), sem("by_made"), sem("by_out")
        tern_in = [sem(f"tern_in{n}") for n in range(2)]
        tern_sum, tern_total, tern_quant, tern_T, tern_out = (
            sem(n) for n in ("tern_sum", "tern_total", "tern_quant", "tern_T", "tern_out"))
        y_in, x1_in, ln3, xT3_mm, xT3_made, score3_mm, score3_max, probs3 = (
            pair(n) for n in ("y_in", "x1_in", "ln3", "xT3_mm", "xT3_made", "score3_mm", "score3_max", "probs3"))
        probsT3_mm, probsT3, attn3_mm, xq_made, xqT_mm, xqT_made = (
            pair(n) for n in ("probsT3_mm", "probsT3", "attn3_mm", "xq_made", "xqT_mm", "xqT_made"))
        gate_mm, relu_made, relu2_made, h_made, h_scale, h_round, hq_made, hqT_mm, hqT_made, down_mm = (
            pair(n) for n in ("gate_mm", "relu_made", "relu2_made", "h_made", "h_scale", "h_round", "hq_made",
                              "hqT_mm", "hqT_made", "down_mm"))
        xo_made, out_done = pair("xo_made"), pair("out_done")
        SMALL = 16 * 12
        SENT = 16 * TJ * TOP * B

        def bank_wide(s):
            return ps[:, 4 * s:4 * s + 2, :]

        def bank_c(s):
            return ps[:, 4 * s + 2, :]

        def bank_d(s):
            return ps[:, 4 * s + 3, :]

        def by_tile(ap, width):
            return ap.rearrange("p (j m) -> p j m", j=TJ)[:, :, 0:width]

        def token_rows(rows_ap, b, s):
            return rows_ap[bass.ds(b * S + s * TJ * P, TJ * P), :].rearrange("(j p) d -> p j d", p=P)

        def block_rows(rows_ap, row):
            return rows_ap[bass.ds(row, BLK), :].rearrange("(h p) c -> p h c", p=P)

        def stage_piece(n):
            return n // 4, n % 4 // 2, n % 2

        def weight_at(which, half, e):
            if which == 0:
                return bass.ds(e * KD + half, 1)
            return bass.ds(e * KH + half * (KH // 2), KH // 2)

        def staged(n, which):
            k = 1 if which == 0 else KH // 2
            return stage[n % 2][:].rearrange("p (k c) -> p k c", k=k)

        block = keep.enter_context(nc.Block())

        @block.sync
        def _(sp):
            for s in range(ST):
                sp.sem_inc(x1_out[s], 16)
                sp.sem_inc(low_done[s], 1)
            sp.dma_start(ctx_sb[:], ctx_in.rearrange("b m d -> m b d")).then_inc(ctx_in_sem, 16)
            for dst, src in ((w0_sb, w0), (wk_sb, wk), (wq_sb, wq), (wv_sb, wv), (wo_sb, wo), (wr_sb, wr)):
                sp.dma_start(dst[:], src.rearrange("(k p) d -> p k d", p=P)).then_inc(weights_in, 16)
            for n, src in enumerate((b0, bq, bv)):
                sp.dma_start(bcols_in[n * KD:(n + 1) * KD, :], src.rearrange("(k p) -> k p", p=P)).then_inc(weights_in, 16)
            sp.dma_start(bo_row[:], bo.rearrange("(a n) -> a n", a=1)).then_inc(weights_in, 16)
            sp.dma_start(bcols_in[3 * KD:, :], b1.rearrange("e (c p) -> (e c) p", p=P)).then_inc(weights_in, 16)
            sp.dma_start(b2_sb[:].rearrange("p e n -> p (e n)"),
                         b2.rearrange("(a e) n -> a (e n)", a=1).to_broadcast([P, E * D])).then_inc(weights_in, 16)
            sp.wait_ge(setup_out, 13)

            w1_p = w1.rearrange("e (k p) n -> (e k) p n", p=P)
            w2_p = w2.rearrange("e (h k p) n -> (e h) p k n", p=P, h=2)
            with sp.Fori(0, B) as b:
                for s in range(ST):
                    sp.wait_ge(x1_out[s], 16 * b + 16)
                    sp.dma_start(xa[s][:], token_rows(x_rows, b, s)).then_inc(x_in[s], 16)
                for n in range(8):
                    e_off, which, half = stage_piece(n)
                    sp.wait_ge(low_done[n % 2], b * 4 + n // 2 + 1)
                    if which == 0:
                        src = w1_p[bass.ds(b * 4 + e_off * 2 + half, 1)].rearrange("o p n -> p o n")
                    else:
                        src = w2_p[bass.ds(b * 4 + e_off * 2 + half, 1)].rearrange("o p k n -> (o p) k n")
                    sp.dma_start(staged(n, which), src).then_inc(stage_full[n % 2], 16)
                for s in range(ST):
                    sp.wait_ge(x1_made[s], b + 1)
                    sp.dma_start(token_rows(x1_rows, b, s), xa[s][:]).then_inc(x1_out[s], 16)

            sp.wait_ge(zeros_made, 1)
            sp.wait_ge(tables, 1)
            for e in range(E):
                row = sp.value_load(pad_row[0:1, e:e + 1], min_val=0, max_val=E * REGION - BLK)
                sp.dma_start(block_rows(sent, row), zrow[:]).then_inc(pads_sent, 16)
            for s in range(ST):
                sp.wait_ge(rows_sent[s], SENT)
            sp.wait_ge(pads_sent, 16 * E)
            sp.wait_ge(y_placed, 1)

            def load_block(n):
                row = sp.value_load(block_row[0:1, bass.ds(n, 1)], min_val=0, max_val=E * REGION - BLK)
                sp.dma_start(bx[:], block_rows(sent, row)).then_inc(bx_in, 16)

            load_block(0)
            with sp.Fori(0, NBLK) as n:
                sp.wait_ge(bxT_mm, n + 1)
                load_block(n + 1)
                sp.wait_ge(by_made, 2 * n + 3)
                sp.dma_start(block_rows(made, n * BLK), by[:]).then_inc(by_out, 16)

            for s in range(ST):
                sp.wait_ge(x1_out[s], 16 * B + 16)
            sp.wait_ge(by_out, 16 * NBLK + 16)
            tern_src = [w.rearrange("(c p) n -> p c n", p=P) for w in (wg, wu, wd)]

            def load_ternary(n):
                c = H // P if n < 2 else KD
                sp.dma_start(tern[n % 2][:].rearrange("p (c n) -> p c n", c=c), tern_src[n])\
                  .then_inc(tern_in[n % 2], 16)

            load_ternary(0)
            load_ternary(1)
            for s in range(ST):
                sp.dma_start(xc[s][:], token_rows(x1_rows, 0, s)).then_inc(x1_in[s], 16)
            sp.wait_ge(tern_quant, 1)
            load_ternary(2)
            with sp.Fori(0, B - 1) as b:
                for s in range(ST):
                    sp.wait_ge(xo_made[s], TJ * b + TJ)
                    sp.dma_start(token_rows(out_rows, b, s), xo[s][:]).then_inc(out_done[s], 16)
                    sp.dma_start(xc[s][:], token_rows(x1_rows, b + 1, s)).then_inc(x1_in[s], 16)
            for s in range(ST):
                sp.wait_ge(xo_made[s], TJ * B)
                sp.dma_start(token_rows(out_rows, B - 1, s), xo[s][:]).then_inc(out_done[s], 16)
            for s in range(ST):
                sp.wait_ge(out_done[s], 16 * B + 16)

        @block.gpsimd
        def _(pool):
            g = nc.gpsimd
            o = Order(pool, pool_order)
            g.memset(ident[:], 0.0)
            g.memset(before[:], 1.0)
            g.memset(ones[:], 1.0)
            g.memset(onesb[:], 1.0)
            g.memset(magic[:], MAGIC)
            g.memset(prior[:], 0.0)
            o.did(g.iota(iota8[:], [[1, E]], base=0, channel_multiplier=0, allow_small_or_imprecise_dtypes=True))
            o.sync()
            g.affine_select(out=ident[:], in_=ident[:], compare_op=ALU.not_equal, fill=1.0,
                            base=0, pattern=[[-1, P]], channel_multiplier=1)
            o.did(g.affine_select(out=before[:], in_=before[:], compare_op=ALU.is_gt, fill=0.0,
                                  base=0, pattern=[[1, P]], channel_multiplier=-1))
            o.sync()
            g.tensor_copy(ident16[:], ident[:])
            g.tensor_copy(identb[:], ident[:]).then_inc(consts_made, 1)
            pool.wait_ge(setup_out, 13)
            g.memset(zrow[:], 0.0).then_inc(zeros_made, 1)

            turn = [pool.alloc_register(f"turn{s}") for s in range(ST)]
            for s in range(ST):
                pool.reg_mov(turn[s], 2)
            with pool.Fori(0, B) as b:
                for n in range(8):
                    e_off, which, half = stage_piece(n)
                    at = weight_at(which, half, b * 2 + e_off)
                    hi, lo = ((w1h, w1l), (w2h, w2l))[which]
                    pool.wait_ge(high_done[n % 2], b * 4 + n // 2 + 1)
                    g.tensor_tensor(lo[:, at, :], staged(n, which), hi[:, at, :], ALU.subtract)\
                     .then_inc(low_done[n % 2], 1)
                for s in range(ST):
                    pool.wait_ge(placed[s], turn[s])
                    pool.reg_add(turn[s], turn[s], 1)
                    for n in range(TJ * TOP):
                        g.indirect_dma_start(sent, bass.IndirectOffsetOnAxis(x_slot[s][:, n:n + 1], 0),
                                             rows[s][:, n // TOP, :], None).then_inc(rows_sent[s], 16)
                for s in range(ST):
                    pool.wait_ge(rows_sent[s], 16 * TJ * TOP * b + 16 * TJ * TOP)
                    pool.sem_inc(rows_free[s], 1)
            for s in range(ST):
                pool.wait_ge(rows_sent[s], SENT)
                pool.wait_ge(x1_out[s], 16 * B + 16)
            g.iota(bnum[:], [[1, NBLK + 1]], base=0, channel_multiplier=0, allow_small_or_imprecise_dtypes=True)
            g.iota(prow[:], [[REGION, E]], base=0, channel_multiplier=0, allow_small_or_imprecise_dtypes=True)\
             .then_inc(consts_made, 1)

            pool.wait_ge(by_out, 16 * NBLK + 16)
            for b in range(B):
                for s in range(ST):
                    if b:
                        pool.wait_ge(y_in[s], 16 * TJ * TOP * b)
                    for n in range(TJ * TOP):
                        m = (b * ST + s) * TJ * TOP + n
                        g.indirect_dma_start(gy[:, m, :], None, made,
                                             bass.IndirectOffsetOnAxis(y_slot[:, m:m + 1], 0)).then_inc(y_in[s], 16)

        @block.scalar
        def _(act):
            a = nc.scalar
            BM = B * M

            def out_of(n, dst, src):
                act.wait_ge(setup_mm, n)
                a.activation(dst, src, ACT.Copy).then_inc(setup_out, 1)

            def two_pieces(bank):
                return ps[:, bank, :].rearrange("p (k n) -> p k n", k=KD)

            act.wait_ge(weights_in, SMALL)
            out_of(1, ctxT[:], ps[:, 0:2, 0:BM])
            out_of(2, bcols[:], ps[:, 6, 0:NROW])
            out_of(3, w0T[:], two_pieces(2))
            out_of(4, wkT[:], two_pieces(3))
            out_of(5, wvT[:], two_pieces(4))
            out_of(6, woT[:], two_pieces(5))
            out_of(7, kpT[:], ps[:, 0:2, 0:BM])
            act.wait_ge(setup_out, 2)
            act.wait_ge(setup_mm, 8)
            for k in range(KD):
                last = a.activation(eoT[:, k, :], ps[:, 2 + k, 0:BM], ACT.Identity, bias=bcols[:, k:k + 1])
            last.then_inc(setup_out, 1)
            act.wait_ge(setup_mm, 9)
            for k in range(KD):
                last = a.activation(vpT[:, k, :], ps[:, 4 + k, 0:BM], ACT.Identity, bias=bcols[:, 2 * KD + k:2 * KD + k + 1])
            last.then_inc(setup_out, 1)
            scale = float(D) ** -0.5
            act.wait_ge(setup_mm, 10)
            a.activation(g0[:], ps[:, 0:2, 0:BM], ACT.Copy)
            a.activation(c0[:], ps[0:1, 6, 0:BM], ACT.Copy).then_inc(setup_out, 1)
            act.wait_ge(setup_mm, 11)
            a.activation(g1[:], ps[:, 2:4, 0:BM], ACT.Copy, scale=scale)
            a.activation(c1[:], ps[0:1, 7, 0:BM], ACT.Copy, scale=scale).then_inc(setup_out, 1)
            for h in range(2):
                out_of(12 + h, vo[:, 2 * h:2 * h + 2, :], ps[0:M, 4 + h, :].rearrange("p (b n) -> p b n", b=2))

            def high_half(b, n):
                e_off, which, half = stage_piece(n)
                at = weight_at(which, half, b * 2 + e_off)
                act.wait_ge(stage_full[n % 2], 16 * (b * 4 + n // 2) + 16)
                a.activation((w1h, w2h)[which][:, at, :], staged(n, which), ACT.Copy).then_inc(high_done[n % 2], 1)

            def exponentials(probs_out, scores, neg_max, sums, done):
                for j in range(TJ):
                    last = a.activation(probs_out[:, j, :], scores[:, j, :], ACT.Exp,
                                        bias=neg_max[:, j:j + 1], accum_out=sums[:, j:j + 1])
                last.then_inc(done, 1)

            with act.Fori(0, B) as b:
                for s in range(ST):
                    act.wait_ge(xT1_mm[s], b + 1)
                    a.activation(xT[s][:], bank_wide(s), ACT.Copy).then_inc(xT1[s], 1)
                for n in range(0, 2):
                    high_half(b, n)
                for s in range(ST):
                    act.wait_ge(score_max[s], b + 1)
                    exponentials(pr[s], by_tile(bank_c(s), M), nmax[s], esum[s], probs[s])
                for s in range(ST):
                    act.wait_ge(probsT_mm[s], b + 1)
                    a.activation(prT[s][:], bank_d(s)[0:M, :], ACT.Copy).then_inc(probsT[s], 1)
                for n in range(2, 5):
                    high_half(b, n)
                for s in range(ST):
                    act.wait_ge(xT2_mm[s], b + 1)
                    a.activation(xT[s][:], bank_wide(s), ACT.Copy).then_inc(xT2[s], 1)
                for s in range(ST):
                    act.wait_ge(logit_max[s], b + 1)
                    logits = bank_c(s)[:, 0:TJ * E].rearrange("p (j m) -> p j m", j=TJ)
                    exponentials(pe_[s], logits, nmax[s], esum[s], gates[s])
                for n in range(5, 8):
                    high_half(b, n)

            act.wait_ge(y_placed, 1)
            act.wait_ge(tables, 1)
            for s in range(ST):
                act.wait_ge(rows_sent[s], SENT)
            with act.Fori(0, NBLK) as n:
                e = act.value_load(block_expert[0:1, bass.ds(n, 1)], min_val=0, max_val=E - 1)
                for c in range(KH):
                    act.wait_ge(hid_mm, KH * n + c + 1)
                    bias = bcols[:, bass.ds(e * KH + (3 * KD + c), 1)]
                    act.wait_ge(tables, 1)
                    a.activation(hid[:, c, :], ps[:, c % 4, 0:BLK], ACT.Gelu_apprx_tanh, bias=bias)\
                     .then_inc(hid_made, 1)

            for n in range(3):
                act.wait_ge(tern_in[n % 2], 16 * (n // 2 + 1))
                if n == 2:
                    act.wait_ge(tern_T, 1)
                a.activation(ternq[n % 2][:], tern[n % 2][:], ACT.Abs, accum_out=tsum[:, n:n + 1])\
                 .then_inc(tern_sum, 1)

            with act.Fori(0, B) as b:
                for s in range(ST):
                    act.wait_ge(xT3_mm[s], b + 1)
                    a.activation(xT3[s][:], bank_wide(s), ACT.Copy).then_inc(xT3_made[s], 1)
                for s in range(ST):
                    act.wait_ge(score3_max[s], b + 1)
                    exponentials(pr3[s], by_tile(bank_c(s), M), nmax3[s], esum3[s], probs3[s])
                for s in range(ST):
                    act.wait_ge(probsT3_mm[s], b + 1)
                    a.activation(prT3[s][:], bank_d(s)[0:M, :], ACT.Copy).then_inc(probsT3[s], 1)
                for s in range(ST):
                    act.wait_ge(xqT_mm[s], b + 1)
                    a.activation(xqT[s][:], bank_c(s).bitcast(BF16).rearrange("p (k n) -> p k n", k=KD), ACT.Copy)\
                     .then_inc(xqT_made[s], 1)
                for j in range(TJ + 1):
                    if j < TJ:
                        for half in range(2):
                            cols = slice(half * 512, half * 512 + 512)
                            for s in range(ST):
                                t = TJ * b + j
                                act.wait_ge(gate_mm[s], 2 * t + half + 1)
                                a.activation(relu[s][:, cols], ps[:, 4 * s, :], ACT.Relu).then_inc(relu_made[s], 1)
                                act.wait_ge(relu_made[s], 2 * t + half + 1)
                                a.activation(relu[s][:, cols], relu[s][:, cols], ACT.Square)\
                                 .then_inc(relu2_made[s], 1)
                    if j >= 1:
                        for s in range(ST):
                            act.wait_ge(hqT_mm[s], TJ * b + j)
                            a.activation(hqT[s][:], bank_c(s).bitcast(BF16).rearrange("p (c n) -> p c n", c=KH),
                                         ACT.Copy).then_inc(hqT_made[s], 1)
                    if j < TJ:
                        for s in range(ST):
                            act.wait_ge(h_scale[s], TJ * b + j + 1)
                            a.activation(hr[s][:], hh[s][:], ACT.Identity, bias=magic[:, 0:1],
                                         scale=hm[s][:, 3, j:j + 1]).then_inc(h_round[s], 1)

        @block.vector
        def _(dve):
            for s in range(ST):
                dve.sem_inc(rows_free[s], 1)
                dve.sem_inc(out_done[s], 16)
            dve.sem_inc(by_out, 16)
            v = nc.vector
            o = Order(dve, vec_order)

            def layer_norm(src, dst, stat_, mv_, nt_):
                for j in range(TJ):
                    last = v.bn_stats(stat_[:, j, :], src[:, j, :])
                o.did(last)
                o.sync()
                for j in range(TJ):
                    last = v.bn_aggr(mv_[:, j, :], stat_[:, j, :])
                o.did(last)
                o.sync()
                ve, y, minus_half, t = (nt_[:, n, :] for n in range(4))
                o.did(v.tensor_scalar(ve, mv_[:, :, 1], LN_EPS, None, ALU.add))
                o.sync()
                v.tensor_scalar(minus_half, ve, -0.5, None, ALU.mult)
                o.did(v.tensor_scalar(t.bitcast(I32), ve.bitcast(I32), 1, None, ALU.logical_shift_right))
                o.sync()
                o.did(v.tensor_scalar(y.bitcast(I32), t.bitcast(I32), -1.0, float(0x5F3759DF), ALU.mult, ALU.add))
                for _ in range(3):
                    o.sync()
                    o.did(v.tensor_tensor(t, y, y, ALU.mult))
                    o.sync()
                    o.did(v.tensor_tensor(t, t, minus_half, ALU.mult))
                    o.sync()
                    o.did(v.scalar_tensor_tensor(y, t, 1.5, y, ALU.add, ALU.mult))
                o.sync()
                for j in range(TJ):
                    last = v.tensor_scalar(dst[:, j, :], src[:, j, :], mv_[:, j, 0:1], nt_[:, 1, j:j + 1],
                                           ALU.subtract, ALU.mult)
                return last

            def neg_max(dst, src, done):
                v.tensor_reduce(dst[:], src, AX.X, ALU.max, negate=True).then_inc(done, 1)

            dve.wait_ge(consts_made, 1)
            dve.wait_ge(setup_out, 13)
            with dve.Fori(0, B) as b:
                for s in range(ST):
                    dve.wait_ge(x_in[s], 16 * b + 16)
                    layer_norm(xa[s], xn[s], stat[s], mv[s], nt[s]).then_inc(ln1[s], 1)
                for s in range(ST):
                    dve.wait_ge(score_mm[s], b + 1)
                    neg_max(nmax[s], by_tile(bank_c(s), M), score_max[s])
                for s in range(ST):
                    dve.wait_ge(probs[s], b + 1)
                    o.did(v.reciprocal(rinv[s][:], esum[s][:]))
                    dve.wait_ge(attn_mm[s], b + 1)
                    o.sync()
                    out4 = bank_wide(s).rearrange("p a (c n) -> p (a c) n", c=2)
                    for j in range(TJ):
                        last = v.scalar_tensor_tensor(xa[s][:, j, :], out4[:, j, :], rinv[s][:, j:j + 1],
                                                      xa[s][:, j, :], ALU.mult, ALU.add)
                    last.then_inc(x1_made[s], 1)
                    dve.wait_ge(x1_made[s], b + 1)
                    layer_norm(xa[s], xn[s], stat[s], mv[s], nt[s]).then_inc(ln2[s], 1)
                    dve.wait_ge(rows_free[s], b + 1)
                    dve.wait_ge(ln2[s], b + 1)
                    o.did(v.tensor_copy(rows[s][:, :, 0:D], xn[s][:]))
                    o.sync()
                    o.did(v.tensor_tensor(rows[s][:, :, D:2 * D], xn[s][:], rows[s][:, :, 0:D], ALU.subtract))
                for s in range(ST):
                    dve.wait_ge(logit_mm[s], b + 1)
                    neg_max(nmax[s], bank_c(s)[:, 0:TJ * E].rearrange("p (j m) -> p j m", j=TJ), logit_max[s])
                for s in range(ST):
                    dve.wait_ge(gates[s], b + 1)
                    o.did(v.reciprocal(rinv[s][:], esum[s][:]))
                    o.sync()
                    o.did(v.tensor_tensor(pe_[s][:], pe_[s][:], rinv[s][:].unsqueeze(2).to_broadcast([P, TJ, E]),
                                          ALU.mult))
                    o.sync()
                    for j in range(TJ):
                        last = v.max(top[s][:, j, :], pe_[s][:, j, :])
                    o.did(last)
                    o.sync()
                    for j in range(TJ):
                        last = v.max_index(topi[s][:, j, :], top[s][:, j, :], pe_[s][:, j, :])
                    o.did(last)
                    o.sync()
                    at = bass.ds((b * ST + s) * TJ * TOP, TJ * TOP)
                    v.tensor_copy(weight[:, at].rearrange("p (j k) -> p j k", k=TOP), top[s][:, :, 0:TOP])
                    o.did(v.tensor_copy(ex2[s][:].rearrange("p (j k) -> p j k", k=TOP), topi[s][:, :, 0:TOP]))
                    o.sync()
                    v.tensor_copy(expert[:, at], ex2[s][:])
                    o.did(v.tensor_tensor(hot[s][:], iota8[:].unsqueeze(1).to_broadcast([P, TJ * TOP, E]),
                                          ex2[s][:].unsqueeze(2).to_broadcast([P, TJ * TOP, E]), ALU.is_equal))
                    o.sync()
                    pairs = hot[s][:].rearrange("p (j k) e -> p j k e", k=TOP)
                    o.did(v.tensor_tensor(picks[s][:], pairs[:, :, 0, :], pairs[:, :, 1, :], ALU.add))
                    for j in range(TJ):
                        o.sync()
                        o.did(v.tensor_tensor(prior[:, j + 1, :], prior[:, j, :], picks[s][:, j, :], ALU.add))
                    o.sync()
                    o.did(v.tensor_copy(pri[s][:], prior[:, 0:TJ, :]))
                    o.sync()
                    v.tensor_copy(prior[:, 0, :], prior[:, TJ, :]).then_inc(picked[s], 1)
                    dve.wait_ge(picked[s], b + 1)
                for s in range(ST):
                    dve.wait_ge(rank_mm[s], b + 1)
                    ranks = bank_c(s)[:, 64:64 + TJ * E].rearrange("p (j e) -> p j e", j=TJ)
                    o.did(v.tensor_tensor(prod[s][:].rearrange("p (j k) e -> p j k e", k=TOP),
                                          hot[s][:].rearrange("p (j k) e -> p j k e", k=TOP),
                                          ranks.unsqueeze(2).to_broadcast([P, TJ, TOP, E]), ALU.mult))
                    o.sync()
                    o.did(v.tensor_reduce(rk2[s][:], prod[s][:], AX.X, ALU.add))
                    o.sync()
                    at = bass.ds((b * ST + s) * TJ * TOP, TJ * TOP)
                    o.did(v.tensor_copy(rank[:, at], rk2[s][:]))
                    v.scalar_tensor_tensor(x_slot[s][:], ex2[s][:], float(REGION), rk2[s][:], ALU.mult, ALU.add)\
                     .then_inc(placed[s], 1)
                o.clear()

            def step(instruction):
                o.did(instruction)
                o.sync()

            dve.wait_ge(consts_made, 2)
            dve.wait_ge(count_mm, 1)
            step(v.tensor_copy(cnt[:], ps[:, 0, 0:E]))
            step(v.tensor_scalar(nb[:], cnt[:], 1.0 / BLK, 0.5 - 0.5 / BLK, ALU.mult, ALU.add))
            step(v.tensor_scalar(nb[:], nb[:], MAGIC, None, ALU.add))
            step(v.tensor_scalar(nb[:], nb[:], MAGIC, None, ALU.subtract))
            step(v.memset(cum[:], 0.0))
            for e in range(E):
                step(v.tensor_tensor(cum[:, e + 1:e + 2], cum[:, e:e + 1], nb[:, e:e + 1], ALU.add))
            step(v.tensor_scalar(bexp[:, 0:1], cum[0:1, E:E + 1], 1.0, None, ALU.subtract))
            step(v.tensor_scalar(bnum[:], bnum[:], bexp[:, 0:1], None, ALU.min))
            NB1 = NBLK + 1
            step(v.tensor_tensor(bcmp[:], cum[0:1, 1:E + 1].unsqueeze(1).to_broadcast([1, NB1, E]),
                                 bnum[:].unsqueeze(2).to_broadcast([1, NB1, E]), ALU.is_le))
            v.tensor_reduce(bexp[:], bcmp[:], AX.X, ALU.add)
            step(v.tensor_tensor(bcnt[:], bcmp[:], nb[0:1, :].unsqueeze(1).to_broadcast([1, NB1, E]), ALU.mult))
            step(v.tensor_reduce(bcum[:], bcnt[:], AX.X, ALU.add))
            v.tensor_copy(block_expert[:], bexp[:])
            step(v.tensor_tensor(bnum[:], bnum[:], bcum[:], ALU.subtract))
            step(v.tensor_scalar(bnum[:], bnum[:], float(BLK), None, ALU.mult))
            v.tensor_tensor(pad_row[:], prow[:], cnt[0:1, :], ALU.add)
            v.scalar_tensor_tensor(block_row[:], bexp[:], float(REGION), bnum[:], ALU.mult, ALU.add)\
             .then_inc(tables, 1)
            NP_ = TILES * TOP
            step(v.tensor_tensor(yhot[:], iota8[:].unsqueeze(1).to_broadcast([P, NP_, E]),
                                 expert[:].unsqueeze(2).to_broadcast([P, NP_, E]), ALU.is_equal))
            step(v.tensor_tensor(yhot[:], yhot[:], cum[:, 0:E].unsqueeze(1).to_broadcast([P, NP_, E]), ALU.mult))
            step(v.tensor_reduce(ybase[:], yhot[:], AX.X, ALU.add))
            v.scalar_tensor_tensor(y_slot[:], ybase[:], float(BLK), rank[:], ALU.mult, ALU.add).then_inc(y_placed, 1)
            dve.wait_ge(y_placed, 1)

            def transposed_block(n):
                dve.wait_ge(bxT_mm, n + 1)
                v.tensor_copy(bxT[:], ps[:, 6, :].bitcast(F16).rearrange("p (c n) -> p c n", c=2 * KD))\
                 .then_inc(bxT_made, 1)

            transposed_block(0)
            o.clear()
            with dve.Fori(0, NBLK) as n:
                e = dve.value_load(block_expert[0:1, bass.ds(n, 1)], min_val=0, max_val=E - 1)
                for c in range(0, KH, 2):
                    dve.wait_ge(hid_made, KH * n + c + 2)
                    o.did(v.tensor_copy(hidh[:, c:c + 2, :], hid[:, c:c + 2, :]))
                    o.sync()
                    v.tensor_tensor(hidl[:, c:c + 2, :], hid[:, c:c + 2, :], hidh[:, c:c + 2, :], ALU.subtract)\
                     .then_inc(hid_split, 1)
                transposed_block(n + 1)
                dve.wait_ge(by_out, 16 * n + 16)
                for h in range(2):
                    dve.wait_ge(by_mm, 2 * n + h + 1)
                    v.tensor_tensor(by[:, h, :], ps[:, 4 + h, 0:D],
                                    b2_sb[:, bass.ds(e, 1), :].rearrange("p a n -> p (a n)"), ALU.add)\
                     .then_inc(by_made, 1)
                o.clear()

            for n in range(3):
                dve.wait_ge(tern_total, n + 1)
                c = slice(n, n + 1)
                step(v.tensor_scalar(wmean[:, c], ps[:, 7, 0:1], 1.0 / (D * H), Q_EPS, ALU.mult, ALU.max))
                step(v.reciprocal(tscale[:, c], wmean[:, c]))
                w = tern[n % 2][:]
                step(v.tensor_scalar(w, w, tscale[:, c], MAGIC, ALU.mult, ALU.add))
                step(v.tensor_scalar(w, w, MAGIC - 1.0, MAGIC + 1.0, ALU.max, ALU.min))
                v.tensor_scalar(ternq[n % 2][:], w, MAGIC, None, ALU.subtract).then_inc(tern_quant, 1)
                dve.wait_ge(tern_T, n + 1)
                for k in range(KD):
                    src = ps[:, 5 + k, :].bitcast(BF16)
                    if n < 2:
                        last = v.tensor_copy((wgT, wuT)[n][:, k, :], src)
                    else:
                        last = v.tensor_copy(wdT[:, :, k * P:(k + 1) * P], src.rearrange("p (c n) -> p c n", c=KH))
                last.then_inc(tern_out, 1)
            o.clear()

            with dve.Fori(0, B) as b:
                for s in range(ST):
                    dve.wait_ge(x1_in[s], 16 * b + 16)
                    dve.wait_ge(y_in[s], 16 * TJ * TOP * b + 16 * TJ * TOP)
                    for k in range(TOP):
                        for j in range(TJ):
                            m = (b * ST + s) * TJ * TOP + j * TOP + k
                            last = v.scalar_tensor_tensor(
                                xc[s][:, j, :], gy[:, bass.ds(m, 1), :].rearrange("p a n -> p (a n)"),
                                weight[:, bass.ds(m, 1)], xc[s][:, j, :], ALU.mult, ALU.add)
                        o.did(last)
                        o.sync()
                    layer_norm(xc[s], xn3[s], stat3[s], mv3[s], nt3[s]).then_inc(ln3[s], 1)
                for s in range(ST):
                    dve.wait_ge(score3_mm[s], b + 1)
                    neg_max(nmax3[s], by_tile(bank_c(s), M), score3_max[s])
                for s in range(ST):
                    dve.wait_ge(probs3[s], b + 1)
                    o.did(v.reciprocal(rinv3[s][:], esum3[s][:]))
                    dve.wait_ge(attn3_mm[s], b + 1)
                    o.sync()
                    out4 = bank_wide(s).rearrange("p a (c n) -> p (a c) n", c=2)
                    for j in range(TJ):
                        last = v.scalar_tensor_tensor(xc[s][:, j, :], out4[:, j, :], rinv3[s][:, j:j + 1],
                                                      xc[s][:, j, :], ALU.mult, ALU.add)
                    o.did(last)
                    o.sync()
                    o.did(layer_norm(xc[s], xn3[s], stat3[s], mv3[s], nt3[s]))
                    o.sync()
                    step(v.tensor_reduce(xmax[s][:], xn3[s][:], AX.X, ALU.max, apply_absolute_value=True))
                    step(v.tensor_scalar(xmax[s][:], xmax[s][:], Q_EPS, None, ALU.max))
                    step(v.reciprocal(xscale[s][:], xmax[s][:]))
                    step(v.tensor_scalar(xscale[s][:], xscale[s][:], 127.0, None, ALU.mult))
                    for j in range(TJ):
                        last = v.tensor_scalar(xn3[s][:, j, :], xn3[s][:, j, :], xscale[s][:, j:j + 1], MAGIC,
                                               ALU.mult, ALU.add)
                    step(last)
                    v.tensor_scalar(xq[s][:], xn3[s][:], MAGIC, None, ALU.subtract).then_inc(xq_made[s], 1)
                    step(v.tensor_scalar(hfac[s][:, 0, :], xmax[s][:], 1.0 / 127.0, wmean[:, 0:1],
                                         ALU.mult, ALU.mult))
                    o.did(v.tensor_scalar(hfac[s][:, 1, :], xmax[s][:], 1.0 / 127.0, wmean[:, 1:2],
                                          ALU.mult, ALU.mult))
                    step(v.tensor_tensor(hfac[s][:, 0, :], hfac[s][:, 0, :], hfac[s][:, 0, :], ALU.mult))
                    step(v.tensor_tensor(hfac[s][:, 0, :], hfac[s][:, 0, :], hfac[s][:, 1, :], ALU.mult))
                for j in range(TJ + 1):
                    if j < TJ:
                        t = TJ * b + j
                        for half in range(2):
                            cols = slice(half * 512, half * 512 + 512)
                            for s in range(ST):
                                dve.wait_ge(relu2_made[s], 2 * t + half + 1)
                                v.tensor_tensor(hh[s][:, cols], relu[s][:, cols], ps[:, 4 * s + 1, :], ALU.mult)\
                                 .then_inc(h_made[s], 1)
                        for s in range(ST):
                            top_, lim, inv, fac, back = (hm[s][:, n, j:j + 1] for n in range(5))
                            dve.wait_ge(h_made[s], 2 * t + 2)
                            step(v.tensor_reduce(top_, hh[s][:], AX.X, ALU.max, apply_absolute_value=True))
                            step(v.tensor_scalar(lim, top_, hfac[s][:, 0, j:j + 1], Q_EPS, ALU.mult, ALU.max))
                            step(v.reciprocal(inv, lim))
                            v.tensor_scalar(fac, inv, 127.0, hfac[s][:, 0, j:j + 1], ALU.mult, ALU.mult)\
                             .then_inc(h_scale[s], 1)
                            o.did(v.tensor_scalar(back, lim, 1.0 / 127.0, wmean[:, 2:3], ALU.mult, ALU.mult))
                    if j >= 1:
                        if j == 1:
                            for s in range(ST):
                                dve.wait_ge(out_done[s], 16 * b + 16)
                        for s in range(ST):
                            dve.wait_ge(down_mm[s], TJ * b + j)
                            o.sync()
                            v.scalar_tensor_tensor(xo[s][:, j - 1, :], bank_d(s)[:, 0:D], hm[s][:, 4, j - 1:j],
                                                   xc[s][:, j - 1, :], ALU.mult, ALU.add).then_inc(xo_made[s], 1)
                    if j < TJ:
                        for s in range(ST):
                            dve.wait_ge(h_round[s], TJ * b + j + 1)
                            v.tensor_scalar(hq[s][:], hr[s][:], MAGIC, None, ALU.subtract).then_inc(hq_made[s], 1)
                o.clear()

        @block.tensor
        def _(pe):
            BM = B * M
            for s in range(ST):
                pe.sem_inc(placed[s], 1)
            pe.sem_inc(by_made, 1)

            def mm(out_, lhsT, rhs, first, last):
                return nc.tensor.matmul(out_, lhsT, rhs, start=first, stop=last)

            def tr(out_, in_, identity):
                return nc.tensor.matmul(out_, in_, identity, start=True, stop=True, is_transpose=True)

            pe.wait_ge(consts_made, 1)
            pe.wait_ge(ctx_in_sem, 16)
            for k in range(KD):
                for b in range(B):
                    last = tr(ps[:, k, b * M:(b + 1) * M], ctx_sb[:, b, k * P:(k + 1) * P], ident[0:M, 0:M])
            last.then_inc(setup_mm, 1)
            pe.wait_ge(weights_in, SMALL)
            tr(ps[:, 6, 0:NROW], bcols_in[:], ident[0:NROW, 0:NROW]).then_inc(setup_mm, 1)
            for n, w in enumerate((w0_sb, wk_sb, wv_sb, wo_sb)):
                for k in range(KD):
                    for c in range(KD):
                        last = tr(ps[:, 2 + n, k * D + c * P:k * D + (c + 1) * P], w[:, c, k * P:(k + 1) * P], ident[:])
                last.then_inc(setup_mm, 1)

            def product(bank, w, rhs):
                for m in range(KD):
                    for k in range(KD):
                        last = mm(ps[:, bank + m, 0:BM], w[:, k, m * P:(m + 1) * P], rhs[:, k, :], k == 0, k == KD - 1)
                return last

            pe.wait_ge(setup_out, 6)
            product(0, wkT, ctxT).then_inc(setup_mm, 1)
            product(2, w0T, ctxT).then_inc(setup_mm, 1)
            product(4, wvT, ctxT).then_inc(setup_mm, 1)
            pe.wait_ge(setup_out, 8)
            for k in range(KD):
                mm(ps[0:1, 6, 0:BM], bcols[:, k:k + 1], eoT[:, k, :], k == 0, k == KD - 1)
            product(0, w0_sb, eoT).then_inc(setup_mm, 1)
            for k in range(KD):
                mm(ps[0:1, 7, 0:BM], bcols[:, KD + k:KD + k + 1], kpT[:, k, :], k == 0, k == KD - 1)
            product(2, wq_sb, kpT).then_inc(setup_mm, 1)
            pe.wait_ge(setup_out, 9)
            for b in range(B):
                dst = ps[0:M, 4 + b // 2, b % 2 * D:b % 2 * D + D]
                for k in range(KD):
                    mm(dst, vpT[:, k, b * M:(b + 1) * M], woT[:, k, :], k == 0, False)
                last = mm(dst, ones[0:1, 0:M], bo_row[:], False, True)
                if b % 2:
                    last.then_inc(setup_mm, 1)
            pe.wait_ge(setup_out, 13)

            def transposed_tiles(s, src, identity, dst):
                for j in range(TJ):
                    for k in range(KD):
                        last = tr(dst[:, k, j * P:(j + 1) * P], src[:, j, k * P:(k + 1) * P], identity)
                return last

            def scores(s, b, xT_, g_, c_):
                at = bass.ds(b * M, M)
                for j in range(TJ):
                    dst = bank_c(s)[:, j * P:j * P + M]
                    for k in range(KD):
                        mm(dst, xT_[:, k, j * P:(j + 1) * P], g_[:, k, at], k == 0, False)
                    last = mm(dst, ones[0:1, :], c_[:, at], False, True)
                return last

            def transposed_probs(s, pr_):
                for j in range(TJ):
                    last = tr(bank_d(s)[0:M, j * P:(j + 1) * P], pr_[:, j, :], ident[:])
                return last

            def attend(s, b, prT_, values):
                rhs = values[:, bass.ds(b, 1), :].rearrange("m o d -> m (o d)")
                for j in range(TJ):
                    last = mm(bank_wide(s)[:, j // 2, j % 2 * D:j % 2 * D + D], prT_[:, j * P:(j + 1) * P], rhs, True, True)
                return last

            with pe.Fori(0, B) as b:
                for s in range(ST):
                    pe.wait_ge(ln1[s], b + 1)
                    transposed_tiles(s, xn[s], ident[:], bank_wide(s)).then_inc(xT1_mm[s], 1)
                for s in range(ST):
                    pe.wait_ge(xT1[s], b + 1)
                    pe.wait_ge(placed[s], b + 1)
                    scores(s, b, xT[s], g0, c0).then_inc(score_mm[s], 1)
                for s in range(ST):
                    pe.wait_ge(probs[s], b + 1)
                    transposed_probs(s, pr[s]).then_inc(probsT_mm[s], 1)
                for s in range(ST):
                    pe.wait_ge(probsT[s], b + 1)
                    attend(s, b, prT[s], ctx_sb).then_inc(attn_mm[s], 1)
                for s in range(ST):
                    pe.wait_ge(ln2[s], b + 1)
                    transposed_tiles(s, xn[s], ident[:], bank_wide(s)).then_inc(xT2_mm[s], 1)
                for s in range(ST):
                    pe.wait_ge(xT2[s], b + 1)
                    for j in range(TJ):
                        for k in range(KD):
                            last = mm(bank_c(s)[:, j * E:(j + 1) * E], xT[s][:, k, j * P:(j + 1) * P], wr_sb[:, k, :],
                                      k == 0, k == KD - 1)
                    last.then_inc(logit_mm[s], 1)
                for s in range(ST):
                    pe.wait_ge(picked[s], b + 1)
                    dst = bank_c(s)[:, 64:64 + TJ * E]
                    mm(dst, before[:], picks[s][:].rearrange("p j e -> p (j e)"), True, False)
                    mm(dst, onesb[:], pri[s][:].rearrange("p j e -> p (j e)"), False, True).then_inc(rank_mm[s], 1)

            for s in range(ST):
                pe.wait_ge(placed[s], B + 1)
            mm(ps[:, 0, 0:E], onesb[:], prior[:, 0, :], True, True).then_inc(count_mm, 1)
            pe.wait_ge(tables, 1)
            for n in range(2):
                pe.wait_ge(low_done[n], 4 * B + 1)

            def transpose_block(n):
                pe.wait_ge(bx_in, 16 * n + 16)
                bank = ps[:, 6, :].bitcast(F16).rearrange("p (c n) -> p c n", c=2 * KD)
                for h in range(2):
                    for c in range(2 * KD):
                        last = tr(bank[:, c, h * P:(h + 1) * P], bx[:, h, c * P:(c + 1) * P], ident16[:])
                last.then_inc(bxT_mm, 1)

            transpose_block(0)
            with pe.Fori(0, NBLK) as n:
                e = pe.value_load(block_expert[0:1, bass.ds(n, 1)], min_val=0, max_val=E - 1)
                pe.wait_ge(bxT_made, n + 1)
                for c in range(KH):
                    if c >= 4:
                        pe.wait_ge(hid_made, KH * n + c - 3)
                    dst = ps[:, c % 4, 0:BLK]
                    cols = slice(c * P, (c + 1) * P)
                    for k in range(KD):
                        hi = w1h[:, bass.ds(e * KD + k, 1), cols].rearrange("p a n -> p (a n)")
                        lo = w1l[:, bass.ds(e * KD + k, 1), cols].rearrange("p a n -> p (a n)")
                        mm(dst, hi, bxT[:, k, :], k == 0, False)
                        mm(dst, hi, bxT[:, KD + k, :], False, False)
                        last = mm(dst, lo, bxT[:, k, :], False, k == KD - 1)
                    last.then_inc(hid_mm, 1)
                transpose_block(n + 1)
                pe.wait_ge(by_made, 2 * n + 1)
                for h in range(2):
                    dst = ps[:, 4 + h, 0:D]
                    rows_ = slice(h * P, (h + 1) * P)
                    for c in range(KH):
                        if h == 0 and c % 2 == 0:
                            pe.wait_ge(hid_split, KH // 2 * n + c // 2 + 1)
                        hi = w2h[:, bass.ds(e * KH + c, 1), :].rearrange("p a n -> p (a n)")
                        lo = w2l[:, bass.ds(e * KH + c, 1), :].rearrange("p a n -> p (a n)")
                        mm(dst, hidh[:, c, rows_], hi, c == 0, False)
                        mm(dst, hidh[:, c, rows_], lo, False, False)
                        last = mm(dst, hidl[:, c, rows_], hi, False, c == KH - 1)
                    last.then_inc(by_mm, 1)

            for n in range(3):
                pe.wait_ge(tern_sum, n + 1)
                if n:
                    pe.wait_ge(tern_quant, n)
                else:
                    pe.wait_ge(by_made, 2 * NBLK + 1)
                    pe.wait_ge(bxT_made, NBLK + 1)
                mm(ps[:, 7, 0:1], ones[:], tsum[:, n:n + 1], True, True).then_inc(tern_total, 1)
                pe.wait_ge(tern_quant, n + 1)
                if n:
                    pe.wait_ge(tern_out, n)
                for k in range(KD):
                    for c in range(KH):
                        at = c * D + k * P if n < 2 else k * H + c * P
                        last = tr(ps[:, 5 + k, :].bitcast(BF16)[:, c * P:(c + 1) * P], ternq[n % 2][:, at:at + P], identb[:])
                last.then_inc(tern_T, 1)
            pe.wait_ge(tern_out, 3)

            with pe.Fori(0, B) as b:
                for s in range(ST):
                    pe.wait_ge(ln3[s], b + 1)
                    transposed_tiles(s, xn3[s], ident[:], bank_wide(s)).then_inc(xT3_mm[s], 1)
                for s in range(ST):
                    pe.wait_ge(xT3_made[s], b + 1)
                    scores(s, b, xT3[s], g1, c1).then_inc(score3_mm[s], 1)
                for s in range(ST):
                    pe.wait_ge(probs3[s], b + 1)
                    transposed_probs(s, pr3[s]).then_inc(probsT3_mm[s], 1)
                for s in range(ST):
                    pe.wait_ge(probsT3[s], b + 1)
                    attend(s, b, prT3[s], vo).then_inc(attn3_mm[s], 1)
                for s in range(ST):
                    pe.wait_ge(xq_made[s], b + 1)
                    transposed_tiles(s, xq[s], identb[:], bank_c(s).bitcast(BF16).rearrange("p (k n) -> p k n", k=KD))\
                        .then_inc(xqT_mm[s], 1)
                for j in range(TJ + 1):
                    if j < TJ:
                        t = TJ * b + j
                        for half in range(2):
                            cols = slice(half * 512, half * 512 + 512)
                            for s in range(ST):
                                if j == 0 and half == 0:
                                    pe.wait_ge(xqT_made[s], b + 1)
                                else:
                                    pe.wait_ge(h_made[s], 2 * t + half)
                                for bank, w in ((4 * s, wgT), (4 * s + 1, wuT)):
                                    for k in range(KD):
                                        last = mm(ps[:, bank, :], xqT[s][:, k, j * P:(j + 1) * P], w[:, k, cols],
                                                  k == 0, k == KD - 1)
                                last.then_inc(gate_mm[s], 1)
                    if j >= 1:
                        for s in range(ST):
                            pe.wait_ge(hq_made[s], TJ * b + j)
                            for c in range(KH):
                                last = tr(bank_c(s).bitcast(BF16)[:, c * P:(c + 1) * P], hq[s][:, c * P:(c + 1) * P],
                                          identb[:])
                            last.then_inc(hqT_mm[s], 1)
                        for s in range(ST):
                            pe.wait_ge(hqT_made[s], TJ * b + j)
                            for c in range(KH):
                                last = mm(bank_d(s)[:, 0:D], hqT[s][:, c, :], wdT[:, c, :], c == 0, c == KH - 1)
                            last.then_inc(down_mm[s], 1)


_INS = ['x', 'ctx_1024', 'L0_xattn_W', 'L0_xattn_b', 'L0_ffn_w_router', 'L0_ffn_w1', 'L0_ffn_b1', 'L0_ffn_w2',
        'L0_ffn_b2', 'L1_xattn_Wk', 'L1_xattn_Wv', 'L1_xattn_bv', 'L1_xattn_Wq', 'L1_xattn_bq', 'L1_xattn_Wo',
        'L1_xattn_bo', 'L1_ffn_w_gate', 'L1_ffn_w_up', 'L1_ffn_w_down']


def kernel(**inputs):
    import numpy as np
    import concourse.bacc as bacc
    from concourse.bass_utils import run_bass_kernel_spmd

    nc = bacc.Bacc("TRN2", target_bir_lowering=False, num_devices=1)
    arrays, args = {}, []
    for name in _INS:
        a = np.ascontiguousarray(inputs[name])
        arrays[f"in_{name}"] = a
        args.append(nc.dram_tensor(f"in_{name}", a.shape, mybir.dt.from_np(a.dtype), kind="ExternalInput").ap())
    out = nc.dram_tensor("out", (B, S, D), F32, kind="ExternalOutput").ap()
    build(nc, *args, out)
    return run_bass_kernel_spmd(nc, [arrays], core_ids=[0]).results[0]["out"]
```

```python
from contextlib import ExitStack

import concourse.bass as bass
from concourse import mybir

ALU = mybir.AluOpType
ACT = mybir.ActivationFunctionType
AX = mybir.AxisListType
F32 = mybir.dt.float32
F16 = mybir.dt.float16
BF16 = mybir.dt.bfloat16
I32 = mybir.dt.int32
U32 = mybir.dt.uint32

P = 128
B, S, D = 4, 1024, 256
M = 77
E, TOP, H = 8, 2, 1024
KD, KH = D // P, H // P
TOK = B * S
ST, TJ = 2, 4
TILES = TOK // P
BLK = 256
NBLK = TOK * TOP // BLK + E - 1
REGION = TOK + BLK
NROW = 3 * KD + E * KH
LN_EPS = 1e-5
Q_EPS = 1e-5
MAGIC = 1.5 * 2.0 ** 23


class Order:

    def __init__(self, eng, sem):
        self.eng, self.sem, self.n = eng, sem, 0

    def did(self, instruction):
        self.n += 1
        instruction.then_inc(self.sem, 1)

    def sync(self):
        if self.n:
            self.eng.wait_ge(self.sem, self.n)

    def clear(self):
        self.sync()
        self.eng.sem_clear(self.sem)
        self.n = 0


def build(nc, x, ctx_in, w0, b0, wr, w1, b1, w2, b2, wk, wv, bv, wq, bq, wo, bo, wg, wu, wd, out):
    x_rows = x.rearrange("b s d -> (b s) d")
    out_rows = out.rearrange("b s d -> (b s) d")
    x1_rows = nc.dram_tensor("x1_rows", (TOK, D), F32, kind="Internal").ap()
    sent = nc.dram_tensor("sent", (E * REGION, 2 * D), F16, kind="Internal").ap()
    made = nc.dram_tensor("made", (NBLK * BLK, D), F32, kind="Internal").ap()

    with ExitStack() as keep:
        def sb(name, shape, dt, stack=keep):
            return stack.enter_context(nc.sbuf_tensor(name, shape, dt))

        def sem(name):
            return keep.enter_context(nc.semaphore(name))

        def pair(name):
            return [sem(f"{name}{s}") for s in range(ST)]

        def pair_sb(name, shape, dt, stack):
            return [sb(f"{name}{s}", shape, dt, stack) for s in range(ST)]

        ps = keep.enter_context(nc.psum_tensor("ps", [P, 8, 512], F32))

        ident = sb("ident", [P, P], F32)
        ident16 = sb("ident16", [P, P], F16)
        identb = sb("identb", [P, P], BF16)
        ones = sb("ones", [P, P], F32)
        onesb = sb("onesb", [P, P], BF16)
        before = sb("before", [P, P], BF16)
        iota8 = sb("iota8", [P, E], F32)
        magic = sb("magic", [P, 1], F32)
        wr_sb = sb("wr_sb", [P, KD, E], F32)
        ctx_sb = sb("ctx_sb", [M, B, D], F32)
        g0 = sb("g0", [P, KD, B * M], F32)
        c0 = sb("c0", [1, B * M], F32)
        g1 = sb("g1", [P, KD, B * M], F32)
        c1 = sb("c1", [1, B * M], F32)
        vo = sb("vo", [M, B, D], F32)
        bcols = sb("bcols", [P, NROW], F32)
        b2_sb = sb("b2_sb", [P, E, D], F32)
        expert = sb("expert", [P, TILES * TOP], F32)
        weight = sb("weight", [P, TILES * TOP], F32)
        rank = sb("rank", [P, TILES * TOP], F32)
        y_slot = sb("y_slot", [P, TILES * TOP], U32)
        prior = sb("prior", [P, TJ + 1, E], BF16)
        block_expert = sb("block_expert", [1, NBLK + 1], I32)
        block_row = sb("block_row", [1, NBLK + 1], I32)
        pad_row = sb("pad_row", [1, E], I32)

        s12 = ExitStack()
        w1h = sb("w1h", [P, E * KD, H], F16, s12)
        w1l = sb("w1l", [P, E * KD, H], F16, s12)
        w2h = sb("w2h", [P, E * KH, D], F16, s12)
        w2l = sb("w2l", [P, E * KH, D], F16, s12)

        s0 = ExitStack()
        w0_sb = sb("w0_sb", [P, KD, D], F32, s0)
        wq_sb = sb("wq_sb", [P, KD, D], F32, s0)
        wk_sb = sb("wk_sb", [P, KD, D], F32, s0)
        wv_sb = sb("wv_sb", [P, KD, D], F32, s0)
        wo_sb = sb("wo_sb", [P, KD, D], F32, s0)
        bcols_in = sb("bcols_in", [NROW, P], F32, s0)
        bo_row = sb("bo_row", [1, D], F32, s0)
        w0T = sb("w0T", [P, KD, D], F32, s0)
        wkT = sb("wkT", [P, KD, D], F32, s0)
        wvT = sb("wvT", [P, KD, D], F32, s0)
        woT = sb("woT", [P, KD, D], F32, s0)
        ctxT = sb("ctxT", [P, KD, B * M], F32, s0)
        eoT = sb("eoT", [P, KD, B * M], F32, s0)
        kpT = sb("kpT", [P, KD, B * M], F32, s0)
        vpT = sb("vpT", [P, KD, B * M], F32, s0)
        s0.close()

        s1 = ExitStack()
        xa = pair_sb("xa", [P, TJ, D], F32, s1)
        xn = pair_sb("xn", [P, TJ, D], F32, s1)
        xT = pair_sb("xT", [P, KD, TJ * P], F32, s1)
        pr = pair_sb("pr", [P, TJ, M], F32, s1)
        prT = pair_sb("prT", [M, TJ * P], F32, s1)
        rows = pair_sb("rows", [P, TJ, 2 * D], F16, s1)
        stage = pair_sb("stage", [P, 1024], F32, s1)
        stat = pair_sb("stat", [P, TJ, 6], F32, s1)
        mv = pair_sb("mv", [P, TJ, 2], F32, s1)
        nt = pair_sb("nt", [P, 4, TJ], F32, s1)
        nmax = pair_sb("nmax", [P, TJ], F32, s1)
        esum = pair_sb("esum", [P, TJ], F32, s1)
        rinv = pair_sb("rinv", [P, TJ], F32, s1)
        pe_ = pair_sb("pe_", [P, TJ, E], F32, s1)
        top = pair_sb("top", [P, TJ, E], F32, s1)
        topi = pair_sb("topi", [P, TJ, E], U32, s1)
        ex2 = pair_sb("ex2", [P, TJ * TOP], F32, s1)
        hot = pair_sb("hot", [P, TJ * TOP, E], F32, s1)
        picks = pair_sb("picks", [P, TJ, E], BF16, s1)
        pri = pair_sb("pri", [P, TJ, E], BF16, s1)
        prod = pair_sb("prod", [P, TJ * TOP, E], F32, s1)
        rk2 = pair_sb("rk2", [P, TJ * TOP], F32, s1)
        x_slot = pair_sb("x_slot", [P, TJ * TOP], U32, s1)
        zrow = sb("zrow", [P, 2, 2 * D], F16, s1)
        s1.close()

        st = ExitStack()
        cnt = sb("cnt", [P, E], F32, st)
        nb = sb("nb", [P, E], F32, st)
        cum = sb("cum", [P, E + 1], F32, st)
        yhot = sb("yhot", [P, TILES * TOP, E], F32, st)
        ybase = sb("ybase", [P, TILES * TOP], F32, st)
        bnum = sb("bnum", [1, NBLK + 1], F32, st)
        bcmp = sb("bcmp", [1, NBLK + 1, E], F32, st)
        bcnt = sb("bcnt", [1, NBLK + 1, E], F32, st)
        bexp = sb("bexp", [1, NBLK + 1], F32, st)
        bcum = sb("bcum", [1, NBLK + 1], F32, st)
        prow = sb("prow", [1, E], F32, st)
        st.close()

        s2 = ExitStack()
        bx = sb("bx", [P, 2, 2 * D], F16, s2)
        bxT = sb("bxT", [P, 2 * KD, BLK], F16, s2)
        hid = sb("hid", [P, KH, BLK], F32, s2)
        hidh = sb("hidh", [P, KH, BLK], F16, s2)
        hidl = sb("hidl", [P, KH, BLK], F16, s2)
        by = sb("by", [P, 2, D], F32, s2)
        s2.close()
        s12.close()

        s3 = ExitStack()
        gy = sb("gy", [P, TJ * TOP, D], F32, s3)
        y_idx = sb("y_idx", [P, TJ * TOP], U32, s3)
        y_wt = sb("y_wt", [P, TJ * TOP], F32, s3)
        xe = pair_sb("xe", [P, TJ, D], F32, s3)
        tern = [sb(f"tern{n}", [P, H // P * D], F32, s3) for n in range(2)]
        ternq = [sb(f"ternq{n}", [P, H // P * D], BF16, s3) for n in range(2)]
        wgT = sb("wgT", [P, KD, H], BF16, s3)
        wuT = sb("wuT", [P, KD, H], BF16, s3)
        wdT = sb("wdT", [P, KH, D], BF16, s3)
        tsum = sb("tsum", [P, 3], F32, s3)
        tscale = sb("tscale", [P, 3], F32, s3)
        wmean = sb("wmean", [P, 3], F32, s3)
        xc = pair_sb("xc", [P, TJ, D], F32, s3)
        xn3 = pair_sb("xn3", [P, TJ, D], F32, s3)
        xT3 = pair_sb("xT3", [P, KD, TJ * P], F32, s3)
        pr3 = pair_sb("pr3", [P, TJ, M], F32, s3)
        prT3 = pair_sb("prT3", [M, TJ * P], F32, s3)
        stat3 = pair_sb("stat3", [P, TJ, 6], F32, s3)
        mv3 = pair_sb("mv3", [P, TJ, 2], F32, s3)
        nt3 = pair_sb("nt3", [P, 5, TJ], F32, s3)
        nmax3 = pair_sb("nmax3", [P, TJ], F32, s3)
        esum3 = pair_sb("esum3", [P, TJ], F32, s3)
        rinv3 = pair_sb("rinv3", [P, TJ], F32, s3)
        xmax = pair_sb("xmax", [P, TJ], F32, s3)
        xscale = pair_sb("xscale", [P, TJ], F32, s3)
        hfac = pair_sb("hfac", [P, 2, TJ], F32, s3)
        xq = pair_sb("xq", [P, TJ, D], BF16, s3)
        xqT = pair_sb("xqT", [P, KD, TJ * P], BF16, s3)
        relu = [sb(f"relu{n}", [P, H], F32, s3) for n in range(2)]
        hh = pair_sb("hh", [P, H], F32, s3)
        hr = pair_sb("hr", [P, H], F32, s3)
        hq = pair_sb("hq", [P, H], BF16, s3)
        hqT = pair_sb("hqT", [P, KH, P], BF16, s3)
        hm = pair_sb("hm", [P, 5, TJ], F32, s3)
        xo = pair_sb("xo", [P, TJ, D], F32, s3)
        s3.close()

        consts_made, pool_order, vec_order = sem("consts_made"), sem("pool_order"), sem("vec_order")
        ctx_in_sem, weights_in = sem("ctx_loaded"), sem("weights_loaded")
        setup_mm, setup_out, act_order = sem("setup_mm"), sem("setup_out"), sem("act_order")
        stage_full, high_done, low_done = pair("stage_full"), pair("high_done"), pair("low_done")
        x_in, ln1, xT1_mm, xT1, score_mm, score_max, probs = (
            pair(n) for n in ("x_in", "ln1", "xT1_mm", "xT1", "score_mm", "score_max", "probs"))
        probsT_mm, probsT, attn_mm, x1_made, x1_out, ln2 = (
            pair(n) for n in ("probsT_mm", "probsT", "attn_mm", "x1_made", "x1_out", "ln2"))
        xT2_mm, xT2, logit_mm, logit_max, gates, picked, rank_mm, placed, rows_sent = (
            pair(n) for n in ("xT2_mm", "xT2", "logit_mm", "logit_max", "gates", "picked", "rank_mm",
                              "placed", "rows_sent"))
        rows_free = pair("rows_free")
        zeros_made, count_mm, tables, pads_sent = sem("zeros_made"), sem("count_mm"), sem("tables"), sem("pads_sent")
        y_placed = sem("y_placed")
        bx_in, bxT_mm, bxT_made = sem("bx_in"), sem("bxT_mm"), sem("bxT_made")
        hid_mm, hid_made, hid_split = sem("hid_mm"), sem("hid_made"), sem("hid_split")
        by_mm, by_made, by_out = sem("by_mm"), sem("by_made"), sem("by_out")
        tern_in = [sem(f"tern_in{n}") for n in range(2)]
        tern_sum, tern_total, tern_quant, tern_T, tern_out = (
            sem(n) for n in ("tern_sum", "tern_total", "tern_quant", "tern_T", "tern_out"))
        y_in, pool_order3 = sem("y_in"), sem("pool_order3")
        x1_in, x2_made, ln3_guess, ln3_rstd, ln3, xT3_mm, xT3_made, score3_mm, score3_max, probs3 = (
            pair(n) for n in ("x1_in", "x2_made", "ln3_guess", "ln3_rstd", "ln3", "xT3_mm", "xT3_made",
                              "score3_mm", "score3_max", "probs3"))
        probsT3_mm, probsT3, attn3_mm, x3_made, ln4_guess, ln4_rstd, ln4, xq_made, xqT_mm, xqT_made = (
            pair(n) for n in ("probsT3_mm", "probsT3", "attn3_mm", "x3_made", "ln4_guess", "ln4_rstd", "ln4",
                              "xq_made", "xqT_mm", "xqT_made"))
        gate_mm, up_mm, relu_made, relu2_made, h_made, h_scale, h_round, hq_made, hqT_mm, hqT_made, down_mm = (
            sem(n) for n in ("gate_mm", "up_mm", "relu_made", "relu2_made", "h_made", "h_scale", "h_round", "hq_made",
                             "hqT_mm", "hqT_made", "down_mm"))
        xo_made, out_done = sem("xo_made"), pair("out_done")
        SMALL = 16 * 12
        SENT = 16 * TJ * TOP * B

        def bank_wide(s):
            return ps[:, 4 * s:4 * s + 2, :]

        def bank_c(s):
            return ps[:, 4 * s + 2, :]

        def bank_d(s):
            return ps[:, 4 * s + 3, :]

        def by_tile(ap, width):
            return ap.rearrange("p (j m) -> p j m", j=TJ)[:, :, 0:width]

        gate_ps = ps[:, 0:2, :].rearrange("p a n -> p (a n)")
        up_ps = ps[:, 2:4, :].rearrange("p a n -> p (a n)")
        turned_ps = ps[:, 4, :].bitcast(BF16)
        down_ps = ps[:, 5, 0:D]
        attn_ps = ps[:, 6:8, :]

        def phase3(unit, loop, start=None):
            if start:
                start()

            def nth(u, b=0):
                return (b + u // ST, u % ST) if not isinstance(b, int) or 0 <= b * ST + u < B * ST else None

            def unit_at(u, b=0):
                unit(*nth(u, b), nth(u - 1, b), nth(u + 1, b), nth(u + 2, b), nth(u + 3, b))

            unit_at(0)
            with loop(0, B - 2) as b:
                unit_at(1, b)
                unit_at(2, b)
            for u in range(B * ST - 3, B * ST):
                unit_at(u)

        def tile_no(b, s, j):
            return b * (ST * TJ) + (s * TJ + j)

        def token_rows(rows_ap, b, s):
            return rows_ap[bass.ds(b * S + s * TJ * P, TJ * P), :].rearrange("(j p) d -> p j d", p=P)

        def block_rows(rows_ap, row):
            return rows_ap[bass.ds(row, BLK), :].rearrange("(h p) c -> p h c", p=P)

        def stage_piece(n):
            return n // 4, n % 4 // 2, n % 2

        def weight_at(which, half, e):
            if which == 0:
                return bass.ds(e * KD + half, 1)
            return bass.ds(e * KH + half * (KH // 2), KH // 2)

        def staged(n, which):
            k = 1 if which == 0 else KH // 2
            return stage[n % 2][:].rearrange("p (k c) -> p k c", k=k)

        block = keep.enter_context(nc.Block())

        @block.sync
        def _(sp):
            for s in range(ST):
                sp.sem_inc(x1_out[s], 16)
                sp.sem_inc(low_done[s], 1)
            sp.dma_start(ctx_sb[:], ctx_in.rearrange("b m d -> m b d")).then_inc(ctx_in_sem, 16)
            for dst, src in ((w0_sb, w0), (wk_sb, wk), (wq_sb, wq), (wv_sb, wv), (wo_sb, wo), (wr_sb, wr)):
                sp.dma_start(dst[:], src.rearrange("(k p) d -> p k d", p=P)).then_inc(weights_in, 16)
            for n, src in enumerate((b0, bq, bv)):
                sp.dma_start(bcols_in[n * KD:(n + 1) * KD, :], src.rearrange("(k p) -> k p", p=P)).then_inc(weights_in, 16)
            sp.dma_start(bo_row[:], bo.rearrange("(a n) -> a n", a=1)).then_inc(weights_in, 16)
            sp.dma_start(bcols_in[3 * KD:, :], b1.rearrange("e (c p) -> (e c) p", p=P)).then_inc(weights_in, 16)
            sp.dma_start(b2_sb[:].rearrange("p e n -> p (e n)"),
                         b2.rearrange("(a e) n -> a (e n)", a=1).to_broadcast([P, E * D])).then_inc(weights_in, 16)
            sp.wait_ge(setup_out, 13)

            w1_p = w1.rearrange("e (k p) n -> (e k) p n", p=P)
            w2_p = w2.rearrange("e (h k p) n -> (e h) p k n", p=P, h=2)
            with sp.Fori(0, B) as b:
                for s in range(ST):
                    sp.wait_ge(x1_out[s], 16 * b + 16)
                    sp.dma_start(xa[s][:], token_rows(x_rows, b, s)).then_inc(x_in[s], 16)
                for n in range(8):
                    e_off, which, half = stage_piece(n)
                    sp.wait_ge(low_done[n % 2], b * 4 + n // 2 + 1)
                    if which == 0:
                        src = w1_p[bass.ds(b * 4 + e_off * 2 + half, 1)].rearrange("o p n -> p o n")
                    else:
                        src = w2_p[bass.ds(b * 4 + e_off * 2 + half, 1)].rearrange("o p k n -> (o p) k n")
                    sp.dma_start(staged(n, which), src).then_inc(stage_full[n % 2], 16)
                for s in range(ST):
                    sp.wait_ge(x1_made[s], b + 1)
                    sp.dma_start(token_rows(x1_rows, b, s), xa[s][:]).then_inc(x1_out[s], 16)

            sp.wait_ge(zeros_made, 1)
            sp.wait_ge(tables, 1)
            for e in range(E):
                row = sp.value_load(pad_row[0:1, e:e + 1], min_val=0, max_val=E * REGION - BLK)
                sp.dma_start(block_rows(sent, row), zrow[:]).then_inc(pads_sent, 16)
            for s in range(ST):
                sp.wait_ge(rows_sent[s], SENT)
            sp.wait_ge(pads_sent, 16 * E)
            sp.wait_ge(y_placed, 1)

            def load_block(n):
                row = sp.value_load(block_row[0:1, bass.ds(n, 1)], min_val=0, max_val=E * REGION - BLK)
                sp.dma_start(bx[:], block_rows(sent, row)).then_inc(bx_in, 16)

            load_block(0)
            with sp.Fori(0, NBLK) as n:
                sp.wait_ge(bxT_mm, n + 1)
                load_block(n + 1)
                sp.wait_ge(by_made, 2 * n + 3)
                sp.dma_start(block_rows(made, n * BLK), by[:]).then_inc(by_out, 16)

            for s in range(ST):
                sp.wait_ge(x1_out[s], 16 * B + 16)
            sp.wait_ge(by_out, 16 * NBLK + 16)
            tern_src = [w.rearrange("(c p) n -> p c n", p=P) for w in (wg, wu, wd)]

            def load_ternary(n):
                c = H // P if n < 2 else KD
                sp.dma_start(tern[n % 2][:].rearrange("p (c n) -> p c n", c=c), tern_src[n])\
                  .then_inc(tern_in[n % 2], 16)

            load_ternary(0)
            load_ternary(1)
            for s in range(ST):
                sp.dma_start(xe[s][:], token_rows(x1_rows, 0, s)).then_inc(x1_in[s], 16)
            sp.wait_ge(tern_quant, 1)
            load_ternary(2)

            def outputs(b, s):
                sp.wait_ge(xo_made, tile_no(b, s, TJ - 1) + 1)
                sp.dma_start(token_rows(out_rows, b, s), xo[s][:]).then_inc(out_done[s], 16)

            def x1_of(b, s):
                sp.dma_start(xe[s][:], token_rows(x1_rows, b, s)).then_inc(x1_in[s], 16)

            def sp_start():
                sp.wait_ge(x3_made[0], 1)
                x1_of(1, 0)

            def sp_unit(b, s, before_, second, first, prep):
                if prep:
                    sp.wait_ge(x3_made[prep[1]], prep[0])
                    x1_of(*prep)
                if before_:
                    outputs(*before_)

            phase3(sp_unit, sp.Fori, sp_start)
            outputs(B - 1, ST - 1)
            for s in range(ST):
                sp.wait_ge(out_done[s], 16 * B + 16)

        @block.gpsimd
        def _(pool):
            g = nc.gpsimd
            o = Order(pool, pool_order)
            g.memset(ident[:], 0.0)
            g.memset(before[:], 1.0)
            g.memset(ones[:], 1.0)
            g.memset(onesb[:], 1.0)
            g.memset(magic[:], MAGIC)
            g.memset(prior[:], 0.0)
            o.did(g.iota(iota8[:], [[1, E]], base=0, channel_multiplier=0, allow_small_or_imprecise_dtypes=True))
            o.sync()
            g.affine_select(out=ident[:], in_=ident[:], compare_op=ALU.not_equal, fill=1.0,
                            base=0, pattern=[[-1, P]], channel_multiplier=1)
            o.did(g.affine_select(out=before[:], in_=before[:], compare_op=ALU.is_gt, fill=0.0,
                                  base=0, pattern=[[1, P]], channel_multiplier=-1))
            o.sync()
            g.tensor_copy(ident16[:], ident[:])
            g.tensor_copy(identb[:], ident[:]).then_inc(consts_made, 1)
            pool.wait_ge(setup_out, 13)
            g.memset(zrow[:], 0.0).then_inc(zeros_made, 1)

            turn = [pool.alloc_register(f"turn{s}") for s in range(ST)]
            for s in range(ST):
                pool.reg_mov(turn[s], 2)
            with pool.Fori(0, B) as b:
                for n in range(8):
                    e_off, which, half = stage_piece(n)
                    at = weight_at(which, half, b * 2 + e_off)
                    hi, lo = ((w1h, w1l), (w2h, w2l))[which]
                    pool.wait_ge(high_done[n % 2], b * 4 + n // 2 + 1)
                    g.tensor_tensor(lo[:, at, :], staged(n, which), hi[:, at, :], ALU.subtract)\
                     .then_inc(low_done[n % 2], 1)
                for s in range(ST):
                    pool.wait_ge(placed[s], turn[s])
                    pool.reg_add(turn[s], turn[s], 1)
                    for n in range(TJ * TOP):
                        g.indirect_dma_start(sent, bass.IndirectOffsetOnAxis(x_slot[s][:, n:n + 1], 0),
                                             rows[s][:, n // TOP, :], None).then_inc(rows_sent[s], 16)
                for s in range(ST):
                    pool.wait_ge(rows_sent[s], 16 * TJ * TOP * b + 16 * TJ * TOP)
                    pool.sem_inc(rows_free[s], 1)
            for s in range(ST):
                pool.wait_ge(rows_sent[s], SENT)
                pool.wait_ge(x1_out[s], 16 * B + 16)
            g.iota(bnum[:], [[1, NBLK + 1]], base=0, channel_multiplier=0, allow_small_or_imprecise_dtypes=True)
            g.iota(prow[:], [[REGION, E]], base=0, channel_multiplier=0, allow_small_or_imprecise_dtypes=True)\
             .then_inc(consts_made, 1)

            pool.wait_ge(by_out, 16 * NBLK + 16)
            o = Order(pool, pool_order3)
            counts = {}

            def awaited(signal, step, key, b, nth):
                pool.wait_ge(signal, step * nth if isinstance(b, int) else counts[key])
                pool.reg_add(counts[key], counts[key], step)

            for key, step in [("y_in", 16 * TJ * TOP), ("round", 1)] + \
                    [(f"{n}{s}", 16 if n == "x1" else 1) for n in ("x1", "g3", "g4") for s in range(ST)]:
                counts[key] = pool.alloc_register(f"next_{key}")
                pool.reg_mov(counts[key], step)

            def step(instruction):
                o.did(instruction)
                o.sync()

            def newton(b, s, guess, key, done):
                awaited(guess, 1, f"{key}{s}", b, b + 1)
                y, minus_half, t, off = (nt3[s][:, n, :] for n in (1, 2, 3, 4))
                for _ in range(3):
                    step(g.tensor_tensor(t, y, y, ALU.mult))
                    step(g.tensor_tensor(t, t, minus_half, ALU.mult))
                    step(g.tensor_scalar(t, t, 1.5, None, ALU.add))
                    step(g.tensor_tensor(y, y, t, ALU.mult))
                step(g.tensor_tensor(t, y, mv3[s][:, :, 0], ALU.mult))
                g.tensor_scalar(off, t, -1.0, None, ALU.mult).then_inc(done, 1)

            def places(b, s):
                at = bass.ds(b * (ST * TJ * TOP) + s * TJ * TOP, TJ * TOP)
                g.tensor_copy(y_wt[:], weight[:, at])
                step(g.tensor_copy(y_idx[:], y_slot[:, at]))

            def gather(ns):
                for n in ns:
                    g.indirect_dma_start(gy[:, n, :], None, made,
                                         bass.IndirectOffsetOnAxis(y_idx[:, n:n + 1], 0)).then_inc(y_in, 16)

            def weighted(b, s):
                awaited(y_in, 16 * TJ * TOP, "y_in", b, b * ST + s + 1)
                weights = y_wt[:].rearrange("p (n o) -> p n o", o=1).broadcast_to([P, TJ * TOP, D])
                step(g.tensor_tensor(gy[:], gy[:], weights, ALU.mult))

            def summed(b, s):
                both = gy[:].rearrange("p (j k) n -> p j k n", k=TOP)
                step(g.tensor_tensor(both[:, :, 0, :], both[:, :, 0, :], both[:, :, 1, :], ALU.add))
                awaited(x1_in[s], 16, f"x1{s}", b, b + 1)
                g.tensor_tensor(xe[s][:], xe[s][:], both[:, :, 0, :], ALU.add).then_inc(x2_made[s], 1)

            def prepared(b, s):
                places(b, s)
                gather(range(TJ * TOP))
                weighted(b, s)
                summed(b, s)
                pool.wait_ge(x2_made[s], b + 1)

            def pool_unit(b, s, before_, second, first, prep):
                if prep:
                    places(*prep)
                    gather(range(0, TJ * TOP // 2))
                if first:
                    newton(*first, ln3_guess[s], "g3", ln3_rstd[s])
                if prep:
                    gather(range(TJ * TOP // 2, TJ * TOP))
                if second:
                    newton(*second, ln4_guess[1 - s], "g4", ln4_rstd[1 - s])
                if prep:
                    weighted(*prep)
                    summed(*prep)
                if first or second:
                    o.clear()

            def pool_start():
                prepared(0, 0)
                newton(0, 0, ln3_guess[0], "g3", ln3_rstd[0])
                o.clear()
                prepared(0, 1)
                newton(0, 0, ln4_guess[0], "g4", ln4_rstd[0])
                newton(0, 1, ln3_guess[1], "g3", ln3_rstd[1])
                o.clear()
                prepared(1, 0)
                o.clear()

            phase3(pool_unit, pool.Fori, pool_start)

        @block.scalar
        def _(act):
            a = nc.scalar
            BM = B * M

            def out_of(n, dst, src):
                act.wait_ge(setup_mm, n)
                a.activation(dst, src, ACT.Copy).then_inc(setup_out, 1)

            def two_pieces(bank):
                return ps[:, bank, :].rearrange("p (k n) -> p k n", k=KD)

            act.wait_ge(weights_in, SMALL)
            out_of(1, ctxT[:], ps[:, 0:2, 0:BM])
            out_of(2, bcols[:], ps[:, 6, 0:NROW])
            out_of(3, w0T[:], two_pieces(2))
            out_of(4, wkT[:], two_pieces(3))
            out_of(5, wvT[:], two_pieces(4))
            out_of(6, woT[:], two_pieces(5))
            out_of(7, kpT[:], ps[:, 0:2, 0:BM])
            act.wait_ge(setup_out, 2)
            act.wait_ge(setup_mm, 8)
            for k in range(KD):
                last = a.activation(eoT[:, k, :], ps[:, 2 + k, 0:BM], ACT.Identity, bias=bcols[:, k:k + 1])
            last.then_inc(setup_out, 1)
            act.wait_ge(setup_mm, 9)
            for k in range(KD):
                last = a.activation(vpT[:, k, :], ps[:, 4 + k, 0:BM], ACT.Identity, bias=bcols[:, 2 * KD + k:2 * KD + k + 1])
            last.then_inc(setup_out, 1)
            scale = float(D) ** -0.5
            act.wait_ge(setup_mm, 10)
            a.activation(g0[:], ps[:, 0:2, 0:BM], ACT.Copy)
            a.activation(c0[:], ps[0:1, 6, 0:BM], ACT.Copy).then_inc(setup_out, 1)
            act.wait_ge(setup_mm, 11)
            a.activation(g1[:], ps[:, 2:4, 0:BM], ACT.Copy, scale=scale)
            a.activation(c1[:], ps[0:1, 7, 0:BM], ACT.Copy, scale=scale).then_inc(setup_out, 1)
            for h in range(2):
                out_of(12 + h, vo[:, 2 * h:2 * h + 2, :], ps[0:M, 4 + h, :].rearrange("p (b n) -> p b n", b=2))

            def high_half(b, n):
                e_off, which, half = stage_piece(n)
                at = weight_at(which, half, b * 2 + e_off)
                act.wait_ge(stage_full[n % 2], 16 * (b * 4 + n // 2) + 16)
                a.activation((w1h, w2h)[which][:, at, :], staged(n, which), ACT.Copy).then_inc(high_done[n % 2], 1)

            def exponentials(probs_out, scores, neg_max, sums, done):
                for j in range(TJ):
                    last = a.activation(probs_out[:, j, :], scores[:, j, :], ACT.Exp,
                                        bias=neg_max[:, j:j + 1], accum_out=sums[:, j:j + 1])
                last.then_inc(done, 1)

            with act.Fori(0, B) as b:
                for s in range(ST):
                    act.wait_ge(xT1_mm[s], b + 1)
                    a.activation(xT[s][:], bank_wide(s), ACT.Copy).then_inc(xT1[s], 1)
                for n in range(0, 2):
                    high_half(b, n)
                for s in range(ST):
                    act.wait_ge(score_max[s], b + 1)
                    exponentials(pr[s], by_tile(bank_c(s), M), nmax[s], esum[s], probs[s])
                for s in range(ST):
                    act.wait_ge(probsT_mm[s], b + 1)
                    a.activation(prT[s][:], bank_d(s)[0:M, :], ACT.Copy).then_inc(probsT[s], 1)
                for n in range(2, 5):
                    high_half(b, n)
                for s in range(ST):
                    act.wait_ge(xT2_mm[s], b + 1)
                    a.activation(xT[s][:], bank_wide(s), ACT.Copy).then_inc(xT2[s], 1)
                for s in range(ST):
                    act.wait_ge(logit_max[s], b + 1)
                    logits = bank_c(s)[:, 0:TJ * E].rearrange("p (j m) -> p j m", j=TJ)
                    exponentials(pe_[s], logits, nmax[s], esum[s], gates[s])
                for n in range(5, 8):
                    high_half(b, n)

            act.wait_ge(y_placed, 1)
            act.wait_ge(tables, 1)
            for s in range(ST):
                act.wait_ge(rows_sent[s], SENT)
            with act.Fori(0, NBLK) as n:
                e = act.value_load(block_expert[0:1, bass.ds(n, 1)], min_val=0, max_val=E - 1)
                for c in range(KH):
                    act.wait_ge(hid_mm, KH * n + c + 1)
                    bias = bcols[:, bass.ds(e * KH + (3 * KD + c), 1)]
                    act.wait_ge(tables, 1)
                    a.activation(hid[:, c, :], ps[:, c % 4, 0:BLK], ACT.Gelu_apprx_tanh, bias=bias)\
                     .then_inc(hid_made, 1)

            for n in range(3):
                act.wait_ge(tern_in[n % 2], 16 * (n // 2 + 1))
                if n == 2:
                    act.wait_ge(tern_T, 1)
                a.activation(ternq[n % 2][:], tern[n % 2][:], ACT.Abs, accum_out=tsum[:, n:n + 1])\
                 .then_inc(tern_sum, 1)

            def normalised(b, s, rstd, done):
                act.wait_ge(rstd[s], b + 1)
                src = xe if rstd is ln3_rstd else xc
                for j in range(TJ):
                    last = a.activation(xn3[s][:, j, :], src[s][:, j, :], ACT.Identity,
                                        bias=nt3[s][:, 4, j:j + 1], scale=nt3[s][:, 1, j:j + 1])
                last.then_inc(done[s], 1)

            def xT3_out(b, s):
                act.wait_ge(xT3_mm[s], b + 1)
                a.activation(xT3[s][:], attn_ps, ACT.Copy).then_inc(xT3_made[s], 1)

            def exps3(b, s):
                act.wait_ge(score3_max[s], b + 1)
                exponentials(pr3[s], by_tile(attn_ps[:, 0, :], M), nmax3[s], esum3[s], probs3[s])

            def probsT3_out(b, s):
                act.wait_ge(probsT3_mm[s], b + 1)
                a.activation(prT3[s][:], attn_ps[0:M, 1, :], ACT.Copy).then_inc(probsT3[s], 1)

            def xqT_out(b, s):
                act.wait_ge(xqT_mm[s], b + 1)
                a.activation(xqT[s][:], turned_ps.rearrange("p (k n) -> p k n", k=KD), ACT.Copy)\
                 .then_inc(xqT_made[s], 1)

            def hqT_out(t, j):
                act.wait_ge(hqT_mm, t + 1)
                a.activation(hqT[j % 2][:], turned_ps.rearrange("p (c n) -> p c n", c=KH), ACT.Copy)\
                 .then_inc(hqT_made, 1)

            def relu_squared(t, j):
                act.wait_ge(gate_mm, t + 1)
                a.activation(relu[j % 2][:], gate_ps, ACT.Relu).then_inc(relu_made, 1)
                act.wait_ge(relu_made, t + 1)
                a.activation(relu[j % 2][:], relu[j % 2][:], ACT.Square).then_inc(relu2_made, 1)

            def act_unit(b, s, before_, second, first, prep):
                for j in range(TJ):
                    t = tile_no(b, s, j)
                    if j == 0:
                        relu_squared(t, j)
                    if j < TJ - 1:
                        relu_squared(t + 1, j + 1)
                    if j or before_:
                        hqT_out(t - 1, j - 1)
                    if j == 0 and second:
                        probsT3_out(*second)
                    if j == 1 and first:
                        normalised(*first, ln3_rstd, ln3)
                    if j == 2:
                        if first:
                            xT3_out(*first)
                        if second:
                            normalised(*second, ln4_rstd, ln4)
                    if j == 3:
                        if second:
                            xqT_out(*second)
                        if first:
                            exps3(*first)
                    act.wait_ge(h_scale, t + 1)
                    a.activation(hr[j % 2][:], hh[j % 2][:], ACT.Identity, bias=magic[:, 0:1],
                                 scale=hm[s][:, 3, j:j + 1]).then_inc(h_round, 1)

            def act_start():
                normalised(0, 0, ln3_rstd, ln3)
                xT3_out(0, 0)
                exps3(0, 0)
                probsT3_out(0, 0)
                normalised(0, 0, ln4_rstd, ln4)
                normalised(0, 1, ln3_rstd, ln3)
                xqT_out(0, 0)
                xT3_out(0, 1)
                exps3(0, 1)

            phase3(act_unit, act.Fori, act_start)
            hqT_out(tile_no(B - 1, ST - 1, TJ - 1), TJ - 1)

        @block.vector
        def _(dve):
            for s in range(ST):
                dve.sem_inc(rows_free[s], 1)
                dve.sem_inc(out_done[s], 16)
            dve.sem_inc(by_out, 16)
            v = nc.vector
            o = Order(dve, vec_order)

            def layer_norm(src, dst, stat_, mv_, nt_):
                for j in range(TJ):
                    last = v.bn_stats(stat_[:, j, :], src[:, j, :])
                o.did(last)
                o.sync()
                for j in range(TJ):
                    last = v.bn_aggr(mv_[:, j, :], stat_[:, j, :])
                o.did(last)
                o.sync()
                ve, y, minus_half, t = (nt_[:, n, :] for n in range(4))
                o.did(v.tensor_scalar(ve, mv_[:, :, 1], LN_EPS, None, ALU.add))
                o.sync()
                v.tensor_scalar(minus_half, ve, -0.5, None, ALU.mult)
                o.did(v.tensor_scalar(t.bitcast(I32), ve.bitcast(I32), 1, None, ALU.logical_shift_right))
                o.sync()
                o.did(v.tensor_scalar(y.bitcast(I32), t.bitcast(I32), -1.0, float(0x5F3759DF), ALU.mult, ALU.add))
                for _ in range(3):
                    o.sync()
                    o.did(v.tensor_tensor(t, y, y, ALU.mult))
                    o.sync()
                    o.did(v.tensor_tensor(t, t, minus_half, ALU.mult))
                    o.sync()
                    o.did(v.scalar_tensor_tensor(y, t, 1.5, y, ALU.add, ALU.mult))
                o.sync()
                for j in range(TJ):
                    last = v.tensor_scalar(dst[:, j, :], src[:, j, :], mv_[:, j, 0:1], nt_[:, 1, j:j + 1],
                                           ALU.subtract, ALU.mult)
                return last

            def neg_max(dst, src, done):
                v.tensor_reduce(dst[:], src, AX.X, ALU.max, negate=True).then_inc(done, 1)

            dve.wait_ge(consts_made, 1)
            dve.wait_ge(setup_out, 13)
            with dve.Fori(0, B) as b:
                for s in range(ST):
                    dve.wait_ge(x_in[s], 16 * b + 16)
                    layer_norm(xa[s], xn[s], stat[s], mv[s], nt[s]).then_inc(ln1[s], 1)
                for s in range(ST):
                    dve.wait_ge(score_mm[s], b + 1)
                    neg_max(nmax[s], by_tile(bank_c(s), M), score_max[s])
                for s in range(ST):
                    dve.wait_ge(probs[s], b + 1)
                    o.did(v.reciprocal(rinv[s][:], esum[s][:]))
                    dve.wait_ge(attn_mm[s], b + 1)
                    o.sync()
                    out4 = bank_wide(s).rearrange("p a (c n) -> p (a c) n", c=2)
                    for j in range(TJ):
                        last = v.scalar_tensor_tensor(xa[s][:, j, :], out4[:, j, :], rinv[s][:, j:j + 1],
                                                      xa[s][:, j, :], ALU.mult, ALU.add)
                    last.then_inc(x1_made[s], 1)
                    dve.wait_ge(x1_made[s], b + 1)
                    layer_norm(xa[s], xn[s], stat[s], mv[s], nt[s]).then_inc(ln2[s], 1)
                    dve.wait_ge(rows_free[s], b + 1)
                    dve.wait_ge(ln2[s], b + 1)
                    o.did(v.tensor_copy(rows[s][:, :, 0:D], xn[s][:]))
                    o.sync()
                    o.did(v.tensor_tensor(rows[s][:, :, D:2 * D], xn[s][:], rows[s][:, :, 0:D], ALU.subtract))
                for s in range(ST):
                    dve.wait_ge(logit_mm[s], b + 1)
                    neg_max(nmax[s], bank_c(s)[:, 0:TJ * E].rearrange("p (j m) -> p j m", j=TJ), logit_max[s])
                for s in range(ST):
                    dve.wait_ge(gates[s], b + 1)
                    o.did(v.reciprocal(rinv[s][:], esum[s][:]))
                    o.sync()
                    o.did(v.tensor_tensor(pe_[s][:], pe_[s][:], rinv[s][:].unsqueeze(2).to_broadcast([P, TJ, E]),
                                          ALU.mult))
                    o.sync()
                    for j in range(TJ):
                        last = v.max(top[s][:, j, :], pe_[s][:, j, :])
                    o.did(last)
                    o.sync()
                    for j in range(TJ):
                        last = v.max_index(topi[s][:, j, :], top[s][:, j, :], pe_[s][:, j, :])
                    o.did(last)
                    o.sync()
                    at = bass.ds((b * ST + s) * TJ * TOP, TJ * TOP)
                    v.tensor_copy(weight[:, at].rearrange("p (j k) -> p j k", k=TOP), top[s][:, :, 0:TOP])
                    o.did(v.tensor_copy(ex2[s][:].rearrange("p (j k) -> p j k", k=TOP), topi[s][:, :, 0:TOP]))
                    o.sync()
                    v.tensor_copy(expert[:, at], ex2[s][:])
                    o.did(v.tensor_tensor(hot[s][:], iota8[:].unsqueeze(1).to_broadcast([P, TJ * TOP, E]),
                                          ex2[s][:].unsqueeze(2).to_broadcast([P, TJ * TOP, E]), ALU.is_equal))
                    o.sync()
                    pairs = hot[s][:].rearrange("p (j k) e -> p j k e", k=TOP)
                    o.did(v.tensor_tensor(picks[s][:], pairs[:, :, 0, :], pairs[:, :, 1, :], ALU.add))
                    for j in range(TJ):
                        o.sync()
                        o.did(v.tensor_tensor(prior[:, j + 1, :], prior[:, j, :], picks[s][:, j, :], ALU.add))
                    o.sync()
                    o.did(v.tensor_copy(pri[s][:], prior[:, 0:TJ, :]))
                    o.sync()
                    v.tensor_copy(prior[:, 0, :], prior[:, TJ, :]).then_inc(picked[s], 1)
                    dve.wait_ge(picked[s], b + 1)
                for s in range(ST):
                    dve.wait_ge(rank_mm[s], b + 1)
                    ranks = bank_c(s)[:, 64:64 + TJ * E].rearrange("p (j e) -> p j e", j=TJ)
                    o.did(v.tensor_tensor(prod[s][:].rearrange("p (j k) e -> p j k e", k=TOP),
                                          hot[s][:].rearrange("p (j k) e -> p j k e", k=TOP),
                                          ranks.unsqueeze(2).to_broadcast([P, TJ, TOP, E]), ALU.mult))
                    o.sync()
                    o.did(v.tensor_reduce(rk2[s][:], prod[s][:], AX.X, ALU.add))
                    o.sync()
                    at = bass.ds((b * ST + s) * TJ * TOP, TJ * TOP)
                    o.did(v.tensor_copy(rank[:, at], rk2[s][:]))
                    v.scalar_tensor_tensor(x_slot[s][:], ex2[s][:], float(REGION), rk2[s][:], ALU.mult, ALU.add)\
                     .then_inc(placed[s], 1)
                o.clear()

            def step(instruction):
                o.did(instruction)
                o.sync()

            dve.wait_ge(consts_made, 2)
            dve.wait_ge(count_mm, 1)
            step(v.tensor_copy(cnt[:], ps[:, 0, 0:E]))
            step(v.tensor_scalar(nb[:], cnt[:], 1.0 / BLK, 0.5 - 0.5 / BLK, ALU.mult, ALU.add))
            step(v.tensor_scalar(nb[:], nb[:], MAGIC, None, ALU.add))
            step(v.tensor_scalar(nb[:], nb[:], MAGIC, None, ALU.subtract))
            step(v.memset(cum[:], 0.0))
            for e in range(E):
                step(v.tensor_tensor(cum[:, e + 1:e + 2], cum[:, e:e + 1], nb[:, e:e + 1], ALU.add))
            step(v.tensor_scalar(bexp[:, 0:1], cum[0:1, E:E + 1], 1.0, None, ALU.subtract))
            step(v.tensor_scalar(bnum[:], bnum[:], bexp[:, 0:1], None, ALU.min))
            NB1 = NBLK + 1
            step(v.tensor_tensor(bcmp[:], cum[0:1, 1:E + 1].unsqueeze(1).to_broadcast([1, NB1, E]),
                                 bnum[:].unsqueeze(2).to_broadcast([1, NB1, E]), ALU.is_le))
            v.tensor_reduce(bexp[:], bcmp[:], AX.X, ALU.add)
            step(v.tensor_tensor(bcnt[:], bcmp[:], nb[0:1, :].unsqueeze(1).to_broadcast([1, NB1, E]), ALU.mult))
            step(v.tensor_reduce(bcum[:], bcnt[:], AX.X, ALU.add))
            v.tensor_copy(block_expert[:], bexp[:])
            step(v.tensor_tensor(bnum[:], bnum[:], bcum[:], ALU.subtract))
            step(v.tensor_scalar(bnum[:], bnum[:], float(BLK), None, ALU.mult))
            v.tensor_tensor(pad_row[:], prow[:], cnt[0:1, :], ALU.add)
            v.scalar_tensor_tensor(block_row[:], bexp[:], float(REGION), bnum[:], ALU.mult, ALU.add)\
             .then_inc(tables, 1)
            NP_ = TILES * TOP
            step(v.tensor_tensor(yhot[:], iota8[:].unsqueeze(1).to_broadcast([P, NP_, E]),
                                 expert[:].unsqueeze(2).to_broadcast([P, NP_, E]), ALU.is_equal))
            step(v.tensor_tensor(yhot[:], yhot[:], cum[:, 0:E].unsqueeze(1).to_broadcast([P, NP_, E]), ALU.mult))
            step(v.tensor_reduce(ybase[:], yhot[:], AX.X, ALU.add))
            v.scalar_tensor_tensor(y_slot[:], ybase[:], float(BLK), rank[:], ALU.mult, ALU.add).then_inc(y_placed, 1)
            dve.wait_ge(y_placed, 1)

            def transposed_block(n):
                dve.wait_ge(bxT_mm, n + 1)
                v.tensor_copy(bxT[:], ps[:, 6, :].bitcast(F16).rearrange("p (c n) -> p c n", c=2 * KD))\
                 .then_inc(bxT_made, 1)

            transposed_block(0)
            o.clear()
            with dve.Fori(0, NBLK) as n:
                e = dve.value_load(block_expert[0:1, bass.ds(n, 1)], min_val=0, max_val=E - 1)
                for c in range(0, KH, 2):
                    dve.wait_ge(hid_made, KH * n + c + 2)
                    o.did(v.tensor_copy(hidh[:, c:c + 2, :], hid[:, c:c + 2, :]))
                    o.sync()
                    v.tensor_tensor(hidl[:, c:c + 2, :], hid[:, c:c + 2, :], hidh[:, c:c + 2, :], ALU.subtract)\
                     .then_inc(hid_split, 1)
                transposed_block(n + 1)
                dve.wait_ge(by_out, 16 * n + 16)
                for h in range(2):
                    dve.wait_ge(by_mm, 2 * n + h + 1)
                    v.tensor_tensor(by[:, h, :], ps[:, 4 + h, 0:D],
                                    b2_sb[:, bass.ds(e, 1), :].rearrange("p a n -> p (a n)"), ALU.add)\
                     .then_inc(by_made, 1)
                o.clear()

            for n in range(3):
                dve.wait_ge(tern_total, n + 1)
                c = slice(n, n + 1)
                step(v.tensor_scalar(wmean[:, c], ps[:, 7, 0:1], 1.0 / (D * H), Q_EPS, ALU.mult, ALU.max))
                step(v.reciprocal(tscale[:, c], wmean[:, c]))
                w = tern[n % 2][:]
                step(v.tensor_scalar(w, w, tscale[:, c], MAGIC, ALU.mult, ALU.add))
                step(v.tensor_scalar(w, w, MAGIC - 1.0, MAGIC + 1.0, ALU.max, ALU.min))
                v.tensor_scalar(ternq[n % 2][:], w, MAGIC, None, ALU.subtract).then_inc(tern_quant, 1)
                dve.wait_ge(tern_T, n + 1)
                for k in range(KD):
                    src = ps[:, 5 + k, :].bitcast(BF16)
                    if n < 2:
                        last = v.tensor_copy((wgT, wuT)[n][:, k, :], src)
                    else:
                        last = v.tensor_copy(wdT[:, :, k * P:(k + 1) * P], src.rearrange("p (c n) -> p c n", c=KH))
                last.then_inc(tern_out, 1)
            o.clear()

            def stats(src, s, done):
                for j in range(TJ):
                    last = v.bn_stats(stat3[s][:, j, :], src[:, j, :])
                step(last)
                for j in range(TJ):
                    last = v.bn_aggr(mv3[s][:, j, :], stat3[s][:, j, :])
                step(last)
                ve, y, minus_half, t = (nt3[s][:, n, :] for n in range(4))
                step(v.tensor_scalar(ve, mv3[s][:, :, 1], LN_EPS, None, ALU.add))
                v.tensor_scalar(minus_half, ve, -0.5, None, ALU.mult)
                step(v.tensor_scalar(t.bitcast(I32), ve.bitcast(I32), 1, None, ALU.logical_shift_right))
                v.tensor_scalar(y.bitcast(I32), t.bitcast(I32), -1.0, float(0x5F3759DF), ALU.mult, ALU.add)\
                 .then_inc(done[s], 1)

            def ln3_stats(b, s):
                dve.wait_ge(x2_made[s], b + 1)
                stats(xe[s], s, ln3_guess)

            def max3(b, s):
                dve.wait_ge(score3_mm[s], b + 1)
                neg_max(nmax3[s], by_tile(attn_ps[:, 0, :], M), score3_max[s])

            def x3(b, s):
                dve.wait_ge(probs3[s], b + 1)
                o.did(v.reciprocal(rinv3[s][:], esum3[s][:]))
                dve.wait_ge(attn3_mm[s], b + 1)
                o.sync()
                out4 = attn_ps.rearrange("p a (c n) -> p (a c) n", c=2)
                for j in range(TJ):
                    last = v.scalar_tensor_tensor(xc[s][:, j, :], out4[:, j, :], rinv3[s][:, j:j + 1],
                                                  xe[s][:, j, :], ALU.mult, ALU.add)
                last.then_inc(x3_made[s], 1)

            def ln4_stats(b, s):
                dve.wait_ge(x3_made[s], b + 1)
                stats(xc[s], s, ln4_guess)

            def row_scales(b, s):
                dve.wait_ge(ln4[s], b + 1)
                step(v.tensor_reduce(xmax[s][:], xn3[s][:], AX.X, ALU.max, apply_absolute_value=True))
                step(v.tensor_scalar(xmax[s][:], xmax[s][:], Q_EPS, None, ALU.max))
                step(v.reciprocal(xscale[s][:], xmax[s][:]))
                step(v.tensor_scalar(xscale[s][:], xscale[s][:], 127.0, None, ALU.mult))
                for j in range(TJ):
                    last = v.tensor_scalar(xn3[s][:, j, :], xn3[s][:, j, :], xscale[s][:, j:j + 1], MAGIC,
                                           ALU.mult, ALU.add)
                o.did(last)

            def row_integers(b, s):
                o.sync()
                v.tensor_scalar(xq[s][:], xn3[s][:], MAGIC, None, ALU.subtract).then_inc(xq_made[s], 1)
                o.did(v.tensor_scalar(hfac[s][:, 0, :], xmax[s][:], 1.0 / 127.0, wmean[:, 0:1], ALU.mult, ALU.mult))
                step(v.tensor_scalar(hfac[s][:, 1, :], xmax[s][:], 1.0 / 127.0, wmean[:, 1:2], ALU.mult, ALU.mult))
                step(v.tensor_tensor(hfac[s][:, 0, :], hfac[s][:, 0, :], hfac[s][:, 0, :], ALU.mult))
                step(v.tensor_tensor(hfac[s][:, 0, :], hfac[s][:, 0, :], hfac[s][:, 1, :], ALU.mult))

            def x4(b, s, j):
                dve.wait_ge(down_mm, tile_no(b, s, j) + 1)
                v.scalar_tensor_tensor(xo[s][:, j, :], down_ps, hm[s][:, 4, j:j + 1], xc[s][:, j, :],
                                       ALU.mult, ALU.add).then_inc(xo_made, 1)

            def dve_unit(b, s, before_, second, first, prep):
                for j in range(TJ):
                    t = tile_no(b, s, j)
                    if j == 3:
                        if second:
                            row_integers(*second)
                        if first:
                            max3(*first)
                    dve.wait_ge(up_mm, t + 1)
                    dve.wait_ge(relu2_made, t + 1)
                    v.tensor_tensor(hh[j % 2][:], relu[j % 2][:], up_ps, ALU.mult).then_inc(h_made, 1)
                    top_, lim, inv, fac, back = (hm[s][:, n, j:j + 1] for n in range(5))
                    dve.wait_ge(h_made, t + 1)
                    step(v.tensor_reduce(top_, hh[j % 2][:], AX.X, ALU.max, apply_absolute_value=True))
                    step(v.tensor_scalar(lim, top_, hfac[s][:, 0, j:j + 1], Q_EPS, ALU.mult, ALU.max))
                    step(v.reciprocal(inv, lim))
                    v.tensor_scalar(fac, inv, 127.0, hfac[s][:, 0, j:j + 1], ALU.mult, ALU.mult).then_inc(h_scale, 1)
                    o.did(v.tensor_scalar(back, lim, 1.0 / 127.0, wmean[:, 2:3], ALU.mult, ALU.mult))
                    if j == 1:
                        dve.wait_ge(out_done[s], 16 * b + 16)
                    if j:
                        x4(b, s, j - 1)
                    elif before_:
                        x4(*before_, TJ - 1)
                    if j == 0 and first:
                        ln3_stats(*first)
                    if j == 1 and second:
                        x3(*second)
                    dve.wait_ge(h_round, t + 1)
                    v.tensor_scalar(hq[j % 2][:], hr[j % 2][:], MAGIC, None, ALU.subtract).then_inc(hq_made, 1)
                    if j == 1 and second:
                        ln4_stats(*second)
                    if j == 2 and second:
                        row_scales(*second)
                o.sync()
                o.clear()

            def dve_start():
                ln3_stats(0, 0)
                max3(0, 0)
                x3(0, 0)
                ln4_stats(0, 0)
                ln3_stats(0, 1)
                row_scales(0, 0)
                row_integers(0, 0)
                max3(0, 1)
                o.clear()

            phase3(dve_unit, dve.Fori, dve_start)
            x4(B - 1, ST - 1, TJ - 1)

        @block.tensor
        def _(pe):
            BM = B * M
            for s in range(ST):
                pe.sem_inc(placed[s], 1)
            pe.sem_inc(by_made, 1)

            def mm(out_, lhsT, rhs, first, last):
                return nc.tensor.matmul(out_, lhsT, rhs, start=first, stop=last)

            def tr(out_, in_, identity):
                return nc.tensor.matmul(out_, in_, identity, start=True, stop=True, is_transpose=True)

            pe.wait_ge(consts_made, 1)
            pe.wait_ge(ctx_in_sem, 16)
            for k in range(KD):
                for b in range(B):
                    last = tr(ps[:, k, b * M:(b + 1) * M], ctx_sb[:, b, k * P:(k + 1) * P], ident[0:M, 0:M])
            last.then_inc(setup_mm, 1)
            pe.wait_ge(weights_in, SMALL)
            tr(ps[:, 6, 0:NROW], bcols_in[:], ident[0:NROW, 0:NROW]).then_inc(setup_mm, 1)
            for n, w in enumerate((w0_sb, wk_sb, wv_sb, wo_sb)):
                for k in range(KD):
                    for c in range(KD):
                        last = tr(ps[:, 2 + n, k * D + c * P:k * D + (c + 1) * P], w[:, c, k * P:(k + 1) * P], ident[:])
                last.then_inc(setup_mm, 1)

            def product(bank, w, rhs):
                for m in range(KD):
                    for k in range(KD):
                        last = mm(ps[:, bank + m, 0:BM], w[:, k, m * P:(m + 1) * P], rhs[:, k, :], k == 0, k == KD - 1)
                return last

            pe.wait_ge(setup_out, 6)
            product(0, wkT, ctxT).then_inc(setup_mm, 1)
            product(2, w0T, ctxT).then_inc(setup_mm, 1)
            product(4, wvT, ctxT).then_inc(setup_mm, 1)
            pe.wait_ge(setup_out, 8)
            for k in range(KD):
                mm(ps[0:1, 6, 0:BM], bcols[:, k:k + 1], eoT[:, k, :], k == 0, k == KD - 1)
            product(0, w0_sb, eoT).then_inc(setup_mm, 1)
            for k in range(KD):
                mm(ps[0:1, 7, 0:BM], bcols[:, KD + k:KD + k + 1], kpT[:, k, :], k == 0, k == KD - 1)
            product(2, wq_sb, kpT).then_inc(setup_mm, 1)
            pe.wait_ge(setup_out, 9)
            for b in range(B):
                dst = ps[0:M, 4 + b // 2, b % 2 * D:b % 2 * D + D]
                for k in range(KD):
                    mm(dst, vpT[:, k, b * M:(b + 1) * M], woT[:, k, :], k == 0, False)
                last = mm(dst, ones[0:1, 0:M], bo_row[:], False, True)
                if b % 2:
                    last.then_inc(setup_mm, 1)
            pe.wait_ge(setup_out, 13)

            def transposed_tiles(s, src, identity, dst):
                for j in range(TJ):
                    for k in range(KD):
                        last = tr(dst[:, k, j * P:(j + 1) * P], src[:, j, k * P:(k + 1) * P], identity)
                return last

            def scores(bank, b, xT_, g_, c_):
                at = bass.ds(b * M, M)
                for j in range(TJ):
                    dst = bank[:, j * P:j * P + M]
                    for k in range(KD):
                        mm(dst, xT_[:, k, j * P:(j + 1) * P], g_[:, k, at], k == 0, False)
                    last = mm(dst, ones[0:1, :], c_[:, at], False, True)
                return last

            def transposed_probs(bank, pr_):
                for j in range(TJ):
                    last = tr(bank[0:M, j * P:(j + 1) * P], pr_[:, j, :], ident[:])
                return last

            def attend(banks, b, prT_, values):
                rhs = values[:, bass.ds(b, 1), :].rearrange("m o d -> m (o d)")
                for j in range(TJ):
                    last = mm(banks[:, j // 2, j % 2 * D:j % 2 * D + D], prT_[:, j * P:(j + 1) * P], rhs, True, True)
                return last

            with pe.Fori(0, B) as b:
                for s in range(ST):
                    pe.wait_ge(ln1[s], b + 1)
                    transposed_tiles(s, xn[s], ident[:], bank_wide(s)).then_inc(xT1_mm[s], 1)
                for s in range(ST):
                    pe.wait_ge(xT1[s], b + 1)
                    pe.wait_ge(placed[s], b + 1)
                    scores(bank_c(s), b, xT[s], g0, c0).then_inc(score_mm[s], 1)
                for s in range(ST):
                    pe.wait_ge(probs[s], b + 1)
                    transposed_probs(bank_d(s), pr[s]).then_inc(probsT_mm[s], 1)
                for s in range(ST):
                    pe.wait_ge(probsT[s], b + 1)
                    attend(bank_wide(s), b, prT[s], ctx_sb).then_inc(attn_mm[s], 1)
                for s in range(ST):
                    pe.wait_ge(ln2[s], b + 1)
                    transposed_tiles(s, xn[s], ident[:], bank_wide(s)).then_inc(xT2_mm[s], 1)
                for s in range(ST):
                    pe.wait_ge(xT2[s], b + 1)
                    for j in range(TJ):
                        for k in range(KD):
                            last = mm(bank_c(s)[:, j * E:(j + 1) * E], xT[s][:, k, j * P:(j + 1) * P], wr_sb[:, k, :],
                                      k == 0, k == KD - 1)
                    last.then_inc(logit_mm[s], 1)
                for s in range(ST):
                    pe.wait_ge(picked[s], b + 1)
                    dst = bank_c(s)[:, 64:64 + TJ * E]
                    mm(dst, before[:], picks[s][:].rearrange("p j e -> p (j e)"), True, False)
                    mm(dst, onesb[:], pri[s][:].rearrange("p j e -> p (j e)"), False, True).then_inc(rank_mm[s], 1)

            for s in range(ST):
                pe.wait_ge(placed[s], B + 1)
            mm(ps[:, 0, 0:E], onesb[:], prior[:, 0, :], True, True).then_inc(count_mm, 1)
            pe.wait_ge(tables, 1)
            for n in range(2):
                pe.wait_ge(low_done[n], 4 * B + 1)

            def transpose_block(n):
                pe.wait_ge(bx_in, 16 * n + 16)
                bank = ps[:, 6, :].bitcast(F16).rearrange("p (c n) -> p c n", c=2 * KD)
                for h in range(2):
                    for c in range(2 * KD):
                        last = tr(bank[:, c, h * P:(h + 1) * P], bx[:, h, c * P:(c + 1) * P], ident16[:])
                last.then_inc(bxT_mm, 1)

            transpose_block(0)
            with pe.Fori(0, NBLK) as n:
                e = pe.value_load(block_expert[0:1, bass.ds(n, 1)], min_val=0, max_val=E - 1)
                pe.wait_ge(bxT_made, n + 1)
                for c in range(KH):
                    if c >= 4:
                        pe.wait_ge(hid_made, KH * n + c - 3)
                    dst = ps[:, c % 4, 0:BLK]
                    cols = slice(c * P, (c + 1) * P)
                    for k in range(KD):
                        hi = w1h[:, bass.ds(e * KD + k, 1), cols].rearrange("p a n -> p (a n)")
                        lo = w1l[:, bass.ds(e * KD + k, 1), cols].rearrange("p a n -> p (a n)")
                        mm(dst, hi, bxT[:, k, :], k == 0, False)
                        mm(dst, hi, bxT[:, KD + k, :], False, False)
                        last = mm(dst, lo, bxT[:, k, :], False, k == KD - 1)
                    last.then_inc(hid_mm, 1)
                transpose_block(n + 1)
                pe.wait_ge(by_made, 2 * n + 1)
                for h in range(2):
                    dst = ps[:, 4 + h, 0:D]
                    rows_ = slice(h * P, (h + 1) * P)
                    for c in range(KH):
                        if h == 0 and c % 2 == 0:
                            pe.wait_ge(hid_split, KH // 2 * n + c // 2 + 1)
                        hi = w2h[:, bass.ds(e * KH + c, 1), :].rearrange("p a n -> p (a n)")
                        lo = w2l[:, bass.ds(e * KH + c, 1), :].rearrange("p a n -> p (a n)")
                        mm(dst, hidh[:, c, rows_], hi, c == 0, False)
                        mm(dst, hidh[:, c, rows_], lo, False, False)
                        last = mm(dst, hidl[:, c, rows_], hi, False, c == KH - 1)
                    last.then_inc(by_mm, 1)

            for n in range(3):
                pe.wait_ge(tern_sum, n + 1)
                if n:
                    pe.wait_ge(tern_quant, n)
                else:
                    pe.wait_ge(by_made, 2 * NBLK + 1)
                    pe.wait_ge(bxT_made, NBLK + 1)
                mm(ps[:, 7, 0:1], ones[:], tsum[:, n:n + 1], True, True).then_inc(tern_total, 1)
                pe.wait_ge(tern_quant, n + 1)
                if n:
                    pe.wait_ge(tern_out, n)
                for k in range(KD):
                    for c in range(KH):
                        at = c * D + k * P if n < 2 else k * H + c * P
                        last = tr(ps[:, 5 + k, :].bitcast(BF16)[:, c * P:(c + 1) * P], ternq[n % 2][:, at:at + P], identb[:])
                last.then_inc(tern_T, 1)
            pe.wait_ge(tern_out, 3)

            def turn3(b, s):
                pe.wait_ge(ln3[s], b + 1)
                transposed_tiles(s, xn3[s], ident[:], attn_ps).then_inc(xT3_mm[s], 1)

            def scores3(b, s):
                pe.wait_ge(xT3_made[s], b + 1)
                scores(attn_ps[:, 0, :], b, xT3[s], g1, c1).then_inc(score3_mm[s], 1)

            def turn_probs3(b, s):
                pe.wait_ge(probs3[s], b + 1)
                transposed_probs(attn_ps[:, 1, :], pr3[s]).then_inc(probsT3_mm[s], 1)

            def attend3(b, s):
                pe.wait_ge(probsT3[s], b + 1)
                attend(attn_ps, b, prT3[s], vo).then_inc(attn3_mm[s], 1)

            def turn_integers(b, s):
                pe.wait_ge(xq_made[s], b + 1)
                transposed_tiles(s, xq[s], identb[:], turned_ps.rearrange("p (k n) -> p k n", k=KD))\
                    .then_inc(xqT_mm[s], 1)

            def turn_hidden(t, j):
                pe.wait_ge(hq_made, t + 1)
                for c in range(KH):
                    last = tr(turned_ps[:, c * P:(c + 1) * P], hq[j % 2][:, c * P:(c + 1) * P], identb[:])
                last.then_inc(hqT_mm, 1)

            def down(t, j):
                pe.wait_ge(hqT_made, t + 1)
                if not isinstance(t, int) or t:
                    pe.wait_ge(xo_made, t)
                for c in range(KH):
                    last = mm(down_ps, hqT[j % 2][:, c, :], wdT[:, c, :], c == 0, c == KH - 1)
                last.then_inc(down_mm, 1)

            def widened(dst, w, s, j):
                for half in range(2):
                    n = slice(half * 512, half * 512 + 512)
                    for k in range(KD):
                        last = mm(dst[:, n], xqT[s][:, k, j * P:(j + 1) * P], w[:, k, n], k == 0, k == KD - 1)
                return last

            def gate(s, t, j, before_=True):
                if before_:
                    pe.wait_ge(relu_made, t)
                widened(gate_ps, wgT, s, j).then_inc(gate_mm, 1)

            def up(s, t, j, before_=True):
                if before_:
                    pe.wait_ge(h_made, t)
                widened(up_ps, wuT, s, j).then_inc(up_mm, 1)

            def pe_unit(b, s, before_, second, first, prep):
                pe.wait_ge(xqT_made[s], b + 1)
                for j in range(TJ):
                    t = tile_no(b, s, j)
                    if j == 0:
                        gate(s, t, j, before_)
                        up(s, t, j, before_)
                        gate(s, t + 1, j + 1)
                    if j or before_:
                        turn_hidden(t - 1, j - 1)
                    if j < TJ - 1:
                        up(s, t + 1, j + 1)
                    if j == 0 and second:
                        turn_probs3(*second)
                    if j or before_:
                        down(t - 1, j - 1)
                    if j < TJ - 2:
                        gate(s, t + 2, j + 2)
                    if j == 0 and second:
                        attend3(*second)
                    if j == 1 and first:
                        if second:
                            pe.wait_ge(x3_made[second[1]], second[0] + 1)
                        turn3(*first)
                    if j == 2 and first:
                        scores3(*first)
                    if j == 3 and second:
                        turn_integers(*second)

            def pe_start():
                turn3(0, 0)
                scores3(0, 0)
                turn_probs3(0, 0)
                attend3(0, 0)
                pe.wait_ge(x3_made[0], 1)
                turn3(0, 1)
                turn_integers(0, 0)
                scores3(0, 1)

            phase3(pe_unit, pe.Fori, pe_start)
            turn_hidden(tile_no(B - 1, ST - 1, TJ - 1), TJ - 1)
            down(tile_no(B - 1, ST - 1, TJ - 1), TJ - 1)


_INS = ['x', 'ctx_1024', 'L0_xattn_W', 'L0_xattn_b', 'L0_ffn_w_router', 'L0_ffn_w1', 'L0_ffn_b1', 'L0_ffn_w2',
        'L0_ffn_b2', 'L1_xattn_Wk', 'L1_xattn_Wv', 'L1_xattn_bv', 'L1_xattn_Wq', 'L1_xattn_bq', 'L1_xattn_Wo',
        'L1_xattn_bo', 'L1_ffn_w_gate', 'L1_ffn_w_up', 'L1_ffn_w_down']


def kernel(**inputs):
    import numpy as np
    import concourse.bacc as bacc
    from concourse.bass_utils import run_bass_kernel_spmd

    nc = bacc.Bacc("TRN2", target_bir_lowering=False, num_devices=1)
    arrays, args = {}, []
    for name in _INS:
        a = np.ascontiguousarray(inputs[name])
        arrays[f"in_{name}"] = a
        args.append(nc.dram_tensor(f"in_{name}", a.shape, mybir.dt.from_np(a.dtype), kind="ExternalInput").ap())
    out = nc.dram_tensor("out", (B, S, D), F32, kind="ExternalOutput").ap()
    build(nc, *args, out)
    return run_bass_kernel_spmd(nc, [arrays], core_ids=[0]).results[0]["out"]
```

```python
from contextlib import ExitStack

import concourse.bass as bass
from concourse import mybir

ALU = mybir.AluOpType
ACT = mybir.ActivationFunctionType
AX = mybir.AxisListType
F32 = mybir.dt.float32
F16 = mybir.dt.float16
BF16 = mybir.dt.bfloat16
I32 = mybir.dt.int32
U32 = mybir.dt.uint32

P = 128
B, S, D = 4, 1024, 256
M = 77
E, TOP, H = 8, 2, 1024
KD, KH = D // P, H // P
TOK = B * S
ST, TJ = 2, 4
TILES = TOK // P
BLK = 256
NBLK = TOK * TOP // BLK + E - 1
REGION = TOK + BLK
NROW = 3 * KD + E * KH
LN_EPS = 1e-5
Q_EPS = 1e-5
STAGES = 4
MAGIC = 1.5 * 2.0 ** 23


class Order:

    def __init__(self, eng, sem):
        self.eng, self.sem, self.n = eng, sem, 0

    def did(self, instruction):
        self.n += 1
        instruction.then_inc(self.sem, 1)

    def sync(self):
        if self.n:
            self.eng.wait_ge(self.sem, self.n)

    def clear(self):
        self.sync()
        self.eng.sem_clear(self.sem)
        self.n = 0


def build(nc, x, ctx_in, w0, b0, wr, w1, b1, w2, b2, wk, wv, bv, wq, bq, wo, bo, wg, wu, wd, out):
    x_rows = x.rearrange("b s d -> (b s) d")
    out_rows = out.rearrange("b s d -> (b s) d")
    x1_rows = nc.dram_tensor("x1_rows", (TOK, D), F32, kind="Internal").ap()
    sent = nc.dram_tensor("sent", (E * REGION, 2 * D), F16, kind="Internal").ap()
    made = nc.dram_tensor("made", (NBLK * BLK, D), F32, kind="Internal").ap()

    with ExitStack() as keep:
        def sb(name, shape, dt, stack=keep):
            return stack.enter_context(nc.sbuf_tensor(name, shape, dt))

        def sem(name):
            return keep.enter_context(nc.semaphore(name))

        def pair(name):
            return [sem(f"{name}{s}") for s in range(ST)]

        def pair_sb(name, shape, dt, stack):
            return [sb(f"{name}{s}", shape, dt, stack) for s in range(ST)]

        ps = keep.enter_context(nc.psum_tensor("ps", [P, 8, 512], F32))

        ident = sb("ident", [P, P], F32)
        ident16 = sb("ident16", [P, P], F16)
        identb = sb("identb", [P, P], BF16)
        ones = sb("ones", [P, P], F32)
        onesb = sb("onesb", [P, P], BF16)
        before = sb("before", [P, P], BF16)
        iota8 = sb("iota8", [P, E], F32)
        magic = sb("magic", [P, 1], F32)
        wr_sb = sb("wr_sb", [P, KD, E], F32)
        ctx_sb = sb("ctx_sb", [M, B, D], F32)
        g0 = sb("g0", [P, KD, B * M], F32)
        c0 = sb("c0", [1, B * M], F32)
        g1 = sb("g1", [P, KD, B * M], F32)
        c1 = sb("c1", [1, B * M], F32)
        vo = sb("vo", [M, B, D], F32)
        bcols = sb("bcols", [P, NROW], F32)
        expert = sb("expert", [P, TILES * TOP], F32)
        weight = sb("weight", [P, TILES * TOP], F32)
        rank = sb("rank", [P, TILES * TOP], F32)
        y_slot = sb("y_slot", [P, TILES * TOP], U32)
        prior = sb("prior", [P, TJ + 1, E], BF16)
        block_expert = sb("block_expert", [1, NBLK + 1], I32)
        block_row = sb("block_row", [1, NBLK + 1], I32)
        pad_row = sb("pad_row", [1, E], I32)
        bnum = sb("bnum", [1, NBLK + 1], F32)
        prow = sb("prow", [1, E], F32)
        tsum = sb("tsum", [P, 3], F32)
        tscale = sb("tscale", [P, 3], F32)
        wmean = sb("wmean", [P, 3], F32)

        s12 = ExitStack()
        w1h = sb("w1h", [P, E * KD, H], F16, s12)
        w1l = sb("w1l", [P, E * KD, H], F16, s12)
        w2h = sb("w2h", [P, E * KH, D], F16, s12)
        w2l = sb("w2l", [P, E * KH, D], F16, s12)

        s0 = ExitStack()
        w0_sb = sb("w0_sb", [P, KD, D], F32, s0)
        wq_sb = sb("wq_sb", [P, KD, D], F32, s0)
        wk_sb = sb("wk_sb", [P, KD, D], F32, s0)
        wv_sb = sb("wv_sb", [P, KD, D], F32, s0)
        wo_sb = sb("wo_sb", [P, KD, D], F32, s0)
        bcols_in = sb("bcols_in", [NROW, P], F32, s0)
        bo_row = sb("bo_row", [1, D], F32, s0)
        w0T = sb("w0T", [P, KD, D], F32, s0)
        wkT = sb("wkT", [P, KD, D], F32, s0)
        wvT = sb("wvT", [P, KD, D], F32, s0)
        woT = sb("woT", [P, KD, D], F32, s0)
        ctxT = sb("ctxT", [P, KD, B * M], F32, s0)
        eoT = sb("eoT", [P, KD, B * M], F32, s0)
        kpT = sb("kpT", [P, KD, B * M], F32, s0)
        vpT = sb("vpT", [P, KD, B * M], F32, s0)
        s0.close()

        s1 = ExitStack()
        xa = pair_sb("xa", [P, TJ, D], F32, s1)
        xn = pair_sb("xn", [P, TJ, D], F32, s1)
        xT = pair_sb("xT", [P, KD, TJ * P], F32, s1)
        pr = pair_sb("pr", [P, TJ, M], F32, s1)
        prT = pair_sb("prT", [M, TJ * P], F32, s1)
        rows = pair_sb("rows", [P, TJ, 2 * D], F16, s1)
        stage = [sb(f"stage{n}", [P, 1024], F32, s1) for n in range(STAGES)]
        stat = pair_sb("stat", [P, TJ, 6], F32, s1)
        mv = pair_sb("mv", [P, TJ, 2], F32, s1)
        nt = pair_sb("nt", [P, 5, TJ], F32, s1)
        nmax = pair_sb("nmax", [P, TJ], F32, s1)
        esum = pair_sb("esum", [P, TJ], F32, s1)
        rinv = pair_sb("rinv", [P, TJ], F32, s1)
        pe_ = pair_sb("pe_", [P, TJ, E], F32, s1)
        top = pair_sb("top", [P, TJ, E], F32, s1)
        topi = pair_sb("topi", [P, TJ, E], U32, s1)
        ex2 = pair_sb("ex2", [P, TJ * TOP], F32, s1)
        hot = pair_sb("hot", [P, TJ * TOP, E], F32, s1)
        picks = pair_sb("picks", [P, TJ, E], BF16, s1)
        pri = pair_sb("pri", [P, TJ, E], BF16, s1)
        prod = pair_sb("prod", [P, TJ * TOP, E], F32, s1)
        rk2 = pair_sb("rk2", [P, TJ * TOP], F32, s1)
        x_slot = pair_sb("x_slot", [P, TJ * TOP], U32, s1)
        zrow = sb("zrow", [P, 2, 2 * D], F16, s1)
        s1.close()

        tern = [sb(f"tern{n}", [P, H // P * D], F32, s12) for n in range(3)]
        ternq = [sb("ternq", [P, H // P * D], BF16, s12)[:]]
        ternq += [tern[0][:].bitcast(BF16)[:, n * H // P * D:(n + 1) * H // P * D] for n in range(2)]

        st = ExitStack()
        sb("still_sent", [P, 12 * 1024], mybir.dt.uint8, st)
        cnt = sb("cnt", [P, E], F32, st)
        nb = sb("nb", [P, E], F32, st)
        cum = sb("cum", [P, E + 1], F32, st)
        yhot = sb("yhot", [P, TILES * TOP, E], F32, st)
        ybase = sb("ybase", [P, TILES * TOP], F32, st)
        bcmp = sb("bcmp", [1, NBLK + 1, E], F32, st)
        bcnt = sb("bcnt", [1, NBLK + 1, E], F32, st)
        bexp = sb("bexp", [1, NBLK + 1], F32, st)
        bcum = sb("bcum", [1, NBLK + 1], F32, st)
        st.close()

        s2 = ExitStack()
        bx = sb("bx", [P, 2, 2 * D], F16, s2)
        bxT = sb("bxT", [P, 2 * KD, BLK], F16, s2)
        hid = sb("hid", [P, KH, BLK], F32, s2)
        hidh = sb("hidh", [P, KH, BLK], F16, s2)
        hidl = sb("hidl", [P, KH, BLK], F16, s2)
        by = sb("by", [P, 2, D], F32, s2)
        b2_sb = sb("b2_sb", [P, E, D], F32, s2)
        s2.close()
        s12.close()

        s3 = ExitStack()
        gy = sb("gy", [P, TJ * TOP, D], F32, s3)
        y_idx = sb("y_idx", [P, TJ * TOP], U32, s3)
        y_wt = sb("y_wt", [P, TJ * TOP], F32, s3)
        xe = pair_sb("xe", [P, TJ, D], F32, s3)
        wgT = sb("wgT", [P, KD, H], BF16, s3)
        wuT = sb("wuT", [P, KD, H], BF16, s3)
        wdT = sb("wdT", [P, KH, D], BF16, s3)
        xc = pair_sb("xc", [P, TJ, D], F32, s3)
        xn3 = pair_sb("xn3", [P, TJ, D], F32, s3)
        xT3 = pair_sb("xT3", [P, KD, TJ * P], F32, s3)
        pr3 = pair_sb("pr3", [P, TJ, M], F32, s3)
        prT3 = pair_sb("prT3", [M, TJ * P], F32, s3)
        stat3 = pair_sb("stat3", [P, TJ, 6], F32, s3)
        mv3 = pair_sb("mv3", [P, TJ, 2], F32, s3)
        nt3 = pair_sb("nt3", [P, 5, TJ], F32, s3)
        nmax3 = pair_sb("nmax3", [P, TJ], F32, s3)
        esum3 = pair_sb("esum3", [P, TJ], F32, s3)
        rinv3 = pair_sb("rinv3", [P, TJ], F32, s3)
        xmax = pair_sb("xmax", [P, TJ], F32, s3)
        xscale = pair_sb("xscale", [P, TJ], F32, s3)
        hfac = pair_sb("hfac", [P, 2, TJ], F32, s3)
        xq = pair_sb("xq", [P, TJ, D], BF16, s3)
        xqT = pair_sb("xqT", [P, KD, TJ * P], BF16, s3)
        relu = [sb(f"relu{n}", [P, H], F32, s3) for n in range(2)]
        hh = pair_sb("hh", [P, H], F32, s3)
        hr = pair_sb("hr", [P, H], F32, s3)
        hq = pair_sb("hq", [P, H], BF16, s3)
        hqT = pair_sb("hqT", [P, KH, P], BF16, s3)
        hm = pair_sb("hm", [P, 5, TJ], F32, s3)
        xo = pair_sb("xo", [P, TJ, D], F32, s3)
        s3.close()

        consts_made, pool_order, vec_order = sem("consts_made"), sem("pool_order"), sem("vec_order")
        ctx_in_sem, weights_in = sem("ctx_loaded"), sem("weights_loaded")
        setup_mm, setup_out, act_order = sem("setup_mm"), sem("setup_out"), sem("act_order")
        stage_full, high_done, low_done = (
            [sem(f"{name}{n}") for n in range(STAGES)] for name in ("stage_full", "high_done", "low_done"))
        x_in, ln1, xT1_mm, xT1, score_mm, score_max, probs = (
            pair(n) for n in ("x_in", "ln1", "xT1_mm", "xT1", "score_mm", "score_max", "probs"))
        probsT_mm, probsT, attn_mm, x1_made, x1_out, ln2 = (
            pair(n) for n in ("probsT_mm", "probsT", "attn_mm", "x1_made", "x1_out", "ln2"))
        xT2_mm, xT2, logit_mm, logit_max, gates, picked, rank_mm, placed, rows_sent = (
            pair(n) for n in ("xT2_mm", "xT2", "logit_mm", "logit_max", "gates", "picked", "rank_mm",
                              "placed", "rows_sent"))
        rows_free, ln1_rstd, ln2_rstd = pair("rows_free"), pair("ln1_rstd"), pair("ln2_rstd")
        zeros_made, count_mm, tables, pads_sent = sem("zeros_made"), sem("count_mm"), sem("tables"), sem("pads_sent")
        y_placed = sem("y_placed")
        bx_in, bxT_mm, bxT_made = sem("bx_in"), sem("bxT_mm"), sem("bxT_made")
        hid_mm, hid_made, hid_split = sem("hid_mm"), sem("hid_made"), sem("hid_split")
        b2_in, by_mm, by_made, by_out = sem("b2_in"), sem("by_mm"), sem("by_made"), sem("by_out")
        tern_in = [sem(f"tern_in{n}") for n in range(3)]
        pads_placed, tern_scaled = sem("pads_placed"), sem("tern_scaled")
        tern_sum, tern_total, tern_quant, tern_T, tern_out = (
            sem(n) for n in ("tern_sum", "tern_total", "tern_quant", "tern_T", "tern_out"))
        y_in, pool_order3 = sem("y_in"), sem("pool_order3")
        x1_in, x2_made, ln3_guess, ln3_rstd, ln3, xT3_mm, xT3_made, score3_mm, score3_max, probs3 = (
            pair(n) for n in ("x1_in", "x2_made", "ln3_guess", "ln3_rstd", "ln3", "xT3_mm", "xT3_made",
                              "score3_mm", "score3_max", "probs3"))
        probsT3_mm, probsT3, attn3_mm, x3_made, ln4_guess, ln4_rstd, ln4, xq_made, xqT_mm, xqT_made = (
            pair(n) for n in ("probsT3_mm", "probsT3", "attn3_mm", "x3_made", "ln4_guess", "ln4_rstd", "ln4",
                              "xq_made", "xqT_mm", "xqT_made"))
        gate_mm, up_mm, relu_made, relu2_made, h_made, h_scale, h_round, hq_made, hqT_mm, hqT_made, down_mm = (
            sem(n) for n in ("gate_mm", "up_mm", "relu_made", "relu2_made", "h_made", "h_scale", "h_round", "hq_made",
                             "hqT_mm", "hqT_made", "down_mm"))
        xo_made, out_done = sem("xo_made"), pair("out_done")
        SMALL = 16 * 11
        SENT = 16 * TJ * TOP * B

        def bank_wide(s):
            return ps[:, 4 * s:4 * s + 2, :]

        def bank_c(s):
            return ps[:, 4 * s + 2, :]

        def bank_d(s):
            return ps[:, 4 * s + 3, :]

        def by_tile(ap, width):
            return ap.rearrange("p (j m) -> p j m", j=TJ)[:, :, 0:width]

        gate_ps = ps[:, 0:2, :].rearrange("p a n -> p (a n)")
        up_ps = ps[:, 2:4, :].rearrange("p a n -> p (a n)")
        turned_ps = ps[:, 4, :].bitcast(BF16)
        down_ps = ps[:, 5, 0:D]
        attn_ps = ps[:, 6:8, :]

        def phase1(unit, loop, start=None):
            if start:
                start()
            with loop(0, B - 1) as b:
                unit((b, 0), (b, 1), (b + 1, 0))
                unit((b, 1), (b + 1, 0), (b + 1, 1))
            unit((B - 1, 0), (B - 1, 1), None)
            unit((B - 1, 1), None, None)

        def phase3(unit, loop, start=None):
            if start:
                start()

            def nth(u, b=0):
                return (b + u // ST, u % ST) if not isinstance(b, int) or 0 <= b * ST + u < B * ST else None

            def unit_at(u, b=0):
                unit(*nth(u, b), nth(u - 1, b), nth(u + 1, b), nth(u + 2, b), nth(u + 3, b))

            unit_at(0)
            with loop(0, B - 2) as b:
                unit_at(1, b)
                unit_at(2, b)
            for u in range(B * ST - 3, B * ST):
                unit_at(u)

        def tile_no(b, s, j):
            return b * (ST * TJ) + (s * TJ + j)

        def token_rows(rows_ap, b, s):
            return rows_ap[bass.ds(b * S + s * TJ * P, TJ * P), :].rearrange("(j p) d -> p j d", p=P)

        def block_rows(rows_ap, row):
            return rows_ap[bass.ds(row, BLK), :].rearrange("(h p) c -> p h c", p=P)

        def stage_piece(n):
            return n // 4, n % 4 // 2, n % 2

        def weight_at(which, half, e):
            if which == 0:
                return bass.ds(e * KD + half, 1)
            return bass.ds(e * KH + half * (KH // 2), KH // 2)

        def staged(n, which):
            k = 1 if which == 0 else KH // 2
            return stage[n % STAGES][:].rearrange("p (k c) -> p k c", k=k)

        block = keep.enter_context(nc.Block())

        def pads(eng, experts):
            eng.wait_ge(zeros_made, 1)
            eng.wait_ge(pads_placed, 1)
            for e in experts:
                row = eng.value_load(pad_row[0:1, e:e + 1], min_val=0, max_val=E * REGION - BLK)
                eng.dma_start(block_rows(sent, row), zrow[:]).then_inc(pads_sent, 16)

        @block.sync
        def _(sp):
            for s in range(ST):
                sp.sem_inc(x1_out[s], 16)
            for n in range(STAGES):
                sp.sem_inc(low_done[n], 1)
            sp.dma_start(ctx_sb[:], ctx_in.rearrange("b m d -> m b d")).then_inc(ctx_in_sem, 16)
            for dst, src in ((w0_sb, w0), (wk_sb, wk), (wq_sb, wq), (wv_sb, wv), (wo_sb, wo), (wr_sb, wr)):
                sp.dma_start(dst[:], src.rearrange("(k p) d -> p k d", p=P)).then_inc(weights_in, 16)
            for n, src in enumerate((b0, bq, bv)):
                sp.dma_start(bcols_in[n * KD:(n + 1) * KD, :], src.rearrange("(k p) -> k p", p=P)).then_inc(weights_in, 16)
            sp.dma_start(bo_row[:], bo.rearrange("(a n) -> a n", a=1)).then_inc(weights_in, 16)
            sp.dma_start(bcols_in[3 * KD:, :], b1.rearrange("e (c p) -> (e c) p", p=P)).then_inc(weights_in, 16)
            sp.wait_ge(setup_out, 13)

            w1_p = w1.rearrange("e (k p) n -> (e k) p n", p=P)
            w2_p = w2.rearrange("e (h k p) n -> (e h) p k n", p=P, h=2)

            def load_x(b, s):
                sp.wait_ge(x1_out[s], 16 * b + 16)
                sp.dma_start(xa[s][:], token_rows(x_rows, b, s)).then_inc(x_in[s], 16)

            def load_piece(b, n):
                e_off, which, half = stage_piece(n)
                sp.wait_ge(low_done[n % STAGES], b * (8 // STAGES) + n // STAGES + 1)
                if which == 0:
                    src = w1_p[bass.ds(b * 4 + e_off * 2 + half, 1)].rearrange("o p n -> p o n")
                else:
                    src = w2_p[bass.ds(b * 4 + e_off * 2 + half, 1)].rearrange("o p k n -> (o p) k n")
                sp.dma_start(staged(n, which), src).then_inc(stage_full[n % STAGES], 16)

            def sp_unit(routing, attention, first):
                b, s = routing
                load_piece(b, 4 * s)
                load_piece(b, 4 * s + 1)
                sp.wait_ge(x1_made[s], b + 1)
                sp.dma_start(token_rows(x1_rows, b, s), xa[s][:]).then_inc(x1_out[s], 16)
                if first:
                    sp.wait_ge(ln2[s], b + 1)
                    load_x(*first)
                load_piece(b, 4 * s + 2)
                load_piece(b, 4 * s + 3)

            def sp_start():
                for s in range(ST):
                    load_x(0, s)

            phase1(sp_unit, sp.Fori, sp_start)

            for s in range(ST):
                sp.wait_ge(x1_out[s], 16 * B + 16)
                sp.wait_ge(picked[s], B)
            for n, w in enumerate((wg, wu, wd)):
                c = H // P if n < 2 else KD
                sp.dma_start(tern[n][:].rearrange("p (c n) -> p c n", c=c), w.rearrange("(c p) n -> p c n", p=P))\
                  .then_inc(tern_in[n], 16)

            pads(sp, range(0, E // 2))
            for s in range(ST):
                sp.wait_ge(rows_sent[s], SENT)
            for n in range(STAGES):
                sp.wait_ge(low_done[n], 8 // STAGES * B + 1)
            sp.wait_ge(pads_sent, 16 * E)
            sp.wait_ge(y_placed, 1)

            def load_block(n):
                row = sp.value_load(block_row[0:1, bass.ds(n, 1)], min_val=0, max_val=E * REGION - BLK)
                sp.dma_start(bx[:], block_rows(sent, row)).then_inc(bx_in, 16)

            load_block(0)
            sp.dma_start(b2_sb[:].rearrange("p e n -> p (e n)"),
                         b2.rearrange("(a e) n -> a (e n)", a=1).to_broadcast([P, E * D])).then_inc(b2_in, 16)
            with sp.Fori(0, NBLK) as n:
                sp.wait_ge(bxT_mm, n + 1)
                load_block(n + 1)
                sp.wait_ge(by_made, 2 * n + 3)
                sp.dma_start(block_rows(made, n * BLK), by[:]).then_inc(by_out, 16)

            sp.wait_ge(by_out, 16 * NBLK + 16)
            for s in range(ST):
                sp.dma_start(xe[s][:], token_rows(x1_rows, 0, s)).then_inc(x1_in[s], 16)

            def outputs(b, s):
                sp.wait_ge(xo_made, tile_no(b, s, TJ - 1) + 1)
                sp.dma_start(token_rows(out_rows, b, s), xo[s][:]).then_inc(out_done[s], 16)

            def x1_of(b, s):
                sp.dma_start(xe[s][:], token_rows(x1_rows, b, s)).then_inc(x1_in[s], 16)

            def sp_start():
                sp.wait_ge(x3_made[0], 1)
                x1_of(1, 0)

            def sp_unit(b, s, before_, second, first, prep):
                if prep:
                    sp.wait_ge(x3_made[prep[1]], prep[0])
                    x1_of(*prep)
                if before_:
                    outputs(*before_)

            phase3(sp_unit, sp.Fori, sp_start)
            outputs(B - 1, ST - 1)
            for s in range(ST):
                sp.wait_ge(out_done[s], 16 * B + 16)

        @block.gpsimd
        def _(pool):
            g = nc.gpsimd
            o = Order(pool, pool_order)
            g.memset(ident[:], 0.0)
            g.memset(before[:], 1.0)
            g.memset(ones[:], 1.0)
            g.memset(onesb[:], 1.0)
            g.memset(magic[:], MAGIC)
            g.memset(prior[:], 0.0)
            o.did(g.iota(iota8[:], [[1, E]], base=0, channel_multiplier=0, allow_small_or_imprecise_dtypes=True))
            o.sync()
            g.affine_select(out=ident[:], in_=ident[:], compare_op=ALU.not_equal, fill=1.0,
                            base=0, pattern=[[-1, P]], channel_multiplier=1)
            o.did(g.affine_select(out=before[:], in_=before[:], compare_op=ALU.is_gt, fill=0.0,
                                  base=0, pattern=[[1, P]], channel_multiplier=-1))
            o.sync()
            g.tensor_copy(ident16[:], ident[:])
            g.tensor_copy(identb[:], ident[:]).then_inc(consts_made, 1)
            pool.wait_ge(setup_out, 13)
            g.memset(zrow[:], 0.0).then_inc(zeros_made, 1)
            g.iota(bnum[:], [[1, NBLK + 1]], base=0, channel_multiplier=0, allow_small_or_imprecise_dtypes=True)
            g.iota(prow[:], [[REGION, E]], base=0, channel_multiplier=0, allow_small_or_imprecise_dtypes=True)\
             .then_inc(consts_made, 1)

            turn = [pool.alloc_register(f"turn{s}") for s in range(ST)]
            for s in range(ST):
                pool.reg_mov(turn[s], 2)

            def low_half(b, n):
                e_off, which, half = stage_piece(n)
                at = weight_at(which, half, b * 2 + e_off)
                hi, lo = ((w1h, w1l), (w2h, w2l))[which]
                pool.wait_ge(high_done[n % STAGES], b * (8 // STAGES) + n // STAGES + 1)
                g.tensor_tensor(lo[:, at, :], staged(n, which), hi[:, at, :], ALU.subtract)\
                 .then_inc(low_done[n % STAGES], 1)

            def send(s, ns):
                for n in ns:
                    g.indirect_dma_start(sent, bass.IndirectOffsetOnAxis(x_slot[s][:, n:n + 1], 0),
                                         rows[s][:, n // TOP, :], None).then_inc(rows_sent[s], 16)

            def pool_unit1(routing, attention, first):
                b, s = routing
                low_half(b, 4 * s)
                low_half(b, 4 * s + 1)
                pool.wait_ge(placed[s], b + 2 if isinstance(b, int) else turn[s])
                pool.reg_add(turn[s], turn[s], 1)
                send(s, range(0, TJ * TOP // 2))
                low_half(b, 4 * s + 2)
                low_half(b, 4 * s + 3)
                send(s, range(TJ * TOP // 2, TJ * TOP))
                pool.wait_ge(rows_sent[s], 16 * TJ * TOP * b + 16 * TJ * TOP)
                pool.sem_inc(rows_free[s], 1)

            phase1(pool_unit1, pool.Fori)
            o = Order(pool, pool_order3)
            pool.wait_ge(tern_scaled, 1)
            for n in range(3):
                w = tern[n][:]
                o.did(g.tensor_scalar(w, w, tscale[:, n:n + 1], MAGIC, ALU.mult, ALU.add))
                o.sync()
                o.did(g.tensor_scalar(w, w, MAGIC - 1.0, MAGIC + 1.0, ALU.max, ALU.min))
                o.sync()
                g.tensor_scalar(ternq[n], w, MAGIC, None, ALU.subtract).then_inc(tern_quant, 1)
                pool.wait_ge(tern_quant, n + 1)
            o.clear()

            pool.wait_ge(by_out, 16 * NBLK + 16)
            counts = {}

            def awaited(signal, step, key, b, nth):
                pool.wait_ge(signal, step * nth if isinstance(b, int) else counts[key])
                pool.reg_add(counts[key], counts[key], step)

            for key, step in [("y_in", 16 * TJ * TOP)] + \
                    [(f"{n}{s}", 16 if n == "x1" else 1) for n in ("x1", "g3", "g4") for s in range(ST)]:
                counts[key] = pool.alloc_register(f"next_{key}")
                pool.reg_mov(counts[key], step)

            def step(instruction):
                o.did(instruction)
                o.sync()

            def newton(b, s, guess, key, done):
                awaited(guess, 1, f"{key}{s}", b, b + 1)
                y, minus_half, t, off = (nt3[s][:, n, :] for n in (1, 2, 3, 4))
                for _ in range(3):
                    step(g.tensor_tensor(t, y, y, ALU.mult))
                    step(g.tensor_tensor(t, t, minus_half, ALU.mult))
                    step(g.tensor_scalar(t, t, 1.5, None, ALU.add))
                    step(g.tensor_tensor(y, y, t, ALU.mult))
                step(g.tensor_tensor(t, y, mv3[s][:, :, 0], ALU.mult))
                g.tensor_scalar(off, t, -1.0, None, ALU.mult).then_inc(done, 1)

            def places(b, s):
                at = bass.ds(b * (ST * TJ * TOP) + s * TJ * TOP, TJ * TOP)
                g.tensor_copy(y_wt[:], weight[:, at])
                step(g.tensor_copy(y_idx[:], y_slot[:, at]))

            def gather(ns):
                for n in ns:
                    g.indirect_dma_start(gy[:, n, :], None, made,
                                         bass.IndirectOffsetOnAxis(y_idx[:, n:n + 1], 0)).then_inc(y_in, 16)

            def weighted(b, s):
                awaited(y_in, 16 * TJ * TOP, "y_in", b, b * ST + s + 1)
                weights = y_wt[:].rearrange("p (n o) -> p n o", o=1).broadcast_to([P, TJ * TOP, D])
                step(g.tensor_tensor(gy[:], gy[:], weights, ALU.mult))

            def summed(b, s):
                both = gy[:].rearrange("p (j k) n -> p j k n", k=TOP)
                step(g.tensor_tensor(both[:, :, 0, :], both[:, :, 0, :], both[:, :, 1, :], ALU.add))
                awaited(x1_in[s], 16, f"x1{s}", b, b + 1)
                g.tensor_tensor(xe[s][:], xe[s][:], both[:, :, 0, :], ALU.add).then_inc(x2_made[s], 1)

            def prepared(b, s):
                places(b, s)
                gather(range(TJ * TOP))
                if (b, s) == (0, 0):
                    pool.wait_ge(x2_made[s], 1)
                    for key, step_ in (("y_in", 16 * TJ * TOP), ("x10", 16), ("g30", 1), ("g40", 1)):
                        pool.reg_add(counts[key], counts[key], step_)
                    return
                weighted(b, s)
                summed(b, s)
                pool.wait_ge(x2_made[s], b + 1)

            def pool_unit(b, s, before_, second, first, prep):
                if prep:
                    places(*prep)
                    gather(range(0, TJ * TOP // 2))
                if first:
                    newton(*first, ln3_guess[s], "g3", ln3_rstd[s])
                if second:
                    newton(*second, ln4_guess[1 - s], "g4", ln4_rstd[1 - s])
                if prep:
                    gather(range(TJ * TOP // 2, TJ * TOP))
                if prep:
                    weighted(*prep)
                    summed(*prep)
                if first or second:
                    o.clear()

            def pool_start():
                prepared(0, 0)
                o.clear()
                prepared(0, 1)
                newton(0, 1, ln3_guess[1], "g3", ln3_rstd[1])
                o.clear()
                prepared(1, 0)
                o.clear()

            phase3(pool_unit, pool.Fori, pool_start)

        @block.scalar
        def _(act):
            a = nc.scalar
            BM = B * M

            def out_of(n, dst, src):
                act.wait_ge(setup_mm, n)
                a.activation(dst, src, ACT.Copy).then_inc(setup_out, 1)

            def two_pieces(bank):
                return ps[:, bank, :].rearrange("p (k n) -> p k n", k=KD)

            act.wait_ge(weights_in, SMALL)
            out_of(1, ctxT[:], ps[:, 0:2, 0:BM])
            out_of(2, bcols[:], ps[:, 6, 0:NROW])
            out_of(3, w0T[:], two_pieces(2))
            out_of(4, wkT[:], two_pieces(3))
            out_of(5, wvT[:], two_pieces(4))
            out_of(6, woT[:], two_pieces(5))
            out_of(7, kpT[:], ps[:, 0:2, 0:BM])
            act.wait_ge(setup_out, 2)
            act.wait_ge(setup_mm, 8)
            for k in range(KD):
                last = a.activation(eoT[:, k, :], ps[:, 2 + k, 0:BM], ACT.Identity, bias=bcols[:, k:k + 1])
            last.then_inc(setup_out, 1)
            act.wait_ge(setup_mm, 9)
            for k in range(KD):
                last = a.activation(vpT[:, k, :], ps[:, 4 + k, 0:BM], ACT.Identity, bias=bcols[:, 2 * KD + k:2 * KD + k + 1])
            last.then_inc(setup_out, 1)
            scale = float(D) ** -0.5
            act.wait_ge(setup_mm, 10)
            a.activation(g0[:], ps[:, 0:2, 0:BM], ACT.Copy)
            a.activation(c0[:], ps[0:1, 6, 0:BM], ACT.Copy).then_inc(setup_out, 1)
            act.wait_ge(setup_mm, 11)
            a.activation(g1[:], ps[:, 2:4, 0:BM], ACT.Copy, scale=scale)
            a.activation(c1[:], ps[0:1, 7, 0:BM], ACT.Copy, scale=scale).then_inc(setup_out, 1)
            for h in range(2):
                out_of(12 + h, vo[:, 2 * h:2 * h + 2, :], ps[0:M, 4 + h, :].rearrange("p (b n) -> p b n", b=2))

            def high_half(b, n):
                e_off, which, half = stage_piece(n)
                at = weight_at(which, half, b * 2 + e_off)
                act.wait_ge(stage_full[n % STAGES], 16 * (b * (8 // STAGES) + n // STAGES) + 16)
                a.activation((w1h, w2h)[which][:, at, :], staged(n, which), ACT.Copy).then_inc(high_done[n % STAGES], 1)

            def exponentials(probs_out, scores, neg_max, sums, done):
                for j in range(TJ):
                    last = a.activation(probs_out[:, j, :], scores[:, j, :], ACT.Exp,
                                        bias=neg_max[:, j:j + 1], accum_out=sums[:, j:j + 1])
                last.then_inc(done, 1)

            def scaled_rows(dst, src, numbers, done):
                for j in range(TJ):
                    last = a.activation(dst[:, j, :], src[:, j, :], ACT.Identity,
                                        bias=numbers[:, 4, j:j + 1], scale=numbers[:, 1, j:j + 1])
                last.then_inc(done, 1)

            def norm1(b, s):
                act.wait_ge(ln1_rstd[s], b + 1)
                scaled_rows(xn[s], xa[s], nt[s], ln1[s])

            def norm2(b, s):
                act.wait_ge(ln2_rstd[s], b + 1)
                scaled_rows(xn[s], xa[s], nt[s], ln2[s])

            def xT1_out(b, s):
                act.wait_ge(xT1_mm[s], b + 1)
                a.activation(xT[s][:], bank_wide(s), ACT.Copy).then_inc(xT1[s], 1)

            def xT2_out(b, s):
                act.wait_ge(xT2_mm[s], b + 1)
                a.activation(xT[s][:], bank_wide(s), ACT.Copy).then_inc(xT2[s], 1)

            def exps1(b, s):
                act.wait_ge(score_max[s], b + 1)
                exponentials(pr[s], by_tile(bank_c(s), M), nmax[s], esum[s], probs[s])

            def probsT_out(b, s):
                act.wait_ge(probsT_mm[s], b + 1)
                a.activation(prT[s][:], bank_d(s)[0:M, :], ACT.Copy).then_inc(probsT[s], 1)

            def gate_exps(b, s):
                act.wait_ge(logit_max[s], b + 1)
                logits = bank_c(s)[:, 0:TJ * E].rearrange("p (j m) -> p j m", j=TJ)
                exponentials(pe_[s], logits, nmax[s], esum[s], gates[s])

            def act_unit1(routing, attention, first):
                b, s = routing
                if attention:
                    xT1_out(*attention)
                norm2(b, s)
                high_half(b, 4 * s)
                xT2_out(b, s)
                if attention:
                    exps1(*attention)
                high_half(b, 4 * s + 1)
                if attention:
                    probsT_out(*attention)
                gate_exps(b, s)
                if first:
                    norm1(*first)
                high_half(b, 4 * s + 2)
                high_half(b, 4 * s + 3)

            def act_start1():
                norm1(0, 0)
                xT1_out(0, 0)
                exps1(0, 0)
                probsT_out(0, 0)
                norm1(0, 1)

            phase1(act_unit1, act.Fori, act_start1)

            for n in range(3):
                act.wait_ge(tern_in[n], 16)
                if n:
                    act.wait_ge(tern_sum, n)
                a.activation(ternq[0], tern[n][:], ACT.Abs, accum_out=tsum[:, n:n + 1]).then_inc(tern_sum, 1)
            pads(act, range(E // 2, E))

            act.wait_ge(y_placed, 1)
            act.wait_ge(tables, 1)
            for s in range(ST):
                act.wait_ge(rows_sent[s], SENT)
            with act.Fori(0, NBLK) as n:
                e = act.value_load(block_expert[0:1, bass.ds(n, 1)], min_val=0, max_val=E - 1)
                for c in range(KH):
                    act.wait_ge(hid_mm, KH * n + c + 1)
                    bias = bcols[:, bass.ds(e * KH + (3 * KD + c), 1)]
                    act.wait_ge(tables, 1)
                    a.activation(hid[:, c, :], ps[:, c % 4, 0:BLK], ACT.Gelu_apprx_tanh, bias=bias)\
                     .then_inc(hid_made, 1)

            def normalised(b, s, rstd, done):
                act.wait_ge(rstd[s], b + 1)
                scaled_rows(xn3[s], (xe if rstd is ln3_rstd else xc)[s], nt3[s], done[s])

            def xT3_out(b, s):
                act.wait_ge(xT3_mm[s], b + 1)
                a.activation(xT3[s][:], attn_ps, ACT.Copy).then_inc(xT3_made[s], 1)

            def exps3(b, s):
                act.wait_ge(score3_max[s], b + 1)
                exponentials(pr3[s], by_tile(attn_ps[:, 0, :], M), nmax3[s], esum3[s], probs3[s])

            def probsT3_out(b, s):
                act.wait_ge(probsT3_mm[s], b + 1)
                a.activation(prT3[s][:], attn_ps[0:M, 1, :], ACT.Copy).then_inc(probsT3[s], 1)

            def xqT_out(b, s):
                act.wait_ge(xqT_mm[s], b + 1)
                a.activation(xqT[s][:], turned_ps.rearrange("p (k n) -> p k n", k=KD), ACT.Copy)\
                 .then_inc(xqT_made[s], 1)

            def hqT_out(t, j):
                act.wait_ge(hqT_mm, t + 1)
                a.activation(hqT[j % 2][:], turned_ps.rearrange("p (c n) -> p c n", c=KH), ACT.Copy)\
                 .then_inc(hqT_made, 1)

            def relu_squared(t, j):
                act.wait_ge(gate_mm, t + 1)
                a.activation(relu[j % 2][:], gate_ps, ACT.Relu).then_inc(relu_made, 1)
                act.wait_ge(relu_made, t + 1)
                a.activation(relu[j % 2][:], relu[j % 2][:], ACT.Square).then_inc(relu2_made, 1)

            def act_unit(b, s, before_, second, first, prep):
                for j in range(TJ):
                    t = tile_no(b, s, j)
                    if j == 0 and not before_:
                        relu_squared(t, j)
                    if j < TJ - 1:
                        relu_squared(t + 1, j + 1)
                    if j == 0 and not before_:
                        exps3(*second)
                    if j == 3 and second:
                        xqT_out(*second)
                    if j or before_:
                        hqT_out(t - 1, j - 1)
                    if j == 0 and second:
                        probsT3_out(*second)
                    if j == 1 and first:
                        normalised(*first, ln3_rstd, ln3)
                    if j == 2:
                        if first:
                            xT3_out(*first)
                    if j == 3 and second:
                        relu_squared(t + 1, 0)
                    act.wait_ge(h_scale, t + 1)
                    a.activation(hr[j % 2][:], hh[j % 2][:], ACT.Identity, bias=magic[:, 0:1],
                                 scale=hm[s][:, 3, j:j + 1]).then_inc(h_round, 1)
                    if j == 3 and first:
                        exps3(*first)
                    if j == 1 and second:
                        normalised(*second, ln4_rstd, ln4)

            def act_start():
                normalised(0, 0, ln3_rstd, ln3)
                xT3_out(0, 0)
                exps3(0, 0)
                probsT3_out(0, 0)
                normalised(0, 0, ln4_rstd, ln4)
                xqT_out(0, 0)
                normalised(0, 1, ln3_rstd, ln3)
                xT3_out(0, 1)

            phase3(act_unit, act.Fori, act_start)
            hqT_out(tile_no(B - 1, ST - 1, TJ - 1), TJ - 1)

        @block.vector
        def _(dve):
            for s in range(ST):
                dve.sem_inc(rows_free[s], 1)
                dve.sem_inc(out_done[s], 16)
            dve.sem_inc(by_out, 16)
            v = nc.vector
            o = Order(dve, vec_order)

            def row_factors(src, stat_, mv_, nt_, done):
                for j in range(TJ):
                    last = v.bn_stats(stat_[:, j, :], src[:, j, :])
                o.did(last)
                o.sync()
                for j in range(TJ):
                    last = v.bn_aggr(mv_[:, j, :], stat_[:, j, :])
                o.did(last)
                o.sync()
                ve, y, minus_half, t, off = (nt_[:, n, :] for n in range(5))
                o.did(v.tensor_scalar(ve, mv_[:, :, 1], LN_EPS, None, ALU.add))
                o.sync()
                v.tensor_scalar(minus_half, ve, -0.5, None, ALU.mult)
                o.did(v.tensor_scalar(t.bitcast(I32), ve.bitcast(I32), 1, None, ALU.logical_shift_right))
                o.sync()
                o.did(v.tensor_scalar(y.bitcast(I32), t.bitcast(I32), -1.0, float(0x5F3759DF), ALU.mult, ALU.add))
                for _ in range(3):
                    o.sync()
                    o.did(v.tensor_tensor(t, y, y, ALU.mult))
                    o.sync()
                    o.did(v.tensor_tensor(t, t, minus_half, ALU.mult))
                    o.sync()
                    o.did(v.scalar_tensor_tensor(y, t, 1.5, y, ALU.add, ALU.mult))
                o.sync()
                v.scalar_tensor_tensor(off, mv_[:, :, 0], -1.0, y, ALU.mult, ALU.mult).then_inc(done, 1)

            def neg_max(dst, src, done):
                v.tensor_reduce(dst[:], src, AX.X, ALU.max, negate=True).then_inc(done, 1)

            dve.wait_ge(consts_made, 1)
            dve.wait_ge(setup_out, 13)
            def first_norm(b, s):
                dve.wait_ge(x_in[s], 16 * b + 16)
                row_factors(xa[s], stat[s], mv[s], nt[s], ln1_rstd[s])

            def max1(b, s):
                dve.wait_ge(score_mm[s], b + 1)
                neg_max(nmax[s], by_tile(bank_c(s), M), score_max[s])

            def x1(b, s):
                dve.wait_ge(probs[s], b + 1)
                o.did(v.reciprocal(rinv[s][:], esum[s][:]))
                dve.wait_ge(attn_mm[s], b + 1)
                o.sync()
                out4 = bank_wide(s).rearrange("p a (c n) -> p (a c) n", c=2)
                for j in range(TJ):
                    last = v.scalar_tensor_tensor(xa[s][:, j, :], out4[:, j, :], rinv[s][:, j:j + 1],
                                                  xa[s][:, j, :], ALU.mult, ALU.add)
                last.then_inc(x1_made[s], 1)

            def second_norm(b, s):
                dve.wait_ge(x1_made[s], b + 1)
                row_factors(xa[s], stat[s], mv[s], nt[s], ln2_rstd[s])

            def sent_rows(b, s):
                dve.wait_ge(rows_free[s], b + 1)
                dve.wait_ge(ln2[s], b + 1)
                o.did(v.tensor_copy(rows[s][:, :, 0:D], xn[s][:]))
                o.sync()
                o.did(v.tensor_tensor(rows[s][:, :, D:2 * D], xn[s][:], rows[s][:, :, 0:D], ALU.subtract))

            def gate_max(b, s):
                dve.wait_ge(logit_mm[s], b + 1)
                neg_max(nmax[s], bank_c(s)[:, 0:TJ * E].rearrange("p (j m) -> p j m", j=TJ), logit_max[s])

            def picked_experts(b, s):
                dve.wait_ge(gates[s], b + 1)
                o.did(v.reciprocal(rinv[s][:], esum[s][:]))
                o.sync()
                o.did(v.tensor_tensor(pe_[s][:], pe_[s][:], rinv[s][:].unsqueeze(2).to_broadcast([P, TJ, E]),
                                      ALU.mult))
                o.sync()
                for j in range(TJ):
                    last = v.max(top[s][:, j, :], pe_[s][:, j, :])
                o.did(last)
                o.sync()
                for j in range(TJ):
                    last = v.max_index(topi[s][:, j, :], top[s][:, j, :], pe_[s][:, j, :])
                o.did(last)
                o.sync()
                at = bass.ds((b * ST + s) * TJ * TOP, TJ * TOP)
                v.tensor_copy(weight[:, at].rearrange("p (j k) -> p j k", k=TOP), top[s][:, :, 0:TOP])
                o.did(v.tensor_copy(ex2[s][:].rearrange("p (j k) -> p j k", k=TOP), topi[s][:, :, 0:TOP]))
                o.sync()
                v.tensor_copy(expert[:, at], ex2[s][:])
                o.did(v.tensor_tensor(hot[s][:], iota8[:].unsqueeze(1).to_broadcast([P, TJ * TOP, E]),
                                      ex2[s][:].unsqueeze(2).to_broadcast([P, TJ * TOP, E]), ALU.is_equal))
                o.sync()
                pairs = hot[s][:].rearrange("p (j k) e -> p j k e", k=TOP)
                o.did(v.tensor_tensor(picks[s][:], pairs[:, :, 0, :], pairs[:, :, 1, :], ALU.add))
                for j in range(TJ):
                    o.sync()
                    o.did(v.tensor_tensor(prior[:, j + 1, :], prior[:, j, :], picks[s][:, j, :], ALU.add))
                o.sync()
                o.did(v.tensor_copy(pri[s][:], prior[:, 0:TJ, :]))
                o.sync()
                v.tensor_copy(prior[:, 0, :], prior[:, TJ, :]).then_inc(picked[s], 1)

            def places(b, s):
                dve.wait_ge(rank_mm[s], b + 1)
                ranks = bank_c(s)[:, 64:64 + TJ * E].rearrange("p (j e) -> p j e", j=TJ)
                o.did(v.tensor_tensor(prod[s][:].rearrange("p (j k) e -> p j k e", k=TOP),
                                      hot[s][:].rearrange("p (j k) e -> p j k e", k=TOP),
                                      ranks.unsqueeze(2).to_broadcast([P, TJ, TOP, E]), ALU.mult))
                o.sync()
                o.did(v.tensor_reduce(rk2[s][:], prod[s][:], AX.X, ALU.add))
                o.sync()
                at = bass.ds((b * ST + s) * TJ * TOP, TJ * TOP)
                o.did(v.tensor_copy(rank[:, at], rk2[s][:]))
                v.scalar_tensor_tensor(x_slot[s][:], ex2[s][:], float(REGION), rk2[s][:], ALU.mult, ALU.add)\
                 .then_inc(placed[s], 1)

            def dve_unit1(routing, attention, first):
                second_norm(*routing)
                sent_rows(*routing)
                if attention:
                    max1(*attention)
                if first:
                    first_norm(*first)
                gate_max(*routing)
                picked_experts(*routing)
                if attention:
                    x1(*attention)
                places(*routing)
                o.clear()

            def dve_start1():
                first_norm(0, 0)
                first_norm(0, 1)
                max1(0, 0)
                x1(0, 0)
                o.clear()

            phase1(dve_unit1, dve.Fori, dve_start1)

            def step(instruction):
                o.did(instruction)
                o.sync()

            dve.wait_ge(consts_made, 2)
            for n in range(2):
                dve.wait_ge(low_done[n], 8 // STAGES * B + 1)
            dve.wait_ge(count_mm, 1)
            step(v.tensor_copy(cnt[:], ps[:, 0, 0:E]))
            v.tensor_tensor(pad_row[:], prow[:], cnt[0:1, :], ALU.add).then_inc(pads_placed, 1)
            step(v.tensor_scalar(nb[:], cnt[:], 1.0 / BLK, 0.5 - 0.5 / BLK, ALU.mult, ALU.add))
            step(v.tensor_scalar(nb[:], nb[:], MAGIC, None, ALU.add))
            step(v.tensor_scalar(nb[:], nb[:], MAGIC, None, ALU.subtract))
            step(v.memset(cum[:], 0.0))
            for e in range(E):
                step(v.tensor_tensor(cum[:, e + 1:e + 2], cum[:, e:e + 1], nb[:, e:e + 1], ALU.add))
            step(v.tensor_scalar(bexp[:, 0:1], cum[0:1, E:E + 1], 1.0, None, ALU.subtract))
            step(v.tensor_scalar(bnum[:], bnum[:], bexp[:, 0:1], None, ALU.min))
            NB1 = NBLK + 1
            step(v.tensor_tensor(bcmp[:], cum[0:1, 1:E + 1].unsqueeze(1).to_broadcast([1, NB1, E]),
                                 bnum[:].unsqueeze(2).to_broadcast([1, NB1, E]), ALU.is_le))
            v.tensor_reduce(bexp[:], bcmp[:], AX.X, ALU.add)
            step(v.tensor_tensor(bcnt[:], bcmp[:], nb[0:1, :].unsqueeze(1).to_broadcast([1, NB1, E]), ALU.mult))
            step(v.tensor_reduce(bcum[:], bcnt[:], AX.X, ALU.add))
            v.tensor_copy(block_expert[:], bexp[:])
            step(v.tensor_tensor(bnum[:], bnum[:], bcum[:], ALU.subtract))
            step(v.tensor_scalar(bnum[:], bnum[:], float(BLK), None, ALU.mult))
            v.scalar_tensor_tensor(block_row[:], bexp[:], float(REGION), bnum[:], ALU.mult, ALU.add)\
             .then_inc(tables, 1)
            NP_ = TILES * TOP
            step(v.tensor_tensor(yhot[:], iota8[:].unsqueeze(1).to_broadcast([P, NP_, E]),
                                 expert[:].unsqueeze(2).to_broadcast([P, NP_, E]), ALU.is_equal))
            step(v.tensor_tensor(yhot[:], yhot[:], cum[:, 0:E].unsqueeze(1).to_broadcast([P, NP_, E]), ALU.mult))
            step(v.tensor_reduce(ybase[:], yhot[:], AX.X, ALU.add))
            v.scalar_tensor_tensor(y_slot[:], ybase[:], float(BLK), rank[:], ALU.mult, ALU.add).then_inc(y_placed, 1)
            dve.wait_ge(y_placed, 1)
            dve.wait_ge(tern_total, 1)
            step(v.tensor_scalar(wmean[:], ps[:, 7, 0:3], 1.0 / (D * H), Q_EPS, ALU.mult, ALU.max))
            v.reciprocal(tscale[:], wmean[:]).then_inc(tern_scaled, 1)

            def transposed_block(n):
                dve.wait_ge(bxT_mm, n + 1)
                v.tensor_copy(bxT[:], ps[:, 6, :].bitcast(F16).rearrange("p (c n) -> p c n", c=2 * KD))\
                 .then_inc(bxT_made, 1)

            transposed_block(0)
            dve.wait_ge(b2_in, 16)
            o.clear()
            with dve.Fori(0, NBLK) as n:
                e = dve.value_load(block_expert[0:1, bass.ds(n, 1)], min_val=0, max_val=E - 1)
                for c in range(0, KH, 2):
                    dve.wait_ge(hid_made, KH * n + c + 2)
                    o.did(v.tensor_copy(hidh[:, c:c + 2, :], hid[:, c:c + 2, :]))
                    o.sync()
                    v.tensor_tensor(hidl[:, c:c + 2, :], hid[:, c:c + 2, :], hidh[:, c:c + 2, :], ALU.subtract)\
                     .then_inc(hid_split, 1)
                transposed_block(n + 1)
                dve.wait_ge(by_out, 16 * n + 16)
                for h in range(2):
                    dve.wait_ge(by_mm, 2 * n + h + 1)
                    v.tensor_tensor(by[:, h, :], ps[:, 4 + h, 0:D],
                                    b2_sb[:, bass.ds(e, 1), :].rearrange("p a n -> p (a n)"), ALU.add)\
                     .then_inc(by_made, 1)
                o.clear()

            for n in range(3):
                dve.wait_ge(tern_T, n + 1)
                for k in range(KD):
                    src = ps[:, 5 + k, :].bitcast(BF16)
                    if n < 2:
                        last = v.tensor_copy((wgT, wuT)[n][:, k, :], src)
                    else:
                        last = v.tensor_copy(wdT[:, :, k * P:(k + 1) * P], src.rearrange("p (c n) -> p c n", c=KH))
                last.then_inc(tern_out, 1)
            o.clear()

            def first_sum():
                dve.wait_ge(y_in, 16 * TJ * TOP)
                dve.wait_ge(x1_in[0], 16)
                for k in range(TOP):
                    for j in range(TJ):
                        n = j * TOP + k
                        last = v.scalar_tensor_tensor(xe[0][:, j, :], gy[:, n, :], y_wt[:, n:n + 1],
                                                      xe[0][:, j, :], ALU.mult, ALU.add)
                    if k < TOP - 1:
                        step(last)
                last.then_inc(x2_made[0], 1)

            def stats(src, s, done):
                for j in range(TJ):
                    last = v.bn_stats(stat3[s][:, j, :], src[:, j, :])
                step(last)
                for j in range(TJ):
                    last = v.bn_aggr(mv3[s][:, j, :], stat3[s][:, j, :])
                step(last)
                ve, y, minus_half, t = (nt3[s][:, n, :] for n in range(4))
                step(v.tensor_scalar(ve, mv3[s][:, :, 1], LN_EPS, None, ALU.add))
                v.tensor_scalar(minus_half, ve, -0.5, None, ALU.mult)
                step(v.tensor_scalar(t.bitcast(I32), ve.bitcast(I32), 1, None, ALU.logical_shift_right))
                v.tensor_scalar(y.bitcast(I32), t.bitcast(I32), -1.0, float(0x5F3759DF), ALU.mult, ALU.add)\
                 .then_inc(done[s], 1)

            def ln3_stats(b, s):
                dve.wait_ge(x2_made[s], b + 1)
                stats(xe[s], s, ln3_guess)

            def max3(b, s):
                dve.wait_ge(score3_mm[s], b + 1)
                neg_max(nmax3[s], by_tile(attn_ps[:, 0, :], M), score3_max[s])

            def x3(b, s):
                dve.wait_ge(probs3[s], b + 1)
                o.did(v.reciprocal(rinv3[s][:], esum3[s][:]))
                dve.wait_ge(attn3_mm[s], b + 1)
                o.sync()
                out4 = attn_ps.rearrange("p a (c n) -> p (a c) n", c=2)
                for j in range(TJ):
                    last = v.scalar_tensor_tensor(xc[s][:, j, :], out4[:, j, :], rinv3[s][:, j:j + 1],
                                                  xe[s][:, j, :], ALU.mult, ALU.add)
                last.then_inc(x3_made[s], 1)

            def ln4_stats(b, s):
                dve.wait_ge(x3_made[s], b + 1)
                stats(xc[s], s, ln4_guess)

            def row_scales(b, s):
                dve.wait_ge(ln4[s], b + 1)
                step(v.tensor_reduce(xmax[s][:], xn3[s][:], AX.X, ALU.max, apply_absolute_value=True))
                step(v.tensor_scalar(xmax[s][:], xmax[s][:], Q_EPS, None, ALU.max))
                step(v.reciprocal(xscale[s][:], xmax[s][:]))
                step(v.tensor_scalar(xscale[s][:], xscale[s][:], 127.0, None, ALU.mult))
                for j in range(TJ):
                    last = v.tensor_scalar(xn3[s][:, j, :], xn3[s][:, j, :], xscale[s][:, j:j + 1], MAGIC,
                                           ALU.mult, ALU.add)
                o.did(last)

            def row_integers(b, s):
                o.sync()
                v.tensor_scalar(xq[s][:], xn3[s][:], MAGIC, None, ALU.subtract).then_inc(xq_made[s], 1)
                o.did(v.tensor_scalar(hfac[s][:, 0, :], xmax[s][:], 1.0 / 127.0, wmean[:, 0:1], ALU.mult, ALU.mult))
                step(v.tensor_scalar(hfac[s][:, 1, :], xmax[s][:], 1.0 / 127.0, wmean[:, 1:2], ALU.mult, ALU.mult))
                step(v.tensor_tensor(hfac[s][:, 0, :], hfac[s][:, 0, :], hfac[s][:, 0, :], ALU.mult))
                step(v.tensor_tensor(hfac[s][:, 0, :], hfac[s][:, 0, :], hfac[s][:, 1, :], ALU.mult))

            def x4(b, s, j):
                dve.wait_ge(down_mm, tile_no(b, s, j) + 1)
                v.scalar_tensor_tensor(xo[s][:, j, :], down_ps, hm[s][:, 4, j:j + 1], xc[s][:, j, :],
                                       ALU.mult, ALU.add).then_inc(xo_made, 1)

            def dve_unit(b, s, before_, second, first, prep):
                for j in range(TJ):
                    t = tile_no(b, s, j)
                    if j == 3 and first:
                        max3(*first)
                    dve.wait_ge(up_mm, t + 1)
                    dve.wait_ge(relu2_made, t + 1)
                    v.tensor_tensor(hh[j % 2][:], relu[j % 2][:], up_ps, ALU.mult).then_inc(h_made, 1)
                    if j == 0 and not before_:
                        max3(*second)
                    top_, lim, inv, fac, back = (hm[s][:, n, j:j + 1] for n in range(5))
                    dve.wait_ge(h_made, t + 1)
                    step(v.tensor_reduce(top_, hh[j % 2][:], AX.X, ALU.max, apply_absolute_value=True))
                    step(v.tensor_scalar(lim, top_, hfac[s][:, 0, j:j + 1], Q_EPS, ALU.mult, ALU.max))
                    step(v.reciprocal(inv, lim))
                    v.tensor_scalar(fac, inv, 127.0, hfac[s][:, 0, j:j + 1], ALU.mult, ALU.mult).then_inc(h_scale, 1)
                    o.did(v.tensor_scalar(back, lim, 1.0 / 127.0, wmean[:, 2:3], ALU.mult, ALU.mult))
                    if j == 0 and first:
                        ln3_stats(*first)
                    if j == 2 and second:
                        row_scales(*second)
                        row_integers(*second)
                    dve.wait_ge(h_round, t + 1)
                    v.tensor_scalar(hq[j % 2][:], hr[j % 2][:], MAGIC, None, ALU.subtract).then_inc(hq_made, 1)
                    if j == 1:
                        dve.wait_ge(out_done[s], 16 * b + 16)
                    if j:
                        x4(b, s, j - 1)
                    elif before_:
                        x4(*before_, TJ - 1)
                    if j == 0 and second:
                        x3(*second)
                        ln4_stats(*second)
                o.sync()
                o.clear()

            def dve_start():
                first_sum()
                dve.wait_ge(x2_made[0], 1)
                row_factors(xe[0], stat3[0], mv3[0], nt3[0], ln3_rstd[0])
                max3(0, 0)
                ln3_stats(0, 1)
                x3(0, 0)
                dve.wait_ge(x3_made[0], 1)
                row_factors(xc[0], stat3[0], mv3[0], nt3[0], ln4_rstd[0])
                dve.sem_inc(ln3_guess[0], 1)
                dve.sem_inc(ln4_guess[0], 1)
                row_scales(0, 0)
                row_integers(0, 0)
                o.clear()

            phase3(dve_unit, dve.Fori, dve_start)
            x4(B - 1, ST - 1, TJ - 1)

        @block.tensor
        def _(pe):
            BM = B * M
            for s in range(ST):
                pe.sem_inc(placed[s], 1)
            pe.sem_inc(by_made, 1)

            def mm(out_, lhsT, rhs, first, last):
                return nc.tensor.matmul(out_, lhsT, rhs, start=first, stop=last)

            def tr(out_, in_, identity):
                return nc.tensor.matmul(out_, in_, identity, start=True, stop=True, is_transpose=True)

            pe.wait_ge(consts_made, 1)
            pe.wait_ge(ctx_in_sem, 16)
            for k in range(KD):
                for b in range(B):
                    last = tr(ps[:, k, b * M:(b + 1) * M], ctx_sb[:, b, k * P:(k + 1) * P], ident[0:M, 0:M])
            last.then_inc(setup_mm, 1)
            pe.wait_ge(weights_in, SMALL)
            tr(ps[:, 6, 0:NROW], bcols_in[:], ident[0:NROW, 0:NROW]).then_inc(setup_mm, 1)
            for n, w in enumerate((w0_sb, wk_sb, wv_sb, wo_sb)):
                for k in range(KD):
                    for c in range(KD):
                        last = tr(ps[:, 2 + n, k * D + c * P:k * D + (c + 1) * P], w[:, c, k * P:(k + 1) * P], ident[:])
                last.then_inc(setup_mm, 1)

            def product(bank, w, rhs):
                for m in range(KD):
                    for k in range(KD):
                        last = mm(ps[:, bank + m, 0:BM], w[:, k, m * P:(m + 1) * P], rhs[:, k, :], k == 0, k == KD - 1)
                return last

            pe.wait_ge(setup_out, 6)
            product(0, wkT, ctxT).then_inc(setup_mm, 1)
            product(2, w0T, ctxT).then_inc(setup_mm, 1)
            product(4, wvT, ctxT).then_inc(setup_mm, 1)
            pe.wait_ge(setup_out, 8)
            for k in range(KD):
                mm(ps[0:1, 6, 0:BM], bcols[:, k:k + 1], eoT[:, k, :], k == 0, k == KD - 1)
            product(0, w0_sb, eoT).then_inc(setup_mm, 1)
            for k in range(KD):
                mm(ps[0:1, 7, 0:BM], bcols[:, KD + k:KD + k + 1], kpT[:, k, :], k == 0, k == KD - 1)
            product(2, wq_sb, kpT).then_inc(setup_mm, 1)
            pe.wait_ge(setup_out, 9)
            for b in range(B):
                dst = ps[0:M, 4 + b // 2, b % 2 * D:b % 2 * D + D]
                for k in range(KD):
                    mm(dst, vpT[:, k, b * M:(b + 1) * M], woT[:, k, :], k == 0, False)
                last = mm(dst, ones[0:1, 0:M], bo_row[:], False, True)
                if b % 2:
                    last.then_inc(setup_mm, 1)
            pe.wait_ge(setup_out, 13)

            def transposed_tiles(s, src, identity, dst):
                for j in range(TJ):
                    for k in range(KD):
                        last = tr(dst[:, k, j * P:(j + 1) * P], src[:, j, k * P:(k + 1) * P], identity)
                return last

            def scores(bank, b, xT_, g_, c_):
                at = bass.ds(b * M, M)
                for j in range(TJ):
                    dst = bank[:, j * P:j * P + M]
                    for k in range(KD):
                        mm(dst, xT_[:, k, j * P:(j + 1) * P], g_[:, k, at], k == 0, False)
                    last = mm(dst, ones[0:1, :], c_[:, at], False, True)
                return last

            def transposed_probs(bank, pr_):
                for j in range(TJ):
                    last = tr(bank[0:M, j * P:(j + 1) * P], pr_[:, j, :], ident[:])
                return last

            def attend(banks, b, prT_, values):
                rhs = values[:, bass.ds(b, 1), :].rearrange("m o d -> m (o d)")
                for j in range(TJ):
                    last = mm(banks[:, j // 2, j % 2 * D:j % 2 * D + D], prT_[:, j * P:(j + 1) * P], rhs, True, True)
                return last

            def turn1(b, s):
                pe.wait_ge(ln1[s], b + 1)
                transposed_tiles(s, xn[s], ident[:], bank_wide(s)).then_inc(xT1_mm[s], 1)

            def scores1(b, s):
                pe.wait_ge(xT1[s], b + 1)
                pe.wait_ge(placed[s], b + 1)
                scores(bank_c(s), b, xT[s], g0, c0).then_inc(score_mm[s], 1)

            def turn_probs1(b, s):
                pe.wait_ge(probs[s], b + 1)
                transposed_probs(bank_d(s), pr[s]).then_inc(probsT_mm[s], 1)

            def attend1(b, s):
                pe.wait_ge(probsT[s], b + 1)
                attend(bank_wide(s), b, prT[s], ctx_sb).then_inc(attn_mm[s], 1)

            def turn2(b, s):
                pe.wait_ge(ln2[s], b + 1)
                transposed_tiles(s, xn[s], ident[:], bank_wide(s)).then_inc(xT2_mm[s], 1)

            def logits(b, s):
                pe.wait_ge(xT2[s], b + 1)
                for j in range(TJ):
                    for k in range(KD):
                        last = mm(bank_c(s)[:, j * E:(j + 1) * E], xT[s][:, k, j * P:(j + 1) * P], wr_sb[:, k, :],
                                  k == 0, k == KD - 1)
                last.then_inc(logit_mm[s], 1)

            def ranks(b, s):
                pe.wait_ge(picked[s], b + 1)
                dst = bank_c(s)[:, 64:64 + TJ * E]
                mm(dst, before[:], picks[s][:].rearrange("p j e -> p (j e)"), True, False)
                mm(dst, onesb[:], pri[s][:].rearrange("p j e -> p (j e)"), False, True).then_inc(rank_mm[s], 1)

            def pe_unit1(routing, attention, first):
                if attention:
                    turn1(*attention)
                    scores1(*attention)
                turn2(*routing)
                if attention:
                    turn_probs1(*attention)
                logits(*routing)
                if attention:
                    attend1(*attention)
                ranks(*routing)

            def pe_start1():
                turn1(0, 0)
                scores1(0, 0)
                turn_probs1(0, 0)
                attend1(0, 0)

            phase1(pe_unit1, pe.Fori, pe_start1)

            for s in range(ST):
                pe.wait_ge(placed[s], B + 1)
            mm(ps[:, 0, 0:E], onesb[:], prior[:, 0, :], True, True).then_inc(count_mm, 1)
            pe.wait_ge(tern_sum, 3)
            mm(ps[:, 7, 0:3], ones[:], tsum[:], True, True).then_inc(tern_total, 1)
            pe.wait_ge(tables, 1)
            for n in range(STAGES):
                pe.wait_ge(low_done[n], 8 // STAGES * B + 1)

            def transpose_block(n):
                pe.wait_ge(bx_in, 16 * n + 16)
                bank = ps[:, 6, :].bitcast(F16).rearrange("p (c n) -> p c n", c=2 * KD)
                for h in range(2):
                    for c in range(2 * KD):
                        last = tr(bank[:, c, h * P:(h + 1) * P], bx[:, h, c * P:(c + 1) * P], ident16[:])
                last.then_inc(bxT_mm, 1)

            transpose_block(0)
            with pe.Fori(0, NBLK) as n:
                e = pe.value_load(block_expert[0:1, bass.ds(n, 1)], min_val=0, max_val=E - 1)
                pe.wait_ge(bxT_made, n + 1)
                for c in range(KH):
                    if c >= 4:
                        pe.wait_ge(hid_made, KH * n + c - 3)
                    dst = ps[:, c % 4, 0:BLK]
                    cols = slice(c * P, (c + 1) * P)
                    for k in range(KD):
                        hi = w1h[:, bass.ds(e * KD + k, 1), cols].rearrange("p a n -> p (a n)")
                        lo = w1l[:, bass.ds(e * KD + k, 1), cols].rearrange("p a n -> p (a n)")
                        mm(dst, hi, bxT[:, k, :], k == 0, False)
                        mm(dst, hi, bxT[:, KD + k, :], False, False)
                        last = mm(dst, lo, bxT[:, k, :], False, k == KD - 1)
                    last.then_inc(hid_mm, 1)
                transpose_block(n + 1)
                pe.wait_ge(by_made, 2 * n + 1)
                for h in range(2):
                    dst = ps[:, 4 + h, 0:D]
                    rows_ = slice(h * P, (h + 1) * P)
                    for c in range(KH):
                        if h == 0 and c % 2 == 0:
                            pe.wait_ge(hid_split, KH // 2 * n + c // 2 + 1)
                        hi = w2h[:, bass.ds(e * KH + c, 1), :].rearrange("p a n -> p (a n)")
                        lo = w2l[:, bass.ds(e * KH + c, 1), :].rearrange("p a n -> p (a n)")
                        mm(dst, hidh[:, c, rows_], hi, c == 0, False)
                        mm(dst, hidh[:, c, rows_], lo, False, False)
                        last = mm(dst, hidl[:, c, rows_], hi, False, c == KH - 1)
                    last.then_inc(by_mm, 1)

            pe.wait_ge(by_made, 2 * NBLK + 1)
            pe.wait_ge(bxT_made, NBLK + 1)
            for n in range(3):
                pe.wait_ge(tern_quant, n + 1)
                if n:
                    pe.wait_ge(tern_out, n)
                for k in range(KD):
                    for c in range(KH):
                        at = c * D + k * P if n < 2 else k * H + c * P
                        last = tr(ps[:, 5 + k, :].bitcast(BF16)[:, c * P:(c + 1) * P], ternq[n][:, at:at + P], identb[:])
                last.then_inc(tern_T, 1)
            pe.wait_ge(tern_out, 3)

            def turn3(b, s):
                pe.wait_ge(ln3[s], b + 1)
                transposed_tiles(s, xn3[s], ident[:], attn_ps).then_inc(xT3_mm[s], 1)

            def scores3(b, s):
                pe.wait_ge(xT3_made[s], b + 1)
                scores(attn_ps[:, 0, :], b, xT3[s], g1, c1).then_inc(score3_mm[s], 1)

            def turn_probs3(b, s):
                pe.wait_ge(probs3[s], b + 1)
                transposed_probs(attn_ps[:, 1, :], pr3[s]).then_inc(probsT3_mm[s], 1)

            def attend3(b, s):
                pe.wait_ge(probsT3[s], b + 1)
                attend(attn_ps, b, prT3[s], vo).then_inc(attn3_mm[s], 1)

            def turn_integers(b, s):
                pe.wait_ge(xq_made[s], b + 1)
                transposed_tiles(s, xq[s], identb[:], turned_ps.rearrange("p (k n) -> p k n", k=KD))\
                    .then_inc(xqT_mm[s], 1)

            def turn_hidden(t, j):
                pe.wait_ge(hq_made, t + 1)
                for c in range(KH):
                    last = tr(turned_ps[:, c * P:(c + 1) * P], hq[j % 2][:, c * P:(c + 1) * P], identb[:])
                last.then_inc(hqT_mm, 1)

            def down(t, j):
                pe.wait_ge(hqT_made, t + 1)
                if not isinstance(t, int) or t:
                    pe.wait_ge(xo_made, t)
                for c in range(KH):
                    last = mm(down_ps, hqT[j % 2][:, c, :], wdT[:, c, :], c == 0, c == KH - 1)
                last.then_inc(down_mm, 1)

            def widened(dst, w, s, j):
                for half in range(2):
                    n = slice(half * 512, half * 512 + 512)
                    for k in range(KD):
                        last = mm(dst[:, n], xqT[s][:, k, j * P:(j + 1) * P], w[:, k, n], k == 0, k == KD - 1)
                return last

            def gate(s, t, j, before_=True):
                if before_:
                    pe.wait_ge(relu_made, t)
                widened(gate_ps, wgT, s, j).then_inc(gate_mm, 1)

            def up(s, t, j, before_=True):
                if before_:
                    pe.wait_ge(h_made, t)
                widened(up_ps, wuT, s, j).then_inc(up_mm, 1)

            def pe_unit(b, s, before_, second, first, prep):
                if not before_:
                    pe.wait_ge(xqT_made[s], b + 1)
                    gate(s, 0, 0, False)
                    up(s, 0, 0, False)
                    gate(s, 1, 1)
                    scores3(*second)
                for j in range(TJ):
                    t = tile_no(b, s, j)
                    if j or before_:
                        if j == 3 and second:
                            pe.wait_ge(xqT_made[second[1]], second[0] + 1)
                        turn_hidden(t - 1, j - 1)
                    if j < TJ - 1:
                        up(s, t + 1, j + 1)
                    elif second:
                        gate(second[1], t + 1, 0)
                        up(second[1], t + 1, 0)
                    if j == 0 and second:
                        turn_probs3(*second)
                    if j or before_:
                        down(t - 1, j - 1)
                    if j < TJ - 2:
                        gate(s, t + 2, j + 2)
                    if j == 3 and second:
                        gate(second[1], t + 2, 1)
                    if j == 0 and second:
                        attend3(*second)
                    if j == 1 and first:
                        if second:
                            pe.wait_ge(x3_made[second[1]], second[0] + 1)
                        turn3(*first)
                    if j == 2:
                        if first:
                            scores3(*first)
                        if second:
                            turn_integers(*second)

            def pe_start():
                turn3(0, 0)
                scores3(0, 0)
                turn_probs3(0, 0)
                attend3(0, 0)
                pe.wait_ge(x3_made[0], 1)
                turn_integers(0, 0)
                turn3(0, 1)

            phase3(pe_unit, pe.Fori, pe_start)
            turn_hidden(tile_no(B - 1, ST - 1, TJ - 1), TJ - 1)
            down(tile_no(B - 1, ST - 1, TJ - 1), TJ - 1)


_INS = ['x', 'ctx_1024', 'L0_xattn_W', 'L0_xattn_b', 'L0_ffn_w_router', 'L0_ffn_w1', 'L0_ffn_b1', 'L0_ffn_w2',
        'L0_ffn_b2', 'L1_xattn_Wk', 'L1_xattn_Wv', 'L1_xattn_bv', 'L1_xattn_Wq', 'L1_xattn_bq', 'L1_xattn_Wo',
        'L1_xattn_bo', 'L1_ffn_w_gate', 'L1_ffn_w_up', 'L1_ffn_w_down']


def kernel(**inputs):
    import numpy as np
    import concourse.bacc as bacc
    from concourse.bass_utils import run_bass_kernel_spmd

    nc = bacc.Bacc("TRN2", target_bir_lowering=False, num_devices=1)
    arrays, args = {}, []
    for name in _INS:
        a = np.ascontiguousarray(inputs[name])
        arrays[f"in_{name}"] = a
        args.append(nc.dram_tensor(f"in_{name}", a.shape, mybir.dt.from_np(a.dtype), kind="ExternalInput").ap())
    out = nc.dram_tensor("out", (B, S, D), F32, kind="ExternalOutput").ap()
    build(nc, *args, out)
    return run_bass_kernel_spmd(nc, [arrays], core_ids=[0]).results[0]["out"]
```
